# Optimizing a Trainium2 kernel written in Bass

```python
import numpy as np
import jax
import jax.numpy as jnp

def _softmax(x, axis=-1):
    return jax.nn.softmax(x, axis=axis)

def _gelu(x):
    return jax.nn.gelu(x, approximate=True)

def _silu(x):
    return jax.nn.silu(x)

def _sigmoid(x):
    return jax.nn.sigmoid(x)

def _layernorm(x, axis=-1, eps=1e-05):
    m = jnp.mean(x, axis=axis, keepdims=True)
    v = jnp.var(x, axis=axis, keepdims=True)
    return (x - m) / jnp.sqrt(v + eps)

def _scatter_add(tgt, idx, src, axis=0):
    return tgt.at[idx].add(src)

def _segment_sum(src, seg, n):
    return jax.ops.segment_sum(src, seg, n)
kernel_name = 'mk_audio_tower_d1_tok_audfeat4096_r4_b67b80'

def setup_inputs(seed: int=0):
    np.random.seed(seed)
    _w = jnp.asarray

    def _rec_inputs():
        import jax
        import jax.numpy as jnp
        _rk = jax.random.key(seed)
        x = -0.000392918 + 0.999932 * jax.random.normal(jax.random.fold_in(_rk, 1), (32, 256, 256), jnp.float32)
        return x
    x = _rec_inputs()

    def _L0_tok_setup():
        import jax, jax.numpy as jnp
        import numpy as np
        STRIDE = 4
        HEADS = 8
        KSIZE = 5
        PAD_L = 4

        def _layernorm(x, g, b, eps=1e-05):
            mu = jnp.mean(x, axis=-1, keepdims=True)
            var = jnp.mean((x - mu) ** 2, axis=-1, keepdims=True)
            return (x - mu) * jax.lax.rsqrt(var + eps) * g + b
        key = jax.random.key(seed)
        ks = jax.random.split(key, 6)
        B, T, C = (8, 512, 256)
        D = 1024
        x = jax.random.normal(ks[0], (B, T, C), dtype=jnp.float32)
        W_proj = jax.random.normal(ks[1], (C * STRIDE, D), dtype=jnp.float32) * 0.02
        b_proj = jnp.zeros((D,), dtype=jnp.float32)
        ln_g = jnp.ones((D,), dtype=jnp.float32)
        ln_b = jnp.zeros((D,), dtype=jnp.float32)
        W_wgen = jax.random.normal(ks[2], (D, HEADS * KSIZE), dtype=jnp.float32) * 0.02
        b_wgen = jnp.zeros((HEADS * KSIZE,), dtype=jnp.float32)
        W_ff = jax.random.normal(ks[3], (D, D), dtype=jnp.float32) * 0.02
        b_ff = jnp.zeros((D,), dtype=jnp.float32)
        return {'x': x, 'W_proj': W_proj, 'b_proj': b_proj, 'ln_g': ln_g, 'ln_b': ln_b, 'W_wgen': W_wgen, 'b_wgen': b_wgen, 'W_ff': W_ff, 'b_ff': b_ff}
    _L0_tok_all = _L0_tok_setup()
    _L0_tok_in = {k: v for k, v in _L0_tok_all.items() if k in ('W_proj', 'b_proj', 'ln_g', 'ln_b', 'W_wgen', 'b_wgen', 'W_ff', 'b_ff')}
    del _L0_tok_all

    def _L0_attn_setup():
        import jax, jax.numpy as jnp
        import numpy as np
        B, S, HIDDEN = (2, 512, 1024)
        TP = 2
        PART = HIDDEN // TP
        NUM_HEADS = 16 // TP
        HEAD_DIM = PART // NUM_HEADS
        MASKED_BIAS = -10000.0
        key = jax.random.key(seed)
        k_x, k_wq, k_bq, k_wo, k_bo = jax.random.split(key, 5)
        x = jax.random.normal(k_x, (B, S, HIDDEN), dtype=jnp.float32)
        w_qkv = jax.random.normal(k_wq, (3 * PART, HIDDEN), dtype=jnp.float32) * 0.02
        b_qkv = jax.random.normal(k_bq, (3 * PART,), dtype=jnp.float32) * 0.02
        w_o = jax.random.normal(k_wo, (HIDDEN, PART), dtype=jnp.float32) * 0.02
        b_o = jax.random.normal(k_bo, (HIDDEN,), dtype=jnp.float32) * 0.02
        return {'x': x, 'w_qkv': w_qkv, 'b_qkv': b_qkv, 'w_o': w_o, 'b_o': b_o}
    _L0_attn_all = _L0_attn_setup()
    _L0_attn_in = {k: v for k, v in _L0_attn_all.items() if k in ('w_qkv', 'b_qkv', 'w_o', 'b_o')}
    del _L0_attn_all

    def _L0_ffn_setup():
        import jax, jax.numpy as jnp
        import numpy as np
        B, L, H, Dh, M = (4, 512, 16, 64, 256)
        D = H * Dh
        key = jax.random.key(seed)
        kx, ku, kd, kp = jax.random.split(key, 4)
        x = jax.random.normal(kx, (B, L, D), dtype=jnp.float32)
        up = jax.random.normal(ku, (H, Dh, M), dtype=jnp.float32)
        down = jax.random.normal(kd, (H, M, Dh), dtype=jnp.float32)
        perm = jax.random.permutation(kp, D)
        return {'x': x, 'up': up, 'down': down, 'perm': perm}
    _L0_ffn_all = _L0_ffn_setup()
    _L0_ffn_in = {k: v for k, v in _L0_ffn_all.items() if k in ('up', 'down', 'perm')}
    del _L0_ffn_all
    return {'x': x, 'L0_tok_W_proj': _L0_tok_in['W_proj'], 'L0_tok_b_proj': _L0_tok_in['b_proj'], 'L0_tok_ln_g': _L0_tok_in['ln_g'], 'L0_tok_ln_b': _L0_tok_in['ln_b'], 'L0_tok_W_wgen': _L0_tok_in['W_wgen'], 'L0_tok_b_wgen': _L0_tok_in['b_wgen'], 'L0_tok_W_ff': _L0_tok_in['W_ff'], 'L0_tok_b_ff': _L0_tok_in['b_ff'], 'L0_attn_w_qkv': _L0_attn_in['w_qkv'], 'L0_attn_b_qkv': _L0_attn_in['b_qkv'], 'L0_attn_w_o': _L0_attn_in['w_o'], 'L0_attn_b_o': _L0_attn_in['b_o'], 'L0_ffn_up': _L0_ffn_in['up'], 'L0_ffn_down': _L0_ffn_in['down'], 'L0_ffn_perm': _L0_ffn_in['perm']}

def reference(x, L0_tok_W_proj, L0_tok_b_proj, L0_tok_ln_g, L0_tok_ln_b, L0_tok_W_wgen, L0_tok_b_wgen, L0_tok_W_ff, L0_tok_b_ff, L0_attn_w_qkv, L0_attn_b_qkv, L0_attn_w_o, L0_attn_b_o, L0_ffn_up, L0_ffn_down, L0_ffn_perm):
    import jax
    import jax.numpy as jnp

    def _L0_tok_ref(x, W_proj, b_proj, ln_g, ln_b, W_wgen, b_wgen, W_ff, b_ff):
        import jax, jax.numpy as jnp
        import numpy as np
        STRIDE = 4
        HEADS = 8
        KSIZE = 5
        PAD_L = 4

        def _layernorm(x, g, b, eps=1e-05):
            mu = jnp.mean(x, axis=-1, keepdims=True)
            var = jnp.mean((x - mu) ** 2, axis=-1, keepdims=True)
            return (x - mu) * jax.lax.rsqrt(var + eps) * g + b
        B, T, C = x.shape
        folded_T = T // STRIDE
        xf = x[:, :folded_T * STRIDE].reshape(B, folded_T, C * STRIDE)
        h = xf @ W_proj + b_proj
        D = h.shape[-1]
        R = D // HEADS
        res = h
        y = _layernorm(h, ln_g, ln_b)
        w = (y @ W_wgen + b_wgen).reshape(B, folded_T, HEADS, KSIZE)
        w = jax.nn.softmax(w, axis=-1)
        yp = jnp.pad(y, ((0, 0), (PAD_L, 0), (0, 0)))
        taps = jnp.stack([yp[:, k:k + folded_T] for k in range(KSIZE)], axis=0)
        taps = taps.reshape(KSIZE, B, folded_T, HEADS, R)
        conv = jnp.einsum('kbthr,bthk->bthr', taps, w).reshape(B, folded_T, D)
        out = res + jax.nn.relu(conv @ W_ff + b_ff)
        return out

    def _L0_attn_ref(x, w_qkv, b_qkv, w_o, b_o):
        import jax, jax.numpy as jnp
        import numpy as np
        B, S, HIDDEN = (2, 512, 1024)
        TP = 2
        PART = HIDDEN // TP
        NUM_HEADS = 16 // TP
        HEAD_DIM = PART // NUM_HEADS
        MASKED_BIAS = -10000.0
        b, s, _ = x.shape
        qkv = x @ w_qkv.T + b_qkv
        q, k, v = jnp.split(qkv, 3, axis=-1)

        def to_heads(a):
            return a.reshape(b, s, NUM_HEADS, HEAD_DIM).transpose(0, 2, 1, 3)
        q, k, v = (to_heads(q), to_heads(k), to_heads(v))
        scores = jnp.einsum('bhfc,bhtc->bhft', k, q)
        causal = jnp.triu(jnp.ones((s, s), dtype=bool))
        scores = jnp.where(causal[None, None], scores, MASKED_BIAS)
        attn = jax.nn.softmax(scores, axis=-2)
        vals = jnp.einsum('bhft,bhfc->bhtc', attn, v)
        vals = vals.transpose(0, 2, 1, 3).reshape(b, s, PART)
        out = vals @ w_o.T + b_o
        return out

    def _L0_ffn_ref(x, up, down, perm):
        import jax, jax.numpy as jnp
        import numpy as np
        B, L, H, Dh, M = (4, 512, 16, 64, 256)
        D = H * Dh
        b, l, Dm = x.shape
        h, d = (up.shape[0], up.shape[1])
        unperm = jnp.argsort(perm)
        t = x.reshape(b * l, Dm)
        t = t[:, perm]
        t = t.reshape(b * l, h, d)
        t = jnp.einsum('bhd,hdm->bhm', t, up)
        t = jax.nn.gelu(t, approximate=False)
        t = jnp.einsum('bhm,hmd->bhd', t, down)
        t = t.reshape(b * l, h * d)
        t = t[:, unperm]
        out = t.reshape(b, l, Dm)
        return out
    h = _L0_tok_ref(x, L0_tok_W_proj, L0_tok_b_proj, L0_tok_ln_g, L0_tok_ln_b, L0_tok_W_wgen, L0_tok_b_wgen, L0_tok_W_ff, L0_tok_b_ff)
    h = h + _L0_attn_ref(_layernorm(h, axis=-1), L0_attn_w_qkv, L0_attn_b_qkv, L0_attn_w_o, L0_attn_b_o)
    h = h + _L0_ffn_ref(_layernorm(h, axis=-1), L0_ffn_up, L0_ffn_down, L0_ffn_perm)
    return h

_drawn_inputs = setup_inputs


def setup_inputs(seed=0):
    import zlib

    import numpy as np

    out = dict(_drawn_inputs(seed))
    spreads = {'L0_tok_b_proj': (0.0, 0.1),
     'L0_tok_ln_g': (1.0, 0.2),
     'L0_tok_ln_b': (0.0, 0.1),
     'L0_tok_b_wgen': (0.0, 0.1),
     'L0_tok_b_ff': (0.0, 0.1)}
    factors = {'L0_attn_b_qkv': 2.821}
    for name, (base, spread) in spreads.items():
        noise = np.random.default_rng([zlib.crc32(name.encode()), seed]).standard_normal(out[name].shape)
        drawn = base * np.exp(spread * noise) if base else spread * noise
        out[name] = jnp.asarray(drawn.astype(out[name].dtype))
    for name, factor in factors.items():
        out[name] = (out[name] * factor).astype(out[name].dtype)
    return out
```

```python
import concourse.bass as bass
from concourse import mybir
from contextlib import ExitStack

BATCH, FRAMES, CHANNELS, STRIDE = 32, 256, 256, 4
SEQ = FRAMES // STRIDE
D = CHANNELS * STRIDE
TOKENS = BATCH * SEQ
P = 128
KB = D // P
N = 512
CH = TOKENS // N
TILES = N // P
TAPS, CONV_HEADS = 5, 8
LOGITS = TAPS * CONV_HEADS
PART = 512
HEAD = 64
PAIRS = PART // P
FF_HEADS, FF_IN, FF_MID = 16, 64, 256
FFB = 2 * FF_MID // P
EPS = 1e-5
MASKED = -10000.0
OTHER = -3.0e38
B_PROJ, LN_G, LN_B, B_FF, B_O, B_Q, B_K, B_V = 0, 8, 16, 24, 32, 40, 44, 48
VECS = 52
BAND = P * (P + 1)
UNITS = TILES * CONV_HEADS


def audio_tower(nc, x_t, w_proj, w_ff, w_gen, w_qkv_t, w_o_t, up, down, vecs, b_gen, perm, *outs):
    F32, F32R, I32, U8 = mybir.dt.float32, mybir.dt.float32r, mybir.dt.int32, mybir.dt.uint8
    ALU, ACT, AX = mybir.AluOpType, mybir.ActivationFunctionType, mybir.AxisListType

    h0_s = nc.dram_tensor("h0_s", [CH, P, KB * N], F32, kind="Internal").ap()
    h1_s = nc.dram_tensor("h1_s", [CH, P, KB * N], F32, kind="Internal").ap()
    vals_s = nc.dram_tensor("vals_s", [CH, P, PAIRS * N], F32, kind="Internal").ap()
    h2_s = [nc.dram_tensor(f"h2_s{c}", [D, N], F32, kind="Internal").ap() for c in range(CH)]
    band_s = nc.dram_tensor("band_s", [UNITS * BAND], F32, kind="Internal").ap()

    ctx = ExitStack()
    with ctx:
        base = (nc.sbuf_base + 63) // 64 * 64
        def place(name, shape, dt, at):
            return nc.alloc_sbuf_tensor_at(name, shape, dt, offset=base + at)

        def sem(name):
            return ctx.enter_context(nc.semaphore(name))

        KIB = 1024
        R1, R2, CONST = 0, 64 * KIB, 128 * KIB
        STAGE = CONST + 7 * KIB
        LNT = STAGE + 8 * KIB
        E = LNT + 10 * KIB
        ident = place("ident", [P, P], F32, CONST)
        mean_w = place("mean_w", [P, P], F32, CONST + 512)
        negs = place("negs", [P, P], F32, CONST + 1024)
        vec = place("vec", [P, VECS], F32, CONST + 1536)
        bgen = place("bgen", [P, LOGITS], F32, CONST + 1792)
        valid = place("valid", [P, TAPS], F32, CONST + 1984)
        eps = place("eps", [P, 1], F32, CONST + 2016)
        rows = place("rows", [P, KB], I32, CONST + 2048)
        masked = place("masked", [P, P], U8, CONST + 2176)
        maskf = place("maskf", [P, P], F32, LNT)
        wg_h = place("wg_h", [P, KB, LOGITS], F32R, CONST + 2304)
        wg_l = place("wg_l", [P, KB, LOGITS], F32R, CONST + 2304 + 1280)
        smax = place("smax", [P, 2, TILES], F32, CONST + 4992)
        ssum = place("ssum", [P, 2, TILES], F32, CONST + 5056)
        mx5 = place("mx5", [P, UNITS], F32, CONST + 5120)
        su5 = place("su5", [P, UNITS], F32, CONST + 5248)
        lg5 = place("lg5", [P, UNITS, TAPS], F32, CONST + 5376)
        wk5 = place("wk5", [P, UNITS, TAPS], F32, CONST + 6016)
        stage = place("stage", [P, 4, N], F32, STAGE)
        wg_raw = place("wg_raw", [P, KB, LOGITS], F32, LNT + 6 * KIB)
        acc = place("acc", [P, N], F32, LNT)
        sq = place("sq", [P, 2, N], F32, LNT + 2 * KIB)
        vacc = place("vacc", [P, N], F32, LNT + 6 * KIB)
        rstd = place("rstd", [P, N], F32, LNT + 8 * KIB)
        wp_h = place("wp_h", [P, KB, D], F32R, R1)
        wp_l = place("wp_l", [P, KB, D], F32R, R1 + 32 * KIB)
        xa_h = place("xa_h", [P, KB, N], F32R, E)
        xa_l = place("xa_l", [P, KB, N], F32R, E + 16 * KIB)
        xs = place("xs", [P, KB, N], F32, R2)
        ho = place("ho", [P, KB, N], F32, R2 + 16 * KIB)
        zero = place("zero", [P, UNITS * BAND // P], F32, R2 + 32 * KIB)
        wf_h = place("wf_h", [P, KB, D], F32R, R2)
        wf_l = place("wf_l", [P, KB, D], F32R, R2 + 32 * KIB)
        db = place("db", [P, KB, N], F32, R1)
        yb = place("yb", [P, KB, N], F32, R1 + 16 * KIB)
        cv_h = place("cv_h", [P, KB, N], F32R, R1 + 32 * KIB)
        cv_l = place("cv_l", [P, KB, N], F32R, R1 + 48 * KIB)
        yr_h = place("yr_h", [P, 2, N], F32R, E)
        yr_l = place("yr_l", [P, 2, N], F32R, E + 4 * KIB)
        yt_h = place("yt_h", [P, 2, N], F32R, E + 8 * KIB)
        yt_l = place("yt_l", [P, 2, N], F32R, E + 12 * KIB)
        ar_h = place("ar_h", [P, 2, N], F32R, E + 16 * KIB)
        ar_l = place("ar_l", [P, 2, N], F32R, E + 20 * KIB)
        band = place("band", [P, UNITS, P], F32, E + 24 * KIB)
        lg = place("lg", [LOGITS, N], F32, E + 40 * KIB)
        res = place("res", [P, 2, N], F32, E + 42 * KIB)
        fo = place("fo", [P, 2, N], F32, E + 46 * KIB)
        wq_h = place("wq_h", [P, KB, PART], F32R, R1)
        wq_l = place("wq_l", [P, KB, PART], F32R, R1 + 16 * KIB)
        wk_h = place("wk_h", [P, KB, PART], F32R, R1 + 32 * KIB)
        wk_l = place("wk_l", [P, KB, PART], F32R, R1 + 48 * KIB)
        wv_h = place("wv_h", [P, KB, PART], F32R, R2)
        wv_l = place("wv_l", [P, KB, PART], F32R, R2 + 16 * KIB)
        dc = place("dc", [P, KB, N], F32, R2 + 32 * KIB)
        v_h = place("v_h", [P, TILES, PART], F32R, R2 + 48 * KIB)
        v_l = place("v_l", [P, TILES, PART], F32R, R2 + 56 * KIB)
        xc_h = place("xc_h", [P, KB, N], F32R, E)
        xc_l = place("xc_l", [P, KB, N], F32R, E + 16 * KIB)
        qk_h = place("qk_h", [P, 2, N], F32R, E + 32 * KIB)
        qk_l = place("qk_l", [P, 2, N], F32R, E + 36 * KIB)
        pr = place("pr", [P, 2, N], F32, E + 40 * KIB)
        pt_h = place("pt_h", [P, 2, N], F32R, E + 44 * KIB)
        pt_l = place("pt_l", [P, 2, N], F32R, E + 48 * KIB)
        vo = place("vo", [P, N], F32, E + 52 * KIB)
        wo_h = place("wo_h", [P, PAIRS, D], F32R, R1)
        wo_l = place("wo_l", [P, PAIRS, D], F32R, R1 + 16 * KIB)
        vs = place("vs", [P, PAIRS, N], F32, E)
        vs_h = place("vs_h", [P, PAIRS, N], F32R, E + 8 * KIB)
        vs_l = place("vs_l", [P, PAIRS, N], F32R, E + 16 * KIB)
        h2 = place("h2", [P, KB, N], F32, E + 24 * KIB)
        up_h = place("up_h", [P, KB, FF_MID], F32R, R2)
        up_l = place("up_l", [P, KB, FF_MID], F32R, R2 + 8 * KIB)
        dn_h = place("dn_h", [P, KB * FFB, P], F32R, R2 + 16 * KIB)
        dn_l = place("dn_l", [P, KB * FFB, P], F32R, R2 + 32 * KIB)
        hg = place("hg", [P, 2 * KB, N], F32, R1)
        dd = place("dd", [P, KB, N], F32, R1 + 32 * KIB)
        gt = place("gt", [P, FFB, N], F32, R1 + 48 * KIB)
        g_h = place("g_h", [P, FFB, N], F32R, R1 + 56 * KIB)
        g_l = place("g_l", [P, FFB, N], F32R, R2 + 48 * KIB)
        xd_h = place("xd_h", [P, KB, N], F32R, E)
        xd_l = place("xd_l", [P, KB, N], F32R, E + 16 * KIB)

        bank = [ctx.enter_context(nc.psum_tensor(f"bank{i}", [P, N], F32)) for i in range(8)]
        LN_BANK = 6

        const_ld = sem("const_ld")
        masks_ok = sem("masks_ok")
        stage_ld = [sem(f"stage_ld{i}") for i in range(4)]
        w_hi = sem("w_hi")
        w_lo_v = sem("w_lo_v")
        w_lo_g = sem("w_lo_g")
        wg_ok = sem("wg_ok")
        zero_ok, band_zeroed = sem("zero_ok"), sem("band_zeroed")
        a_ld = [sem(f"a_ld{k}") for k in range(KB)]
        a_hi, a_lo, a_used, a_mm, a_ev = (sem(s) for s in ("a_hi", "a_lo", "a_used", "a_mm", "a_ev"))
        a_st = [sem(f"a_st{g}") for g in range(2)]
        ln_pool, ln_mean, ln_d, ln_sq, ln_var, ln_std, ln_rstd = (
            sem(s) for s in ("ln_pool", "ln_mean", "ln_d", "ln_sq", "ln_var", "ln_std", "ln_rstd"))
        b_ld = sem("b_ld")
        y_scaled, y_b, yr_hi, yr_lo, yr_used, lg_ev, lgt_mm = (
            sem(s) for s in ("y_scaled", "y_b", "yr_hi", "yr_lo", "yr_used", "lg_ev", "lgt_mm"))
        sm5, exp5, skewed, band_ld = (sem(s) for s in ("sm5", "exp5", "skewed", "band_ld"))
        yt_mm, at_mm, yt_hi, ar_hi, yt_lo, ar_lo = (
            sem(s) for s in ("yt_mm", "at_mm", "yt_hi", "ar_hi", "yt_lo", "ar_lo"))
        cv_mm, cv_hi, cv_lo, ff_mm, ff_ev, ff_add = (
            sem(s) for s in ("cv_mm", "cv_hi", "cv_lo", "ff_mm", "ff_ev", "ff_add"))
        res_ld = [sem(f"res_ld{i}") for i in range(2)]
        fo_st = [sem(f"fo_st{i}") for i in range(2)]
        c_ld, xc_sc, xc_hi, xc_lo, xc_used = (sem(s) for s in ("c_ld", "xc_sc", "xc_hi", "xc_lo", "xc_used"))
        v_mm, v_hi, v_lo, qk_mm, qk_hi, qk_lo = (
            sem(s) for s in ("v_mm", "v_hi", "v_lo", "qk_mm", "qk_hi", "qk_lo"))
        s_mm, s_masked, s_max, s_sub, s_exp, s_sum, s_rec, s_norm = (
            sem(s) for s in ("s_mm", "s_masked", "s_max", "s_sub", "s_exp", "s_sum", "s_rec", "s_norm"))
        pt_mm, pt_hi, pt_lo, pv_mm, vo_ev, vo_st = (
            sem(s) for s in ("pt_mm", "pt_hi", "pt_lo", "pv_mm", "vo_ev", "vo_st"))
        vs_ld, vs_hi, vs_lo, vs_used, o_mm, o_ev = (
            sem(s) for s in ("vs_ld", "vs_hi", "vs_lo", "vs_used", "o_mm", "o_ev"))
        o_ld = [sem(f"o_ld{g}") for g in range(2)]
        o_st = [sem(f"o_st{g}") for g in range(2)]
        g_ld, xd_sc, xd_hi, xd_lo = (sem(s) for s in ("g_ld", "xd_sc", "xd_hi", "xd_lo"))
        up_mm, gelu_ok, g_hi, g_lo, g_used, d_ev, d_st, dn_zero = (
            sem(s) for s in ("up_mm", "gelu_ok", "g_hi", "g_lo", "g_used", "d_ev", "d_st", "dn_zero"))

        def since(e, s, c, per, k):
            if isinstance(c, int):
                if c * per + k > 0:
                    e.wait_ge(s, c * per + k)
            else:
                e.wait_ge(s, c * per + k)

        def chunks(e, first, last, body):
            body(first)
            if last - first > 1:
                with e.Fori(first + 1, last) as c:
                    body(c)

        def released(e, c, k, blocks, used, done):
            if k < blocks - 1:
                since(e, used, c, blocks - 1, k + 1)
            else:
                since(e, done, c, 8, 8)

        def weight_units():
            units = []
            for half in range(2):
                for k in range(KB):
                    cols = slice(half * N, half * N + N)
                    units.append((w_proj[k * P:(k + 1) * P, cols], wp_h[:, k, cols], wp_l[:, k, cols], "v"))
            for half in range(2):
                for k in range(KB):
                    cols = slice(half * N, half * N + N)
                    units.append((w_ff[k * P:(k + 1) * P, cols], wf_h[:, k, cols], wf_l[:, k, cols], "g"))
            for col, h, l, who in ((2, wv_h, wv_l, "g"), (0, wq_h, wq_l, "v"), (1, wk_h, wk_l, "g")):
                for k in range(KB):
                    units.append((w_qkv_t[k * P:(k + 1) * P, col * PART:(col + 1) * PART],
                                  h[:, k, :], l[:, k, :], who))
            for half in range(2):
                for k in range(PAIRS):
                    cols = slice(half * N, half * N + N)
                    units.append((w_o_t[k * P:(k + 1) * P, cols], wo_h[:, k, cols], wo_l[:, k, cols], "g"))
            for k in range(0, KB, 2):
                src = up[2 * k:2 * k + 4].rearrange("(a s) d m -> (s d) a m", s=2)
                units.append((src, up_h[:, k:k + 2, :], up_l[:, k:k + 2, :], "g"))
            for head in range(0, FF_HEADS, 4):
                src = down[head:head + 4].rearrange("h (b p) d -> p h b d", p=P)
                sl = slice(2 * head, 2 * head + 8)
                units.append((src, dn_h[:, sl, :], dn_l[:, sl, :], "g"))
            return units

        units = weight_units()
        U_PROJ, U_FF, U_V, U_Q, U_K, U_O, U_UP, U_DN, U_END = 0, 16, 32, 40, 48, 56, 64, 68, 72
        lo_before = [[sum(1 for u in units[:n] if u[3] == who) for n in range(len(units) + 1)] for who in "vg"]

        def wait_units(e, upto):
            if lo_before[0][upto]:
                e.wait_ge(w_lo_v, lo_before[0][upto])
            if lo_before[1][upto]:
                e.wait_ge(w_lo_g, lo_before[1][upto])

        def unit_load(e, u):
            if u >= 4:
                who = 0 if units[u - 4][3] == "v" else 1
                e.wait_ge((w_lo_v, w_lo_g)[who], lo_before[who][u - 3])
            src = units[u][0]
            if u >= U_DN:
                for i in range(4):
                    e.dma_start(stage[:, u % 4, i * P:(i + 1) * P].rearrange("p (b d) -> p b d", b=2),
                                src[:, i]).then_inc(stage_ld[u % 4], 16)
            else:
                dst = stage[:, u % 4, :]
                if u >= U_UP:
                    for i in range(2):
                        for s in range(2):
                            e.dma_start(stage[64 * s:64 * s + 64, u % 4, i * FF_MID:(i + 1) * FF_MID],
                                        up[4 * (u - U_UP) + 2 * i + s]).then_inc(stage_ld[u % 4], 16)
                else:
                    e.dma_start(dst, src).then_inc(stage_ld[u % 4], 16)

        def slot_count(u):
            return sum(16 * (4 if v >= U_UP else 1) for v in range(u % 4, u + 1, 4))

        def unit_views(u):
            st = stage[:, u % 4, :]
            if u < U_UP:
                return [(st, units[u][1], units[u][2])]
            if u < U_DN:
                return [(st.rearrange("p (a m) -> p a m", a=2), units[u][1], units[u][2])]
            v4 = st.rearrange("p (a s b d) -> p a s b d", a=2, s=2, b=2)
            out_views = []
            for s in range(2):
                h, l = (t.rearrange("p (a s b) (c d) -> p a s b c d", a=2, s=2, c=2)[:, :, s, :, s, :]
                        for t in (units[u][1], units[u][2]))
                out_views.append((v4[:, :, s], h, l))
            return out_views

        def unit_hi(act, u):
            act.wait_ge(stage_ld[u % 4], slot_count(u))
            for i, (st, h, _) in enumerate(unit_views(u)):
                ins = act.activation(h, st, ACT.Copy)
            ins.then_inc(w_hi, 1)

        def unit_lo(e, u):
            e.wait_ge(w_hi, u + 1)
            e.wait_ge(stage_ld[u % 4], slot_count(u))
            s = w_lo_v if units[u][3] == "v" else w_lo_g
            for i, (st, h, l) in enumerate(unit_views(u)):
                ins = e.tensor_tensor(l, st, h.bitcast(F32), ALU.subtract)
            ins.then_inc(s, 1)

        def split3(pe, o, w_hl, x_hl, start, stop):
            (wh, wl), (xh, xl) = w_hl, x_hl
            pe.matmul(o, wh, xh, start=start, stop=False)
            pe.matmul(o, wh, xl, start=False, stop=False)
            return pe.matmul(o, wl, xh, start=False, stop=stop)

        def ln_sum_pool(g, L, blk):
            g.tensor_tensor(acc[:, :], blk(0), blk(1), ALU.add).then_inc(ln_pool, 1)
            for k in range(2, KB):
                since(g, ln_pool, L, 14, k - 1)
                g.tensor_tensor(acc[:, :], acc[:, :], blk(k), ALU.add).then_inc(ln_pool, 1)

        def ln_mean_pe(pe, L):
            since(pe, ln_pool, L, 14, 7)
            since(pe, ln_std, L - 1, 1, 1)
            pe.matmul(bank[LN_BANK][:, :], mean_w[:, :], acc[:, :], start=True, stop=True).then_inc(ln_mean, 1)

        def ln_center_dve(v, L, k, src, dst):
            if k == 0:
                since(v, ln_mean, L, 1, 1)
            v.tensor_tensor(dst, src, bank[LN_BANK][:, :], ALU.subtract).then_inc(ln_d, 1)

        def ln_square_act(act, L, k, d):
            since(act, ln_d, L, 8, k + 1)
            if k >= 2:
                since(act, ln_pool, L, 14, 7 + max(1, k - 2))
            act.activation(sq[:, k % 2, :], d, ACT.Square).then_inc(ln_sq, 1)

        def ln_var_pool(g, L):
            for k in range(1, KB):
                since(g, ln_sq, L, 8, k + 1)
                if k == 1:
                    g.tensor_tensor(vacc[:, :], sq[:, 0, :], sq[:, 1, :], ALU.add).then_inc(ln_pool, 1)
                else:
                    since(g, ln_pool, L, 14, 7 + k - 1)
                    g.tensor_tensor(vacc[:, :], vacc[:, :], sq[:, k % 2, :], ALU.add).then_inc(ln_pool, 1)

        def ln_var_pe(pe, L):
            since(pe, ln_pool, L, 14, 14)
            since(pe, ln_d, L, 8, 8)
            pe.matmul(bank[LN_BANK][:, :], mean_w[:, :], vacc[:, :], start=True, stop=True).then_inc(ln_var, 1)

        def ln_std_act(act, L, last_scale):
            since(act, ln_var, L, 1, 1)
            last_scale(act)
            act.activation(rstd[:, :], bank[LN_BANK][:, :], ACT.Sqrt, bias=eps[:, 0:1]).then_inc(ln_std, 1)

        def ln_rstd_dve(v, L):
            since(v, ln_std, L, 1, 1)
            v.reciprocal(rstd[:, :], rstd[:, :]).then_inc(ln_rstd, 1)
            since(v, ln_rstd, L, 1, 1)

        block = ctx.enter_context(nc.Block())

        @block.sync
        def _(sp):
            sp.dma_start(vec[:, :], vecs).then_inc(const_ld, 16)
            sp.wait_ge(const_ld, 16)
            sp.dma_start(bgen[:, :], b_gen.partition_broadcast(P)).then_inc(const_ld, 16)
            sp.wait_ge(const_ld, 32)
            sp.dma_start(rows[:, :], perm).then_inc(const_ld, 16)
            for k in range(KB):
                unit_load(sp, U_PROJ + k)
                sp.dma_start(xs[:, k, :], x_t[k * P:(k + 1) * P, 0:N]).then_inc(a_ld[k], 16)
            for k in range(KB):
                unit_load(sp, U_PROJ + KB + k)
            sp.wait_ge(zero_ok, 1)
            sp.dma_start(band_s.rearrange("(p n) -> p n", p=P), zero[:, :]).then_inc(band_zeroed, 16)

            def a_load(c):
                for k in range(KB):
                    sp.wait_ge(a_lo, (c - 1) * KB + k + 1)
                    sp.dma_start(xs[:, k, :], x_t[k * P:(k + 1) * P, c * N:(c + 1) * N]).then_inc(a_ld[k], 16)

            for c in range(CH):
                if c + 1 < CH:
                    a_load(c + 1)
                for g in range(2):
                    sp.wait_ge(a_ev, c * KB + 4 * g + 4)
                    sp.dma_start(h0_s[c, :, g * 4 * N:(g + 1) * 4 * N],
                                 ho[:, 4 * g:4 * g + 4, :]).then_inc(a_st[g], 16)
            def b_load(n):
                if n == 0:
                    sp.wait_ge(a_mm, CH * KB)
                else:
                    sp.wait_ge(yr_hi, n * KB)
                for g in range(2):
                    sp.wait_ge(a_st[g], 16 * (n + 1))
                sp.dma_start(db[:, :, :], h0_s[n]).then_inc(b_ld, 16)

            def band_move(n):
                sp.wait_ge(sm5, n * 7 + 7)
                sp.wait_ge(band_zeroed, 16)
                if n > 0:
                    sp.wait_ge(band_ld, 16 * n)
                dst = band_s.rearrange("(u n) -> u n", u=UNITS)[:, 0:P * (P + 1)]
                dst = dst.rearrange("u (t n) -> t u n", t=P)[:, :, 0:TAPS]
                sp.dma_start(dst, wk5[:, :, :]).then_inc(skewed, 16)
                sp.wait_ge(skewed, 16 * (n + 1))
                if n > 0:
                    sp.wait_ge(at_mm, n * KB)
                else:
                    sp.wait_ge(a_mm, CH * KB)
                src = band_s.rearrange("(u n) -> u n", u=UNITS)[:, TAPS - 1:TAPS - 1 + P * P]
                sp.dma_start(band[:, :, :], src.rearrange("u (t n) -> t u n", t=P)).then_inc(band_ld, 16)

            b_load(0)
            sp.wait_ge(a_st[0], 16 * CH)
            sp.wait_ge(a_st[1], 16 * CH)
            for u in range(U_FF, U_FF + 4):
                unit_load(sp, u)
            b_load(1)
            for u in range(U_FF + 4, U_V):
                unit_load(sp, u)
            band_move(0)

            def res_load(c, m):
                if 8 * c + m >= 2:
                    sp.wait_ge(ff_add, 8 * c + m - 1)
                sp.dma_start(res[:, m % 2, :], h0_s[c, :, m * N:(m + 1) * N]).then_inc(res_ld[m % 2], 16)

            def ff_store(c, m):
                sp.wait_ge(ff_add, 8 * c + m + 1)
                sp.dma_start(h1_s[c, :, m * N:(m + 1) * N], fo[:, m % 2, :]).then_inc(fo_st[m % 2], 16)

            for c in range(CH):
                res_load(c, 0)
                res_load(c, 1)
                if c + 2 < CH:
                    b_load(c + 2)
                for m in range(KB):
                    if m == 3 and c + 1 < CH:
                        band_move(c + 1)
                    ff_store(c, m)
                    if m + 2 < KB:
                        res_load(c, m + 2)
            def c_load(n):
                if n > 0:
                    sp.wait_ge(xc_lo, n * KB)
                for i in range(2):
                    sp.wait_ge(fo_st[i], 16 * 4 * (n + 1))
                sp.dma_start(dc[:, :, :], h1_s[n]).then_inc(c_ld, 16)

            sp.wait_ge(ff_mm, CH * KB)
            c_load(0)
            for u in range(U_V, U_O):
                unit_load(sp, u)

            def vo_store(c, m):
                sp.wait_ge(vo_ev, 8 * c + 2 * m + 2)
                sp.dma_start(vals_s[c, :, m * N:(m + 1) * N], vo[:, :]).then_inc(vo_st, 16)

            for c in range(CH):
                if c + 1 < CH:
                    c_load(c + 1)
                for m in range(PAIRS):
                    vo_store(c, m)
            def vs_load(c):
                if c == 0:
                    sp.wait_ge(pv_mm, 8 * CH)
                else:
                    sp.wait_ge(vs_lo, 4 * c)
                sp.wait_ge(vo_st, 16 * 4 * CH)
                sp.dma_start(vs[:, :, :], vals_s[c]).then_inc(vs_ld, 16)

            def h2_load(c, g):
                if c > 0:
                    sp.wait_ge(o_st[g], 16 * c)
                sp.dma_start(h2[:, 4 * g:4 * g + 4, :], h1_s[c, :, g * 4 * N:(g + 1) * 4 * N])\
                  .then_inc(o_ld[g], 16)

            vs_load(0)
            for u in range(U_O, U_UP):
                unit_load(sp, u)
                if u == U_O + 3:
                    h2_load(0, 0)
                    h2_load(0, 1)
            for u in range(U_UP, U_END):
                unit_load(sp, u)
            for c in range(CH):
                if c + 1 < CH:
                    vs_load(c + 1)
                for g in range(2):
                    sp.wait_ge(o_ev, 8 * c + 4 * g + 4)
                    sp.dma_start(h2_s[c][g * 4 * P:(g + 1) * 4 * P, :]
                                 .rearrange("(k p) n -> p k n", p=P),
                                 h2[:, 4 * g:4 * g + 4, :]).then_inc(o_st[g], 16)
                if c + 1 < CH:
                    for g in range(2):
                        h2_load(c + 1, g)
            sp.wait_ge(d_st, 16 * KB * CH)

        @block.gpsimd
        def _(g):
            for t, value in ((ident, 0.0), (mean_w, 1.0 / D), (eps, EPS), (valid, 1.0), (maskf, 1.0), (negs, OTHER)):
                g.memset(t[:, :], value).then_inc(masks_ok, 1)
            g.wait_ge(masks_ok, 6)
            g.affine_select(out=ident[:, :], in_=ident[:, :], compare_op=ALU.not_equal, fill=1.0, base=0,
                            pattern=[[-1, P]], channel_multiplier=1).then_inc(masks_ok, 1)
            for s in range(P // SEQ):
                part = slice(s * SEQ, (s + 1) * SEQ)
                g.wait_ge(masks_ok, 7 + 3 * s)
                g.affine_select(out=valid[part, :], in_=valid[part, :], compare_op=ALU.is_ge, fill=0.0,
                                base=1 - TAPS, pattern=[[1, TAPS]], channel_multiplier=1).then_inc(masks_ok, 1)
                g.wait_ge(masks_ok, 8 + 3 * s)
                g.affine_select(out=maskf[part, part], in_=maskf[part, part], compare_op=ALU.is_gt, fill=0.0,
                                base=0, pattern=[[1, SEQ]], channel_multiplier=-1).then_inc(masks_ok, 1)
                g.wait_ge(masks_ok, 9 + 3 * s)
                g.memset(negs[part, part], MASKED).then_inc(masks_ok, 1)
            g.wait_ge(masks_ok, 13)
            g.tensor_copy(masked[:, :], maskf[:, :]).then_inc(masks_ok, 1)
            g.memset(zero[:, :], 0.0).then_inc(zero_ok, 1)

            def b_sum(n):
                since(g, b_ld, n, 16, 16)
                ln_sum_pool(g, n, lambda k: db[:, k, :])

            b_sum(0)
            ln_var_pool(g, 0)
            for u in range(U_FF, U_FF + 4):
                unit_lo(g, u)
            b_sum(1)
            ln_var_pool(g, 1)
            for u in range(U_FF + 4, U_V):
                unit_lo(g, u)

            def b_add(c, m):
                since(g, ff_ev, c, 8, m + 1)
                since(g, res_ld[m % 2], c, 64, 16 * (m // 2 + 1))
                g.tensor_tensor(fo[:, m % 2, :], fo[:, m % 2, :], res[:, m % 2, :], ALU.add).then_inc(ff_add, 1)

            def b_step(c):
                b_sum(c + 2)
                for m in range(3):
                    b_add(c, m)
                ln_var_pool(g, c + 2)
                for m in range(3, KB):
                    b_add(c, m)

            with g.Fori(0, CH - 2) as c:
                b_step(c)
            with g.Fori(CH - 2, CH) as c:
                for m in range(KB):
                    b_add(c, m)

            def c_norm(n):
                since(g, c_ld, n, 16, 16)
                ln_sum_pool(g, n + CH, lambda k: dc[:, k, :])
                ln_var_pool(g, n + CH)

            c_norm(0)
            for u in range(U_V, U_O):
                if units[u][3] == "g":
                    unit_lo(g, u)
            with g.Fori(1, CH) as n:
                c_norm(n)
            for u in range(U_O, U_UP):
                unit_lo(g, u)
            g.memset(dn_h[:, :, :].bitcast(F32), 0.0).then_inc(dn_zero, 1)
            g.memset(dn_l[:, :, :].bitcast(F32), 0.0).then_inc(dn_zero, 1)
            g.wait_ge(dn_zero, 2)
            for u in range(U_UP, U_END):
                unit_lo(g, u)

            def gather(n):
                for half in range(2):
                    g.wait_ge(o_st[half], 16 * (n + 1))
                if n == 0:
                    g.wait_ge(o_mm, 8 * CH)
                if n >= 2:
                    g.wait_ge(d_st, 16 * KB * (n - 1))
                for k in range(KB):
                    g.indirect_dma_start(out=hg[:, (n % 2) * KB + k, :], out_offset=None, in_=h2_s[n],
                                         in_offset=bass.IndirectOffsetOnAxis(ap=rows[:, k:k + 1], axis=0))\
                     .then_inc(g_ld, 16)

            def d_norm(n):
                g.wait_ge(g_ld, 16 * KB * (n + 1))
                ln_sum_pool(g, n + 2 * CH, lambda k: hg[:, (n % 2) * KB + k, :])
                ln_var_pool(g, n + 2 * CH)

            g.wait_ge(const_ld, 48)
            gather(0)
            d_norm(0)
            for c in range(CH):
                if c + 1 < CH:
                    gather(c + 1)
                    d_norm(c + 1)
                for k in range(KB):
                    g.wait_ge(d_ev, 8 * c + k + 1)
                    g.indirect_dma_start(out=outs[c],
                                         out_offset=bass.IndirectOffsetOnAxis(ap=rows[:, k:k + 1], axis=0),
                                         in_=hg[:, (c % 2) * KB + k, :], in_offset=None).then_inc(d_st, 16)
            g.wait_ge(d_st, 16 * KB * CH)

        @block.scalar
        def _(act):
            act.dma_start(wg_raw[:, :, :], w_gen.rearrange("(k p) n -> p k n", p=P)).then_inc(wg_ok, 16)
            act.wait_ge(const_ld, 48)

            def a_high(c, k):
                since(act, a_ld[k], c, 16, 16)
                released(act, c - 1, k, KB, a_used, a_mm)
                act.activation(xa_h[:, k, :], xs[:, k, :], ACT.Copy).then_inc(a_hi, 1)

            for k in range(KB):
                unit_hi(act, U_PROJ + k)
                a_high(0, k)
            for k in range(KB):
                unit_hi(act, U_PROJ + KB + k)
            act.wait_ge(wg_ok, 16)
            act.activation(wg_h[:, :, :], wg_raw[:, :, :], ACT.Copy).then_inc(wg_ok, 1)

            def a_evac(c, grp):
                since(act, a_st[grp], c, 16, 0)
                for m in range(4 * grp, 4 * grp + 4):
                    since(act, a_mm, c, 8, m + 1)
                    act.activation(ho[:, m, :], bank[m][:, :], ACT.Identity,
                                   bias=vec[:, B_PROJ + m:B_PROJ + m + 1]).then_inc(a_ev, 1)

            def a_step(c):
                a_evac(c, 0)
                for k in range(KB):
                    a_high(c + 1, k)
                a_evac(c, 1)

            chunks(act, 0, CH - 1, a_step)
            a_evac(CH - 1, 0)
            a_evac(CH - 1, 1)

            def b_squares(n):
                for k in range(KB):
                    ln_square_act(act, n, k, db[:, k, :])

            def b_std(n):
                ln_std_act(act, n, lambda e: since(e, y_scaled, n - 1, 8, 8))

            def y_make(n, k):
                since(act, y_scaled, n, 8, k + 1)
                if k == 0:
                    since(act, yt_mm, n - 1, 8, 8)
                bias = vec[:, LN_B + k:LN_B + k + 1]
                act.activation(yb[:, k, :], db[:, k, :], ACT.Identity, bias=bias).then_inc(y_b, 1)
                since(act, yr_used, n, 8, k - 1)
                act.activation(yr_h[:, k % 2, :], db[:, k, :], ACT.Identity, bias=bias).then_inc(yr_hi, 1)

            def gates(n):
                since(act, yr_used, n, 8, 8)
                since(act, lgt_mm, n - 1, 1, 1)
                act.activation(lg[:, :], bank[7][0:LOGITS, :], ACT.Copy).then_inc(lg_ev, 1)
                since(act, sm5, n, 7, 3)
                act.activation(lg5[:, :, :], lg5[:, :, :], ACT.Exp).then_inc(exp5, 1)

            def conv_evac(n):
                for h in range(CONV_HEADS + 1):
                    if h < CONV_HEADS:
                        since(act, yt_mm, n, 8, h + 1)
                        since(act, cv_mm, n, 8, h - 1)
                        act.activation(yt_h[:, h % 2, :], bank[2 + h % 2][:, :], ACT.Copy).then_inc(yt_hi, 1)
                        since(act, at_mm, n, 8, h + 1)
                        act.activation(ar_h[:, h % 2, :], bank[4 + h % 2][:, :], ACT.Copy).then_inc(ar_hi, 1)
                    if h >= 1:
                        since(act, cv_mm, n, 8, h)
                        act.activation(cv_h[:, h - 1, :], bank[(h - 1) % 2][:, :], ACT.Copy).then_inc(cv_hi, 1)

            def ff_relu(c, m):
                since(act, ff_mm, c, 8, m + 1)
                since(act, fo_st[m % 2], c, 64, 16 * (m // 2))
                b = FF_BANK[m]
                act.activation(fo[:, m % 2, :], bank[b][:, :], ACT.Relu,
                               bias=vec[:, B_FF + m:B_FF + m + 1]).then_inc(ff_ev, 1)

            b_squares(0)
            b_std(0)
            for k in range(KB):
                y_make(0, k)
            for grp in range(2):
                act.wait_ge(a_st[grp], 16 * CH)
            act.wait_ge(band_zeroed, 16)
            for u in range(U_FF, U_FF + 4):
                unit_hi(act, u)
            gates(0)
            b_squares(1)
            for u in range(U_FF + 4, U_V):
                unit_hi(act, u)
            b_std(1)
            conv_evac(0)

            def b_step(c, ahead):
                n = c + 1
                for k in range(KB):
                    y_make(n, k)
                gates(n)
                for m in range(3):
                    ff_relu(c, m)
                if ahead:
                    b_squares(c + 2)
                for m in range(3, 6):
                    ff_relu(c, m)
                if ahead:
                    b_std(c + 2)
                for m in range(6, KB):
                    ff_relu(c, m)
                conv_evac(n)

            chunks(act, 0, CH - 2, lambda c: b_step(c, True))
            b_step(CH - 2, False)
            for m in range(KB):
                ff_relu(CH - 1, m)

            def c_squares(n):
                for k in range(KB):
                    ln_square_act(act, n + CH, k, dc[:, k, :])

            def c_std(n):
                if isinstance(n, int) and n == 0:
                    last = lambda e: e.wait_ge(y_scaled, 8 * CH)
                else:
                    last = lambda e: since(e, xc_sc, n - 1, 8, 8)
                ln_std_act(act, n + CH, last)

            def xc_high(n, k):
                since(act, xc_sc, n, 8, k + 1)
                released(act, n - 1, k, KB, xc_used, qk_mm)
                act.activation(xc_h[:, k, :], dc[:, k, :], ACT.Copy).then_inc(xc_hi, 1)

            def c_softmax_exp(c, m):
                for j in range(2):
                    since(act, s_sub, c, 8, 2 * m + j + 1)
                    act.activation(pr[:, j, :], pr[:, j, :], ACT.Exp).then_inc(s_exp, 1)

            def c_qk(c, m):
                for i, b0 in ((0, B_Q), (1, B_K)):
                    since(act, qk_mm, c, 8, 2 * m + i + 1)
                    if i == 0:
                        since(act, s_mm, c, 8, 2 * m)
                    act.activation(qk_h[:, i, :], bank[i][:, :], ACT.Identity,
                                   bias=vec[:, b0 + m:b0 + m + 1]).then_inc(qk_hi, 1)

            def c_pt(c, m):
                for j in range(2):
                    since(act, pt_mm, c, 8, 2 * m + j + 1)
                    since(act, pv_mm, c, 8, 2 * m + j - 1)
                    act.activation(pt_h[:, j, :], bank[PT_BANK[j]][:, :], ACT.Copy).then_inc(pt_hi, 1)

            def c_vals(c, m):
                for j in range(2):
                    rowsj = slice(HEAD * j, HEAD * j + HEAD)
                    since(act, pv_mm, c, 8, 2 * m + j + 1)
                    if j == 0:
                        since(act, vo_st, c, 64, 16 * m)
                    act.activation(vo[rowsj, :], bank[7][rowsj, :], ACT.Identity,
                                   bias=vec[rowsj, B_V + m:B_V + m + 1]).then_inc(vo_ev, 1)

            c_squares(0)
            c_std(0)
            for k in range(KB):
                xc_high(0, k)
            for u in range(U_V, U_O):
                unit_hi(act, u)

            def c_step(c, ahead):
                for t in range(TILES):
                    since(act, v_mm, c, 4, t + 1)
                    since(act, pv_mm, c - 1, 8, 8)
                    act.activation(v_h[:, t, :], bank[t][:, :], ACT.Copy).then_inc(v_hi, 1)
                c_qk(c, 0)
                c_softmax_exp(c, 0)
                c_qk(c, 1)
                c_pt(c, 0)
                c_softmax_exp(c, 1)
                if ahead:
                    c_squares(c + 1)
                c_qk(c, 2)
                c_vals(c, 0)
                c_pt(c, 1)
                c_softmax_exp(c, 2)
                if ahead:
                    c_std(c + 1)
                if ahead:
                    for k in range(KB):
                        xc_high(c + 1, k)
                c_qk(c, 3)
                c_vals(c, 1)
                c_pt(c, 2)
                c_softmax_exp(c, 3)
                c_vals(c, 2)
                c_pt(c, 3)
                c_vals(c, 3)

            chunks(act, 0, CH - 1, lambda c: c_step(c, True))
            c_step(CH - 1, False)

            def vs_high(c):
                for k in range(PAIRS):
                    since(act, vs_ld, c, 16, 16)
                    released(act, c - 1, k, PAIRS, vs_used, o_mm)
                    act.activation(vs_h[:, k, :], vs[:, k, :], ACT.Copy).then_inc(vs_hi, 1)

            vs_high(0)
            for u in range(U_O, U_UP):
                unit_hi(act, u)
            act.wait_ge(dn_zero, 2)
            for u in range(U_UP, U_END):
                unit_hi(act, u)
            with act.Fori(1, CH) as c:
                vs_high(c)

            def d_squares(n):
                for k in range(KB):
                    ln_square_act(act, n + 2 * CH, k, dd[:, k, :])

            def d_std(n):
                if isinstance(n, int) and n == 0:
                    last = lambda e: e.wait_ge(xc_sc, 8 * CH)
                else:
                    last = lambda e: since(e, xd_sc, n - 1, 8, 8)
                ln_std_act(act, n + 2 * CH, last)

            def xd_high(n, k):
                since(act, xd_sc, n, 8, k + 1)
                since(act, up_mm, n - 1, 32, 4 * k + 4)
                act.activation(xd_h[:, k, :], dd[:, k, :], ACT.Copy).then_inc(xd_hi, 1)

            def gelus(c, a):
                for i in range(FFB):
                    since(act, up_mm, c, 32, 4 * a + i + 1)
                    since(act, g_lo, c, 32, 4 * a + i - 3)
                    act.activation(gt[:, i, :], bank[i][:, :], ACT.Gelu).then_inc(gelu_ok, 1)
                    since(act, gelu_ok, c, 32, 4 * a + i + 1)
                    since(act, g_used, c, 32, 4 * a + i - 3)
                    act.activation(g_h[:, i, :], gt[:, i, :], ACT.Copy).then_inc(g_hi, 1)

            d_squares(0)
            d_std(0)
            for k in range(KB):
                xd_high(0, k)

            def d_step(c, ahead):
                for a in range(KB):
                    gelus(c, a)
                    if ahead and a == 4:
                        for k in range(4):
                            ln_square_act(act, c + 1 + 2 * CH, k, dd[:, k, :])
                    if ahead and a == 5:
                        for k in range(4, KB):
                            ln_square_act(act, c + 1 + 2 * CH, k, dd[:, k, :])
                if ahead:
                    d_std(c + 1)
                    for k in range(KB):
                        xd_high(c + 1, k)

            chunks(act, 0, CH - 1, lambda c: d_step(c, True))
            d_step(CH - 1, False)

        @block.vector
        def _(v):
            def a_low(c, k):
                since(v, a_hi, c, 8, k + 1)
                v.tensor_tensor(xa_l[:, k, :], xs[:, k, :], xa_h[:, k, :].bitcast(F32),
                                ALU.subtract).then_inc(a_lo, 1)

            for k in range(KB):
                unit_lo(v, U_PROJ + k)
                a_low(0, k)
            for k in range(KB):
                unit_lo(v, U_PROJ + KB + k)
            v.wait_ge(wg_ok, 17)
            v.tensor_tensor(wg_l[:, :, :], wg_raw[:, :, :], wg_h[:, :, :].bitcast(F32), ALU.subtract).then_inc(wg_ok, 1)
            with v.Fori(1, CH) as c:
                for k in range(KB):
                    a_low(c, k)

            def b_center(n):
                for k in range(KB):
                    ln_center_dve(v, n, k, db[:, k, :], db[:, k, :])

            def y_scale(n, k):
                if k == 0:
                    ln_rstd_dve(v, n)
                    since(v, ln_sq, n, 8, 8)
                v.scalar_tensor_tensor(out=db[:, k, :], in0=db[:, k, :], scalar=vec[:, LN_G + k:LN_G + k + 1],
                                       in1=rstd[:, :], op0=ALU.mult, op1=ALU.mult).then_inc(y_scaled, 1)

            def y_low(n, k):
                since(v, y_b, n, 8, k + 1)
                since(v, yr_hi, n, 8, k + 1)
                v.tensor_tensor(yr_l[:, k % 2, :], yb[:, k, :], yr_h[:, k % 2, :].bitcast(F32),
                                ALU.subtract).then_inc(yr_lo, 1)

            def y_split(n):
                y_scale(n, 0)
                for k in range(KB):
                    if k + 1 < KB:
                        y_scale(n, k + 1)
                    y_low(n, k)

            def gates(n):
                since(v, lgt_mm, n, 1, 1)
                since(v, skewed, n - 1, 16, 16)
                per = [P, UNITS, TAPS]
                v.tensor_tensor(lg5[:, :, :].rearrange("p (t h) k -> p t (h k)", t=TILES),
                                bank[7][:, 0:TILES * LOGITS].rearrange("p (t n) -> p t n", t=TILES),
                                bgen[:, :].unsqueeze(1).to_broadcast([P, TILES, LOGITS]),
                                ALU.add).then_inc(sm5, 1)
                since(v, sm5, n, 7, 1)
                v.tensor_reduce(mx5[:, :], lg5[:, :, :], AX.X, ALU.max).then_inc(sm5, 1)
                since(v, sm5, n, 7, 2)
                v.tensor_tensor(lg5[:, :, :], lg5[:, :, :], mx5[:, :].unsqueeze(2).to_broadcast(per),
                                ALU.subtract).then_inc(sm5, 1)
                since(v, exp5, n, 1, 1)
                v.tensor_reduce(su5[:, :], lg5[:, :, :], AX.X, ALU.add).then_inc(sm5, 1)
                since(v, sm5, n, 7, 4)
                v.reciprocal(su5[:, :], su5[:, :]).then_inc(sm5, 1)
                v.tensor_tensor(wk5[:, :, :], lg5[:, :, :], valid[:, :].unsqueeze(1).to_broadcast(per),
                                ALU.mult).then_inc(sm5, 1)
                since(v, sm5, n, 7, 6)
                v.tensor_tensor(wk5[:, :, :], wk5[:, :, :], su5[:, :].unsqueeze(2).to_broadcast(per),
                                ALU.mult).then_inc(sm5, 1)

            def conv_evac(n):
                for h in range(CONV_HEADS + 1):
                    if h < CONV_HEADS:
                        since(v, yt_hi, n, 8, h + 1)
                        v.tensor_tensor(yt_l[:, h % 2, :], bank[2 + h % 2][:, :],
                                        yt_h[:, h % 2, :].bitcast(F32), ALU.subtract).then_inc(yt_lo, 1)
                        since(v, ar_hi, n, 8, h + 1)
                        v.tensor_tensor(ar_l[:, h % 2, :], bank[4 + h % 2][:, :],
                                        ar_h[:, h % 2, :].bitcast(F32), ALU.subtract).then_inc(ar_lo, 1)
                    if h >= 1:
                        since(v, cv_hi, n, 8, h)
                        v.tensor_tensor(cv_l[:, h - 1, :], bank[(h - 1) % 2][:, :],
                                        cv_h[:, h - 1, :].bitcast(F32), ALU.subtract).then_inc(cv_lo, 1)

            v.wait_ge(masks_ok, 14)
            b_center(0)
            y_split(0)
            gates(0)
            b_center(1)
            conv_evac(0)

            def b_step(c, ahead):
                y_split(c + 1)
                gates(c + 1)
                if ahead:
                    b_center(c + 2)
                conv_evac(c + 1)

            chunks(v, 0, CH - 2, lambda c: b_step(c, True))
            b_step(CH - 2, False)

            def c_center(n):
                for k in range(KB):
                    ln_center_dve(v, n + CH, k, dc[:, k, :], dc[:, k, :])

            def c_scale(n):
                ln_rstd_dve(v, n + CH)
                since(v, ln_sq, n + CH, 8, 8)
                for k in range(KB):
                    v.tensor_tensor(dc[:, k, :], dc[:, k, :], rstd[:, :], ALU.mult).then_inc(xc_sc, 1)

            def xc_low(n, k):
                since(v, xc_hi, n, 8, k + 1)
                since(v, xc_sc, n, 8, k + 1)
                v.tensor_tensor(xc_l[:, k, :], dc[:, k, :], xc_h[:, k, :].bitcast(F32),
                                ALU.subtract).then_inc(xc_lo, 1)

            def c_qk(c, m):
                for i, b0 in ((0, B_Q), (1, B_K)):
                    since(v, qk_hi, c, 8, 2 * m + i + 1)
                    v.scalar_tensor_tensor(out=qk_l[:, i, :], in0=bank[i][:, :],
                                           scalar=vec[:, b0 + m:b0 + m + 1], in1=qk_h[:, i, :].bitcast(F32),
                                           op0=ALU.add, op1=ALU.subtract).then_inc(qk_lo, 1)

            def c_softmax_in(c, m):
                for j in range(2):
                    i = 2 * m + j + 1
                    S = bank[4 + j]
                    view = S[:, :].rearrange("p (t n) -> p t n", t=TILES)
                    since(v, s_mm, c, 8, i)
                    v.memset(smax[:, j, :], 0.0)
                    v.copy_predicated(view, masked[:, :].unsqueeze(1).to_broadcast([P, TILES, P]),
                                      negs[:, :].unsqueeze(1).to_broadcast([P, TILES, P])).then_inc(s_masked, 1)
                    since(v, s_masked, c, 8, i)
                    v.tensor_reduce(smax[:, j, :], view, AX.X, ALU.max).then_inc(s_max, 1)
                    since(v, s_max, c, 8, i)
                    since(v, pt_mm, c, 8, i - 2)
                    v.tensor_tensor(pr[:, j, :].rearrange("p (t n) -> p t n", t=TILES), view,
                                    smax[:, j, :].unsqueeze(2).to_broadcast([P, TILES, P]),
                                    ALU.subtract).then_inc(s_sub, 1)

            def c_softmax_out(c, m):
                for j in range(2):
                    i = 2 * m + j + 1
                    view = pr[:, j, :].rearrange("p (t n) -> p t n", t=TILES)
                    since(v, s_exp, c, 8, i)
                    v.tensor_reduce(ssum[:, j, :], view, AX.X, ALU.add).then_inc(s_sum, 1)
                    since(v, s_sum, c, 8, i)
                    v.reciprocal(ssum[:, j, :], ssum[:, j, :]).then_inc(s_rec, 1)
                    since(v, s_rec, c, 8, i)
                    v.tensor_tensor(view, view, ssum[:, j, :].unsqueeze(2).to_broadcast([P, TILES, P]),
                                    ALU.mult).then_inc(s_norm, 1)

            def c_pt(c, m):
                for j in range(2):
                    since(v, pt_hi, c, 8, 2 * m + j + 1)
                    v.tensor_tensor(pt_l[:, j, :], bank[PT_BANK[j]][:, :], pt_h[:, j, :].bitcast(F32),
                                    ALU.subtract).then_inc(pt_lo, 1)

            c_center(0)
            c_scale(0)
            for k in range(KB):
                xc_low(0, k)
            for u in range(U_V, U_O):
                if units[u][3] == "v":
                    unit_lo(v, u)

            def c_step(c, ahead):
                for t in range(TILES):
                    since(v, v_hi, c, 4, t + 1)
                    v.tensor_tensor(v_l[:, t, :], bank[t][:, :], v_h[:, t, :].bitcast(F32),
                                    ALU.subtract).then_inc(v_lo, 1)
                c_qk(c, 0)
                c_softmax_in(c, 0)
                c_softmax_out(c, 0)
                if ahead:
                    c_center(c + 1)
                c_qk(c, 1)
                c_pt(c, 0)
                c_softmax_in(c, 1)
                c_softmax_out(c, 1)
                c_qk(c, 2)
                c_pt(c, 1)
                c_softmax_in(c, 2)
                c_softmax_out(c, 2)
                if ahead:
                    c_scale(c + 1)
                    for k in range(KB):
                        xc_low(c + 1, k)
                c_qk(c, 3)
                c_pt(c, 2)
                c_softmax_in(c, 3)
                c_softmax_out(c, 3)
                c_pt(c, 3)

            chunks(v, 0, CH - 1, lambda c: c_step(c, True))
            c_step(CH - 1, False)

            def o_low(c):
                for k in range(PAIRS):
                    since(v, vs_hi, c, 4, k + 1)
                    v.tensor_tensor(vs_l[:, k, :], vs[:, k, :], vs_h[:, k, :].bitcast(F32),
                                    ALU.subtract).then_inc(vs_lo, 1)

            def o_evac(c, grp):
                since(v, o_ld[grp], c, 16, 16)
                for m in range(4 * grp, 4 * grp + 4):
                    since(v, o_mm, c, 8, m + 1)
                    v.scalar_tensor_tensor(out=h2[:, m, :], in0=bank[m][:, :], scalar=vec[:, B_O + m:B_O + m + 1],
                                           in1=h2[:, m, :], op0=ALU.add, op1=ALU.add).then_inc(o_ev, 1)

            o_low(0)

            def o_step(c):
                o_evac(c, 0)
                o_low(c + 1)
                o_evac(c, 1)

            with v.Fori(0, CH - 1) as c:
                o_step(c)
            o_evac(CH - 1, 0)
            o_evac(CH - 1, 1)

            def d_center(n, ks):
                par = (n % 2) * KB
                for k in ks:
                    if k == 0:
                        since(v, xd_lo, n - 1, 8, 8)
                        since(v, xd_hi, n - 1, 8, 8)
                    if isinstance(n, int):
                        src = hg[:, par + k, :]
                        dst = dd[:, k, :]
                    else:
                        src = hg[:, bass.ds(par + k, 1), :]
                        dst = dd[:, k:k + 1, :]
                    if k == 0:
                        since(v, ln_mean, n + 2 * CH, 1, 1)
                    mean = bank[LN_BANK][:, :] if isinstance(n, int) else bank[LN_BANK][:, :].unsqueeze(1)
                    v.tensor_tensor(dst, src, mean, ALU.subtract).then_inc(ln_d, 1)

            def d_scale(n):
                ln_rstd_dve(v, n + 2 * CH)
                since(v, ln_sq, n + 2 * CH, 8, 8)
                for k in range(KB):
                    v.tensor_tensor(dd[:, k, :], dd[:, k, :], rstd[:, :], ALU.mult).then_inc(xd_sc, 1)
                    since(v, xd_hi, n, 8, k + 1)
                    v.tensor_tensor(xd_l[:, k, :], dd[:, k, :], xd_h[:, k, :].bitcast(F32),
                                    ALU.subtract).then_inc(xd_lo, 1)

            def d_add(c, a):
                since(v, g_used, c, 32, 4 * a + 4)
                if isinstance(c, int):
                    dst, src = hg[:, (c % 2) * KB + a, :], bank[4 + a % 2][:, :]
                else:
                    dst, src = hg[:, bass.ds((c % 2) * KB + a, 1), :], bank[4 + a % 2][:, :].unsqueeze(1)
                v.tensor_tensor(dst, src, dst, ALU.add).then_inc(d_ev, 1)

            d_center(0, range(KB))
            for grp in range(2):
                v.wait_ge(o_st[grp], 16 * CH)
            d_scale(0)

            def d_step(c, ahead):
                for a in range(KB):
                    for i in range(FFB):
                        since(v, g_hi, c, 32, 4 * a + i + 1)
                        v.tensor_tensor(g_l[:, i, :], gt[:, i, :], g_h[:, i, :].bitcast(F32),
                                        ALU.subtract).then_inc(g_lo, 1)
                    if a >= 1:
                        d_add(c, a - 1)
                    if ahead and a == 4:
                        d_center(c + 1, range(4))
                    if ahead and a == 5:
                        d_center(c + 1, range(4, KB))
                if ahead:
                    d_scale(c + 1)
                d_add(c, KB - 1)

            chunks(v, 0, CH - 1, lambda c: d_step(c, True))
            d_step(CH - 1, False)

        @block.tensor
        def _(pe):
            pe.wait_ge(masks_ok, 14)

            def a_step(c):
                for grp in range(2):
                    since(pe, a_ev, c - 1, 8, 4 * grp + 4)
                    for k in range(KB):
                        if grp == 0:
                            since(pe, a_lo, c, 8, k + 1)
                        if isinstance(c, int) and c == 0:
                            wait_units(pe, U_PROJ + KB * grp + k + 1)
                        for m in range(4 * grp, 4 * grp + 4):
                            cols = slice(m * P, (m + 1) * P)
                            mm = split3(pe, bank[m][:, :], (wp_h[:, k, cols], wp_l[:, k, cols]),
                                        (xa_h[:, k, :], xa_l[:, k, :]), k == 0, k == KB - 1)
                            if k == KB - 1:
                                mm.then_inc(a_mm, 1)
                        if grp == 1 and k < KB - 1:
                            mm.then_inc(a_used, 1)

            chunks(pe, 0, CH, a_step)

            def gate_block(n, k):
                since(pe, yr_lo, n, 8, k + 1)
                if k == 0:
                    since(pe, sm5, n - 1, 7, 1)
                mm = split3(pe, bank[7][0:LOGITS, :], (wg_h[:, k, :], wg_l[:, k, :]),
                            (yr_h[:, k % 2, :], yr_l[:, k % 2, :]), k == 0, k == KB - 1)
                mm.then_inc(yr_used, 1)

            def gate_turn(n):
                since(pe, lg_ev, n, 1, 1)
                for t in range(TILES):
                    mm = pe.transpose(bank[7][:, t * LOGITS:(t + 1) * LOGITS], lg[:, t * P:(t + 1) * P],
                                      ident[0:LOGITS, 0:LOGITS])
                mm.then_inc(lgt_mm, 1)

            def conv(n):
                def turn(h):
                    if h == 0:
                        since(pe, y_b, n, 8, 8)
                        since(pe, ff_ev, n - 1, 8, 6)
                        since(pe, band_ld, n, 16, 16)
                    if h >= 2:
                        since(pe, yt_lo, n, 8, h - 1)
                    for t in range(TILES):
                        mm = pe.transpose(bank[2 + h % 2][:, t * P:(t + 1) * P], yb[:, h, t * P:(t + 1) * P],
                                          ident[:, :])
                    mm.then_inc(yt_mm, 1)
                    if h >= 2:
                        since(pe, ar_lo, n, 8, h - 1)
                    for t in range(TILES):
                        mm = pe.transpose(bank[4 + h % 2][:, t * P:(t + 1) * P], band[:, t * CONV_HEADS + h, :],
                                          ident[:, :])
                    mm.then_inc(at_mm, 1)

                turn(0)
                for h in range(CONV_HEADS):
                    if h + 1 < CONV_HEADS:
                        turn(h + 1)
                    if h == 0:
                        since(pe, ff_ev, n - 1, 8, 8)
                    if h >= 2:
                        since(pe, cv_lo, n, 8, h - 1)
                    since(pe, yt_lo, n, 8, h + 1)
                    since(pe, ar_lo, n, 8, h + 1)
                    for t in range(TILES):
                        cols = slice(t * P, (t + 1) * P)
                        mm = split3(pe, bank[h % 2][:, cols], (yt_h[:, h % 2, cols], yt_l[:, h % 2, cols]),
                                    (ar_h[:, h % 2, cols], ar_l[:, h % 2, cols]), True, True)
                    mm.then_inc(cv_mm, 1)

            def ff_block(c, ms, k):
                if k == 0 and ms[0] == 0:
                    since(pe, cv_lo, c, 8, 8)
                if isinstance(c, int) and c == 0:
                    wait_units(pe, U_FF + (0 if ms[-1] < 4 else KB) + k + 1)
                for m in ms:
                    cols = slice(m * P, (m + 1) * P)
                    mm = split3(pe, bank[FF_BANK[m]][:, :], (wf_h[:, k, cols], wf_l[:, k, cols]),
                                (cv_h[:, k, :], cv_l[:, k, :]), k == 0, k == KB - 1)
                    if k == KB - 1:
                        mm.then_inc(ff_mm, 1)

            def b_step(c, gate, ahead):
                for k in range(KB):
                    ff_block(c, [0, 1, 2], k)
                    if gate:
                        gate_block(c + 1, k)
                for k in range(KB):
                    ff_block(c, [3, 4, 5], k)
                    if gate and k == 1:
                        gate_turn(c + 1)
                    if ahead and k == 4:
                        ln_mean_pe(pe, c + 2)
                since(pe, ff_ev, c, 8, 2)
                for k in range(KB):
                    ff_block(c, [6, 7], k)
                if ahead:
                    ln_var_pe(pe, c + 2)
                if gate:
                    conv(c + 1)

            pe.wait_ge(wg_ok, 18)
            pe.wait_ge(a_ev, 8 * CH)
            ln_mean_pe(pe, 0)
            ln_var_pe(pe, 0)
            for k in range(KB):
                gate_block(0, k)
            gate_turn(0)
            ln_mean_pe(pe, 1)
            ln_var_pe(pe, 1)
            conv(0)
            chunks(pe, 0, CH - 2, lambda c: b_step(c, True, True))
            b_step(CH - 2, True, False)
            b_step(CH - 1, False, False)

            def c_values(c):
                if isinstance(c, int) and c == 0:
                    pe.wait_ge(ff_ev, 8 * CH)
                since(pe, qk_lo, c - 1, 8, 8)
                since(pe, pt_lo, c - 1, 8, 8)
                since(pe, ln_std, c + CH, 1, 1)
                for k in range(KB):
                    since(pe, xc_lo, c, 8, k + 1)
                    if isinstance(c, int) and c == 0:
                        wait_units(pe, U_V + k + 1)
                    for t in range(TILES):
                        cols = slice(t * P, (t + 1) * P)
                        mm = split3(pe, bank[t][:, :], (xc_h[:, k, cols], xc_l[:, k, cols]),
                                    (wv_h[:, k, :], wv_l[:, k, :]), k == 0, k == KB - 1)
                        if k == KB - 1:
                            mm.then_inc(v_mm, 1)

            def c_qk(c, m):
                if m == 0:
                    since(pe, v_lo, c, 4, 2)
                    if isinstance(c, int) and c == 0:
                        wait_units(pe, U_O)
                cols = slice(m * P, (m + 1) * P)
                for k in range(KB):
                    for i, (wh, wl) in enumerate(((wq_h, wq_l), (wk_h, wk_l))):
                        mm = split3(pe, bank[i][:, :], (wh[:, k, cols], wl[:, k, cols]),
                                    (xc_h[:, k, :], xc_l[:, k, :]), k == 0, k == KB - 1)
                        if k == KB - 1:
                            mm.then_inc(qk_mm, 1)
                    if m == PAIRS - 1 and k < KB - 1:
                        mm.then_inc(xc_used, 1)

            def c_scores(c, m):
                since(pe, qk_lo, c, 8, 2 * m + 2)
                for j in range(2):
                    since(pe, s_sub, c, 8, 2 * m + j - 1)
                    r = slice(HEAD * j, HEAD * j + HEAD)
                    for t in range(TILES):
                        cols = slice(t * P, (t + 1) * P)
                        mm = split3(pe, bank[4 + j][:, cols], (qk_h[r, 0, cols], qk_l[r, 0, cols]),
                                    (qk_h[r, 1, cols], qk_l[r, 1, cols]), True, True)
                    mm.then_inc(s_mm, 1)

            def c_turn(c, m):
                for j in range(2):
                    since(pe, s_norm, c, 8, 2 * m + j + 1)
                    if m == 0 and j == 0:
                        since(pe, v_lo, c, 4, 4)
                    since(pe, pt_lo, c, 8, 2 * m + j - 1)
                    for t in range(TILES):
                        cols = slice(t * P, (t + 1) * P)
                        mm = pe.transpose(bank[PT_BANK[j]][:, cols], pr[:, j, cols], ident[:, :])
                    mm.then_inc(pt_mm, 1)

            def c_mix(c, m):
                for j in range(2):
                    since(pe, pt_lo, c, 8, 2 * m + j + 1)
                    since(pe, vo_ev, c, 8, 2 * m + j)
                    since(pe, v_lo, c, 4, 4)
                    for t in range(TILES):
                        cols = slice(t * P, (t + 1) * P)
                        pair = slice(m * P, (m + 1) * P)
                        mm = split3(pe, bank[7][:, cols], (v_h[:, t, pair], v_l[:, t, pair]),
                                    (pt_h[:, j, cols], pt_l[:, j, cols]), True, True)
                    mm.then_inc(pv_mm, 1)

            def c_step(c, ahead):
                c_values(c)
                c_qk(c, 0)
                c_scores(c, 0)
                if ahead:
                    ln_mean_pe(pe, c + 1 + CH)
                c_qk(c, 1)
                c_turn(c, 0)
                c_scores(c, 1)
                c_qk(c, 2)
                c_mix(c, 0)
                c_turn(c, 1)
                c_scores(c, 2)
                if ahead:
                    ln_var_pe(pe, c + 1 + CH)
                c_qk(c, 3)
                c_mix(c, 1)
                c_turn(c, 2)
                c_scores(c, 3)
                c_mix(c, 2)
                c_turn(c, 3)
                c_mix(c, 3)

            ln_mean_pe(pe, CH)
            ln_var_pe(pe, CH)
            chunks(pe, 0, CH - 1, lambda c: c_step(c, True))
            c_step(CH - 1, False)

            def o_step(c):
                if isinstance(c, int) and c == 0:
                    pe.wait_ge(vo_ev, 8 * CH)
                for grp in range(2):
                    since(pe, o_ev, c - 1, 8, 4 * grp + 4)
                    for k in range(PAIRS):
                        if grp == 0:
                            since(pe, vs_lo, c, 4, k + 1)
                        if isinstance(c, int) and c == 0:
                            wait_units(pe, U_O + PAIRS * grp + k + 1)
                        for m in range(4 * grp, 4 * grp + 4):
                            cols = slice(m * P, (m + 1) * P)
                            mm = split3(pe, bank[m][:, :], (wo_h[:, k, cols], wo_l[:, k, cols]),
                                        (vs_h[:, k, :], vs_l[:, k, :]), k == 0, k == PAIRS - 1)
                            if k == PAIRS - 1:
                                mm.then_inc(o_mm, 1)
                        if grp == 1 and k < PAIRS - 1:
                            mm.then_inc(vs_used, 1)

            chunks(pe, 0, CH, o_step)

            def ff_up(c, a, i):
                j, blk = i // 2, i % 2
                if i == 0:
                    since(pe, xd_lo, c, 8, a + 1)
                since(pe, gelu_ok, c, 32, 4 * a + i - 3)
                r = slice(FF_IN * j, FF_IN * (j + 1))
                cols = slice(blk * P, (blk + 1) * P)
                mm = split3(pe, bank[i][:, :], (up_h[r, a, cols], up_l[r, a, cols]),
                            (xd_h[r, a, :], xd_l[r, a, :]), True, True)
                mm.then_inc(up_mm, 1)

            def ff_down(c, a, i):
                since(pe, g_lo, c, 32, 4 * a + i + 1)
                if i == 0:
                    since(pe, d_ev, c, 8, a - 1)
                mm = split3(pe, bank[4 + a % 2][:, :], (dn_h[:, FFB * a + i, :], dn_l[:, FFB * a + i, :]),
                            (g_h[:, i, :], g_l[:, i, :]), i == 0, i == FFB - 1)
                mm.then_inc(g_used, 1)

            def d_step(c, ahead):
                for a in range(KB):
                    for i in range(FFB):
                        if a + 1 < KB:
                            ff_up(c, a + 1, i)
                        ff_down(c, a, i)
                    if ahead and a == 3:
                        ln_mean_pe(pe, c + 1 + 2 * CH)
                if ahead:
                    ln_var_pe(pe, c + 1 + 2 * CH)
                    for i in range(FFB):
                        ff_up(c + 1, 0, i)

            pe.wait_ge(o_ev, 8 * CH)
            ln_mean_pe(pe, 2 * CH)
            ln_var_pe(pe, 2 * CH)
            wait_units(pe, U_END)
            for i in range(FFB):
                ff_up(0, 0, i)
            chunks(pe, 0, CH - 1, lambda c: d_step(c, True))
            d_step(CH - 1, False)


FF_BANK = [0, 1, 2, 3, 4, 5, 0, 1]
PT_BANK = [2, 3]


def kernel(**inputs):
    import numpy as np
    import concourse.bacc as bacc
    from concourse.bass_utils import run_bass_kernel_spmd

    a = {k: np.asarray(v) for k, v in inputs.items()}

    def cols(v):
        return v.reshape(-1, P).T

    arrays = {
        "x_t": a["x"].reshape(TOKENS, D).T,
        "w_proj": a["L0_tok_W_proj"],
        "w_ff": a["L0_tok_W_ff"],
        "w_gen": a["L0_tok_W_wgen"],
        "w_qkv_t": a["L0_attn_w_qkv"].T,
        "w_o_t": a["L0_attn_w_o"].T,
        "up": a["L0_ffn_up"],
        "down": a["L0_ffn_down"],
        "vecs": np.concatenate([cols(a["L0_tok_b_proj"]), cols(a["L0_tok_ln_g"]), cols(a["L0_tok_ln_b"]),
                                cols(a["L0_tok_b_ff"]), cols(a["L0_attn_b_o"]), cols(a["L0_attn_b_qkv"])], axis=1),
        "b_gen": a["L0_tok_b_wgen"],
        "perm": cols(a["L0_ffn_perm"]),
    }
    nc = bacc.Bacc("TRN2", target_bir_lowering=False, num_devices=1)
    given, args = {}, []
    for name, v in arrays.items():
        v = np.ascontiguousarray(v)
        given[name] = v
        args.append(nc.dram_tensor(name, v.shape, mybir.dt.from_np(v.dtype), kind="ExternalInput").ap())
    for c in range(CH):
        args.append(nc.dram_tensor(f"out_{c}", (D, N), mybir.dt.float32, kind="ExternalOutput").ap())
    audio_tower(nc, *args)
    r = run_bass_kernel_spmd(nc, [given], core_ids=[0])
    got = np.stack([r.results[0][f"out_{c}"].T for c in range(CH)])
    return np.ascontiguousarray(got).reshape(BATCH, SEQ, D)
```

```python
import concourse.bass as bass
from concourse import mybir
from contextlib import ExitStack

BATCH, FRAMES, CHANNELS, STRIDE = 32, 256, 256, 4
SEQ = FRAMES // STRIDE
D = CHANNELS * STRIDE
TOKENS = BATCH * SEQ
P = 128
KB = D // P
N = 512
CH = TOKENS // N
TILES = N // P
TAPS, CONV_HEADS = 5, 8
LOGITS = TAPS * CONV_HEADS
PART = 512
HEAD = 64
PAIRS = PART // P
FF_HEADS, FF_IN, FF_MID = 16, 64, 256
FFB = 2 * FF_MID // P
EPS = 1e-5
MASKED = -10000.0
OTHER = -3.0e38
B_PROJ, LN_G, LN_B, B_FF, B_O, B_Q, B_K, B_V = 0, 8, 16, 24, 32, 40, 44, 48
VECS = 52
BAND = P * (P + 1)
UNITS = TILES * CONV_HEADS


def audio_tower(nc, x_t, w_proj, w_ff, w_gen, w_qkv_t, w_o_t, up, down, vecs, b_gen, perm, *outs):
    F32, F32R, I32, U8 = mybir.dt.float32, mybir.dt.float32r, mybir.dt.int32, mybir.dt.uint8
    ALU, ACT, AX = mybir.AluOpType, mybir.ActivationFunctionType, mybir.AxisListType

    h0_s = nc.dram_tensor("h0_s", [CH, P, KB * N], F32, kind="Internal").ap()
    h1_s = nc.dram_tensor("h1_s", [CH, P, KB * N], F32, kind="Internal").ap()
    vals_s = nc.dram_tensor("vals_s", [CH, P, PAIRS * N], F32, kind="Internal").ap()
    h2_s = [nc.dram_tensor(f"h2_s{c}", [D, N], F32, kind="Internal").ap() for c in range(CH)]
    stat_s = nc.dram_tensor("stat_s", [2 * CH, 2, N], F32, kind="Internal").ap()
    band_s = nc.dram_tensor("band_s", [UNITS * BAND], F32, kind="Internal").ap()

    ctx = ExitStack()
    with ctx:
        base = (nc.sbuf_base + 63) // 64 * 64
        def place(name, shape, dt, at):
            return nc.alloc_sbuf_tensor_at(name, shape, dt, offset=base + at)

        def sem(name):
            return ctx.enter_context(nc.semaphore(name))

        KIB = 1024
        R1, R2, CONST = 0, 64 * KIB, 128 * KIB
        STAGE = CONST + 7 * KIB
        LNT = STAGE + 8 * KIB
        E = LNT + 10 * KIB
        ident = place("ident", [P, P], F32, CONST)
        mean_w = place("mean_w", [P, P], F32, CONST + 512)
        negs = place("negs", [P, P], F32, CONST + 1024)
        vec = place("vec", [P, VECS], F32, CONST + 1536)
        bgen = place("bgen", [P, LOGITS], F32, CONST + 1792)
        valid = place("valid", [P, TAPS], F32, CONST + 1984)
        eps = place("eps", [P, 1], F32, CONST + 2016)
        rows = place("rows", [P, KB], I32, CONST + 2048)
        masked = place("masked", [P, P], U8, CONST + 2176)
        maskf = place("maskf", [P, P], F32, LNT)
        wg_h = place("wg_h", [P, KB, LOGITS], F32R, CONST + 2304)
        wg_l = place("wg_l", [P, KB, LOGITS], F32R, CONST + 2304 + 1280)
        smax = place("smax", [P, 2, TILES], F32, CONST + 4992)
        ssum = place("ssum", [P, 2, TILES], F32, CONST + 5056)
        mx5 = place("mx5", [P, UNITS], F32, CONST + 5120)
        su5 = place("su5", [P, UNITS], F32, CONST + 5248)
        lg5 = place("lg5", [P, UNITS, TAPS], F32, CONST + 5376)
        wk5 = place("wk5", [P, UNITS, TAPS], F32, CONST + 6016)
        stage = place("stage", [P, 4, N], F32, STAGE)
        wg_raw = place("wg_raw", [P, KB, LOGITS], F32, LNT + 6 * KIB)
        acc = place("acc", [P, N], F32, LNT)
        sq = place("sq", [P, 2, N], F32, LNT + 2 * KIB)
        vacc = place("vacc", [P, N], F32, LNT + 6 * KIB)
        rstd = place("rstd", [P, N], F32, LNT + 8 * KIB)
        wp_h = place("wp_h", [P, KB, D], F32R, R1)
        wp_l = place("wp_l", [P, KB, D], F32R, R1 + 32 * KIB)
        xa_h = place("xa_h", [P, KB, N], F32R, E)
        xa_l = place("xa_l", [P, KB, N], F32R, E + 16 * KIB)
        xs = place("xs", [P, KB, N], F32, R2)
        ho = place("ho", [P, KB, N], F32, R2 + 16 * KIB)
        zero = place("zero", [P, UNITS * BAND // P], F32, E + 32 * KIB)
        mean_t = place("mean_t", [P, N], F32, E + 52 * KIB)
        db0 = place("db0", [P, KB, N], F32, R2 + 32 * KIB)
        band0 = place("band0", [P, UNITS, P], F32, R2 + 32 * KIB)
        yb0 = place("yb0", [P, KB, N], F32, R2 + 48 * KIB)
        wf_h = place("wf_h", [P, KB, D], F32R, R2)
        wf_l = place("wf_l", [P, KB, D], F32R, R2 + 32 * KIB)
        db = place("db", [P, KB, N], F32, R1)
        yb = place("yb", [P, KB, N], F32, R1 + 16 * KIB)
        cv_h = place("cv_h", [P, KB, N], F32R, R1 + 32 * KIB)
        cv_l = place("cv_l", [P, KB, N], F32R, R1 + 48 * KIB)
        yt_h = place("yt_h", [P, 2, N], F32R, E)
        yt_l = place("yt_l", [P, 2, N], F32R, E + 4 * KIB)
        ar_h = place("ar_h", [P, 2, N], F32R, E + 8 * KIB)
        ar_l = place("ar_l", [P, 2, N], F32R, E + 12 * KIB)
        band = place("band", [P, UNITS, P], F32, E + 16 * KIB)
        yr_h = place("yr_h", [P, 2, N], F32R, E + 32 * KIB)
        yr_l = place("yr_l", [P, 2, N], F32R, E + 36 * KIB)
        lg = place("lg", [LOGITS, N], F32, E + 40 * KIB)
        mt = place("mt", [P, N], F32, E + 42 * KIB)
        rt = place("rt", [P, N], F32, E + 44 * KIB)
        res = place("res", [P, 2, N], F32, E + 46 * KIB)
        fo = place("fo", [P, 2, N], F32, E + 50 * KIB)
        dc = place("dc", [P, KB, N], F32, R1)
        v_h = place("v_h", [P, TILES, PART], F32R, R1 + 16 * KIB)
        v_l = place("v_l", [P, TILES, PART], F32R, R1 + 24 * KIB)
        wk_h = place("wk_h", [P, KB, PART], F32R, R1 + 32 * KIB)
        wk_l = place("wk_l", [P, KB, PART], F32R, R1 + 48 * KIB)
        wv_h = place("wv_h", [P, KB, PART], F32R, R2)
        wv_l = place("wv_l", [P, KB, PART], F32R, R2 + 16 * KIB)
        wq_h = place("wq_h", [P, KB, PART], F32R, R2 + 32 * KIB)
        wq_l = place("wq_l", [P, KB, PART], F32R, R2 + 48 * KIB)
        xc_h = place("xc_h", [P, KB, N], F32R, E)
        xc_l = place("xc_l", [P, KB, N], F32R, E + 16 * KIB)
        qk_h = place("qk_h", [P, 2, N], F32R, E + 32 * KIB)
        qk_l = place("qk_l", [P, 2, N], F32R, E + 36 * KIB)
        pr = place("pr", [P, 2, N], F32, E + 40 * KIB)
        pt_h = place("pt_h", [P, 2, N], F32R, E + 44 * KIB)
        pt_l = place("pt_l", [P, 2, N], F32R, E + 48 * KIB)
        vo = place("vo", [P, N], F32, E + 52 * KIB)
        wo_h = place("wo_h", [P, PAIRS, D], F32R, R2)
        wo_l = place("wo_l", [P, PAIRS, D], F32R, R2 + 16 * KIB)
        vs_h = place("vs_h", [P, PAIRS, N], F32R, R1)
        vs_l = place("vs_l", [P, PAIRS, N], F32R, R1 + 8 * KIB)
        vs = place("vs", [P, PAIRS, N], F32, E + 16 * KIB)
        h2 = [place(f"h2_{i}", [P, KB, N], F32, E + 32 * i * KIB) for i in range(2)]
        up_h = place("up_h", [P, KB, FF_MID], F32R, R1 + 16 * KIB)
        up_l = place("up_l", [P, KB, FF_MID], F32R, R1 + 24 * KIB)
        dn_h = place("dn_h", [P, KB * FFB, P], F32R, R1 + 32 * KIB)
        dn_l = place("dn_l", [P, KB * FFB, P], F32R, R1 + 48 * KIB)
        gt = place("gt", [P, FFB, N], F32, R2)
        g_h = place("g_h", [P, FFB, N], F32R, R2 + 8 * KIB)
        g_l = place("g_l", [P, FFB, N], F32R, R1)
        hg = place("hg", [P, 2 * KB, N], F32, R2 + 16 * KIB)
        dd = place("dd", [P, KB, N], F32, R2 + 48 * KIB)
        xd_h = place("xd_h", [P, KB, N], F32R, E)
        xd_l = place("xd_l", [P, KB, N], F32R, E + 16 * KIB)
        mtd = place("mtd", [P, N], F32, E + 48 * KIB)
        rtd = place("rtd", [P, N], F32, E + 50 * KIB)

        bank = [ctx.enter_context(nc.psum_tensor(f"bank{i}", [P, N], F32)) for i in range(8)]
        LN_BANK = 6

        const_ld = sem("const_ld")
        masks_ok = sem("masks_ok")
        stage_ld = [sem(f"stage_ld{i}") for i in range(4)]
        w_hi = sem("w_hi")
        w_lo_v = sem("w_lo_v")
        w_lo_g = sem("w_lo_g")
        wg_ok = sem("wg_ok")
        zero_ok, band_zeroed = sem("zero_ok"), sem("band_zeroed")
        a_ld = [sem(f"a_ld{k}") for k in range(KB)]
        a_hi, a_lo, a_used, a_mm, a_ev = (sem(s) for s in ("a_hi", "a_lo", "a_used", "a_mm", "a_ev"))
        a_st = [sem(f"a_st{g}") for g in range(2)]
        ln_pool, ln_mean, ln_d, ln_sq, ln_var, ln_std, ln_rstd = (
            sem(s) for s in ("ln_pool", "ln_mean", "ln_d", "ln_sq", "ln_var", "ln_std", "ln_rstd"))
        st_copied, st_st = sem("st_copied"), sem("st_st")
        b_ld, y_cent = sem("b_ld"), sem("y_cent")
        y_scaled, y_b, yr_hi, yr_lo, yr_used, lg_ev, lgt_mm = (
            sem(s) for s in ("y_scaled", "y_b", "yr_hi", "yr_lo", "yr_used", "lg_ev", "lgt_mm"))
        sm5, exp5, skewed, band_ld = (sem(s) for s in ("sm5", "exp5", "skewed", "band_ld"))
        yt_mm, at_mm, yt_hi, ar_hi, yt_lo, ar_lo = (
            sem(s) for s in ("yt_mm", "at_mm", "yt_hi", "ar_hi", "yt_lo", "ar_lo"))
        cv_mm, cv_hi, cv_lo, ff_mm, ff_ev, ff_add = (
            sem(s) for s in ("cv_mm", "cv_hi", "cv_lo", "ff_mm", "ff_ev", "ff_add"))
        res_ld = [sem(f"res_ld{i}") for i in range(2)]
        fo_st = [sem(f"fo_st{i}") for i in range(2)]
        c_ld, xc_sc, xc_hi, xc_lo, xc_used = (sem(s) for s in ("c_ld", "xc_sc", "xc_hi", "xc_lo", "xc_used"))
        v_mm, v_hi, v_lo, qk_mm, qk_hi, qk_lo = (
            sem(s) for s in ("v_mm", "v_hi", "v_lo", "qk_mm", "qk_hi", "qk_lo"))
        s_mm, s_masked, s_max, s_sub, s_exp, s_sum, s_rec, s_norm = (
            sem(s) for s in ("s_mm", "s_masked", "s_max", "s_sub", "s_exp", "s_sum", "s_rec", "s_norm"))
        pt_mm, pt_hi, pt_lo, pv_mm, vo_ev, vo_st = (
            sem(s) for s in ("pt_mm", "pt_hi", "pt_lo", "pv_mm", "vo_ev", "vo_st"))
        vs_ld, vs_hi, vs_lo, vs_used, o_mm, o_ev = (
            sem(s) for s in ("vs_ld", "vs_hi", "vs_lo", "vs_used", "o_mm", "o_ev"))
        o_ld = [[sem(f"o_ld{i}{g}") for g in range(2)] for i in range(2)]
        o_st = [[sem(f"o_st{i}{g}") for g in range(2)] for i in range(2)]
        d_ld, d_cent = sem("d_ld"), sem("d_cent")
        g_ld, xd_sc, xd_hi, xd_lo = (sem(s) for s in ("g_ld", "xd_sc", "xd_hi", "xd_lo"))
        up_mm, gelu_ok, g_hi, g_lo, g_used, d_ev, d_st, dn_zero = (
            sem(s) for s in ("up_mm", "gelu_ok", "g_hi", "g_lo", "g_used", "d_ev", "d_st", "dn_zero"))

        def since(e, s, c, per, k):
            if isinstance(c, int):
                if c * per + k > 0:
                    e.wait_ge(s, c * per + k)
            else:
                e.wait_ge(s, c * per + k)

        def chunks(e, first, last, body):
            body(first)
            if last - first > 1:
                with e.Fori(first + 1, last) as c:
                    body(c)

        def released(e, c, k, blocks, used, done):
            if k < blocks - 1:
                since(e, used, c, blocks - 1, k + 1)
            else:
                since(e, done, c, 8, 8)

        def weight_units():
            units = []
            for half in range(2):
                for k in range(KB):
                    cols = slice(half * N, half * N + N)
                    units.append((w_proj[k * P:(k + 1) * P, cols], wp_h[:, k, cols], wp_l[:, k, cols], "v"))
            for half in range(2):
                for k in range(KB):
                    cols = slice(half * N, half * N + N)
                    units.append((w_ff[k * P:(k + 1) * P, cols], wf_h[:, k, cols], wf_l[:, k, cols], "g"))
            for k in range(KB):
                units.append((w_qkv_t[k * P:(k + 1) * P, 2 * PART:3 * PART], wv_h[:, k, :], wv_l[:, k, :], "v"))
            for k in range(KB):
                for col, h, l, who in ((0, wq_h, wq_l, "g"), (1, wk_h, wk_l, "v")):
                    units.append((w_qkv_t[k * P:(k + 1) * P, col * PART:(col + 1) * PART],
                                  h[:, k, :], l[:, k, :], who))
            for half in range(2):
                for k in range(PAIRS):
                    cols = slice(half * N, half * N + N)
                    units.append((w_o_t[k * P:(k + 1) * P, cols], wo_h[:, k, cols], wo_l[:, k, cols], "g"))
            for k in range(0, KB, 2):
                src = up[2 * k:2 * k + 4].rearrange("(a s) d m -> (s d) a m", s=2)
                units.append((src, up_h[:, k:k + 2, :], up_l[:, k:k + 2, :], "g"))
            for head in range(0, FF_HEADS, 4):
                src = down[head:head + 4].rearrange("h (b p) d -> p h b d", p=P)
                sl = slice(2 * head, 2 * head + 8)
                units.append((src, dn_h[:, sl, :], dn_l[:, sl, :], "g"))
            return units

        units = weight_units()
        U_PROJ, U_FF, U_V, U_QK, U_O, U_UP, U_DN, U_END = 0, 16, 32, 40, 56, 64, 68, 72
        lo_before = [[sum(1 for u in units[:n] if u[3] == who) for n in range(len(units) + 1)] for who in "vg"]

        def wait_units(e, upto):
            if lo_before[0][upto]:
                e.wait_ge(w_lo_v, lo_before[0][upto])
            if lo_before[1][upto]:
                e.wait_ge(w_lo_g, lo_before[1][upto])

        def unit_load(e, u):
            if u >= 4:
                who = 0 if units[u - 4][3] == "v" else 1
                e.wait_ge((w_lo_v, w_lo_g)[who], lo_before[who][u - 3])
            src = units[u][0]
            if u >= U_DN:
                for i in range(4):
                    e.dma_start(stage[:, u % 4, i * P:(i + 1) * P].rearrange("p (b d) -> p b d", b=2),
                                src[:, i]).then_inc(stage_ld[u % 4], 16)
            else:
                dst = stage[:, u % 4, :]
                if u >= U_UP:
                    for i in range(2):
                        for s in range(2):
                            e.dma_start(stage[64 * s:64 * s + 64, u % 4, i * FF_MID:(i + 1) * FF_MID],
                                        up[4 * (u - U_UP) + 2 * i + s]).then_inc(stage_ld[u % 4], 16)
                else:
                    e.dma_start(dst, src).then_inc(stage_ld[u % 4], 16)

        def slot_count(u):
            return sum(16 * (4 if v >= U_UP else 1) for v in range(u % 4, u + 1, 4))

        def unit_views(u):
            st = stage[:, u % 4, :]
            if u < U_UP:
                return [(st, units[u][1], units[u][2])]
            if u < U_DN:
                return [(st.rearrange("p (a m) -> p a m", a=2), units[u][1], units[u][2])]
            v4 = st.rearrange("p (a s b d) -> p a s b d", a=2, s=2, b=2)
            out_views = []
            for s in range(2):
                h, l = (t.rearrange("p (a s b) (c d) -> p a s b c d", a=2, s=2, c=2)[:, :, s, :, s, :]
                        for t in (units[u][1], units[u][2]))
                out_views.append((v4[:, :, s], h, l))
            return out_views

        def unit_hi(act, u):
            act.wait_ge(stage_ld[u % 4], slot_count(u))
            for i, (st, h, _) in enumerate(unit_views(u)):
                ins = act.activation(h, st, ACT.Copy)
            ins.then_inc(w_hi, 1)

        def unit_lo(e, u):
            e.wait_ge(w_hi, u + 1)
            e.wait_ge(stage_ld[u % 4], slot_count(u))
            s = w_lo_v if units[u][3] == "v" else w_lo_g
            for i, (st, h, l) in enumerate(unit_views(u)):
                ins = e.tensor_tensor(l, st, h.bitcast(F32), ALU.subtract)
            ins.then_inc(s, 1)

        def split3(pe, o, w_hl, x_hl, start, stop):
            (wh, wl), (xh, xl) = w_hl, x_hl
            pe.matmul(o, wh, xh, start=start, stop=False)
            pe.matmul(o, wh, xl, start=False, stop=False)
            return pe.matmul(o, wl, xh, start=False, stop=stop)

        def ln_sum_pool(g, L, blk):
            g.tensor_tensor(acc[:, :], blk(0), blk(1), ALU.add).then_inc(ln_pool, 1)
            for k in range(2, KB):
                since(g, ln_pool, L, 14, k - 1)
                g.tensor_tensor(acc[:, :], acc[:, :], blk(k), ALU.add).then_inc(ln_pool, 1)

        def ln_mean_pe(pe, L):
            since(pe, ln_pool, L, 14, 7)
            since(pe, ln_std, L - 1, 1, 1)
            pe.matmul(bank[LN_BANK][:, :], mean_w[:, :], acc[:, :], start=True, stop=True).then_inc(ln_mean, 1)

        def ln_center_dve(v, L, k, src, dst):
            if k == 0:
                since(v, ln_mean, L, 1, 1)
            v.tensor_tensor(dst, src, bank[LN_BANK][:, :], ALU.subtract).then_inc(ln_d, 1)

        def ln_square_act(act, L, k, d):
            since(act, ln_d, L, 8, k + 1)
            if k >= 2:
                since(act, ln_pool, L, 14, 7 + max(1, k - 2))
            act.activation(sq[:, k % 2, :], d, ACT.Square).then_inc(ln_sq, 1)

        def ln_var_pool(g, L):
            for k in range(1, KB):
                since(g, ln_sq, L, 8, k + 1)
                if k == 1:
                    g.tensor_tensor(vacc[:, :], sq[:, 0, :], sq[:, 1, :], ALU.add).then_inc(ln_pool, 1)
                else:
                    since(g, ln_pool, L, 14, 7 + k - 1)
                    g.tensor_tensor(vacc[:, :], vacc[:, :], sq[:, k % 2, :], ALU.add).then_inc(ln_pool, 1)

        def ln_var_pe(pe, L):
            since(pe, ln_pool, L, 14, 14)
            since(pe, ln_d, L, 8, 8)
            pe.matmul(bank[LN_BANK][:, :], mean_w[:, :], vacc[:, :], start=True, stop=True).then_inc(ln_var, 1)

        def ln_std_act(act, L, last_scale):
            since(act, ln_var, L, 1, 1)
            last_scale(act)
            act.activation(rstd[:, :], bank[LN_BANK][:, :], ACT.Sqrt, bias=eps[:, 0:1]).then_inc(ln_std, 1)

        def ln_rstd_dve(v, L):
            since(v, ln_std, L, 1, 1)
            v.reciprocal(rstd[:, :], rstd[:, :]).then_inc(ln_rstd, 1)
            since(v, ln_rstd, L, 1, 1)

        def stat_sum_pool(g, L, k, blk):
            if k > 1:
                since(g, ln_pool, L, 14, k - 1)
            g.tensor_tensor(acc[:, :], blk(0) if k == 1 else acc[:, :], blk(k), ALU.add).then_inc(ln_pool, 1)

        def stat_copy_act(act, L, S):
            since(act, st_st, S - 1, 32, 32)
            since(act, ln_d, L - 1, 8, 8)
            since(act, ln_mean, L, 1, 1)
            act.activation(mean_t[:, :], bank[LN_BANK][:, :], ACT.Copy).then_inc(st_copied, 1)

        def stat_center_dve(v, L, S, k, src):
            if k == 0:
                since(v, st_copied, S, 1, 1)
            if k >= 2:
                since(v, ln_pool, L, 14, 7 + max(1, k - 2))
            v.tensor_tensor(sq[:, k % 2, :], src, mean_t[:, :], ALU.subtract).then_inc(ln_d, 1)

        def stat_square_act(act, L, k):
            since(act, ln_d, L, 8, k + 1)
            act.activation(sq[:, k % 2, :], sq[:, k % 2, :], ACT.Square).then_inc(ln_sq, 1)

        def stat_mean_pe(pe, L):
            since(pe, ln_pool, L, 14, 7)
            pe.matmul(bank[LN_BANK][:, :], mean_w[:, :], acc[:, :], start=True, stop=True).then_inc(ln_mean, 1)

        def stat_var_pe(pe, L, S, b=LN_BANK):
            since(pe, ln_pool, L, 14, 14)
            since(pe, st_copied, S, 1, 1)
            pe.matmul(bank[b][:, :], mean_w[:, :], vacc[:, :], start=True, stop=True).then_inc(ln_var, 1)

        def stat_std_act(act, L, b=LN_BANK):
            since(act, ln_var, L, 1, 1)
            act.activation(rstd[:, :], bank[b][:, :], ACT.Sqrt, bias=eps[:, 0:1]).then_inc(ln_std, 1)

        def stat_recip_dve(v, L):
            since(v, ln_std, L, 1, 1)
            v.reciprocal(rstd[:, :], rstd[:, :]).then_inc(ln_rstd, 1)

        block = ctx.enter_context(nc.Block())

        @block.sync
        def _(sp):
            for k in range(KB):
                unit_load(sp, U_PROJ + k)
                sp.dma_start(xs[:, k, :], x_t[k * P:(k + 1) * P, 0:N]).then_inc(a_ld[k], 16)
                if k == 3:
                    sp.dma_start(vec[:, :], vecs).then_inc(const_ld, 16)
                    sp.dma_start(bgen[:, :], b_gen.partition_broadcast(P)).then_inc(const_ld, 16)
                    sp.dma_start(rows[:, :], perm).then_inc(const_ld, 16)
            for k in range(KB):
                unit_load(sp, U_PROJ + KB + k)
            sp.wait_ge(zero_ok, 1)
            sp.dma_start(band_s.rearrange("(p n) -> p n", p=P), zero[:, :]).then_inc(band_zeroed, 16)

            for u in range(U_FF, U_FF + 4):
                unit_load(sp, u)

            def a_load(c):
                for k in range(KB):
                    sp.wait_ge(a_lo, (c - 1) * KB + k + 1)
                    sp.dma_start(xs[:, k, :], x_t[k * P:(k + 1) * P, c * N:(c + 1) * N]).then_inc(a_ld[k], 16)

            def stat_store(S, i):
                if i == 0:
                    sp.wait_ge(st_copied, S + 1)
                    sp.dma_start(stat_s[S, 0:1, :], mean_t[0:1, :]).then_inc(st_st, 16)
                else:
                    sp.wait_ge(ln_rstd, S + 1 if S < CH else S + CH + 1)
                    sp.dma_start(stat_s[S, 1:2, :], rstd[0:1, :]).then_inc(st_st, 16)

            def a_store(c, g):
                sp.wait_ge(a_ev, c * KB + 4 * g + 4)
                sp.dma_start(h0_s[c, :, g * 4 * N:(g + 1) * 4 * N],
                             ho[:, 4 * g:4 * g + 4, :]).then_inc(a_st[g], 16)

            def b_load(n):
                if n == 0:
                    sp.wait_ge(band_zeroed, 16)
                elif n == 1:
                    sp.wait_ge(a_mm, CH * KB)
                if n > 0:
                    sp.wait_ge(yr_hi, n * KB)
                for g in range(2):
                    sp.wait_ge(a_st[g], 16 * (n + 1))
                sp.wait_ge(st_st, 32 * (n + 1))
                dst = db0 if n == 0 else db
                sp.dma_start(dst[:, :, :], h0_s[n]).then_inc(b_ld, 16)
                sp.dma_start(mt[:, :], stat_s[n, 0].partition_broadcast(P)).then_inc(b_ld, 16)
                sp.dma_start(rt[:, :], stat_s[n, 1].partition_broadcast(P)).then_inc(b_ld, 16)

            def band_skew(n):
                sp.wait_ge(sm5, n * 7 + 7)
                sp.wait_ge(band_zeroed, 16)
                if n > 0:
                    sp.wait_ge(band_ld, 16 * n)
                dst = band_s.rearrange("(u n) -> u n", u=UNITS)[:, 0:P * (P + 1)]
                dst = dst.rearrange("u (t n) -> t u n", t=P)[:, :, 0:TAPS]
                sp.dma_start(dst, wk5[:, :, :]).then_inc(skewed, 16)

            def band_load(n):
                sp.wait_ge(skewed, 16 * (n + 1))
                if n > 0:
                    sp.wait_ge(at_mm, n * KB)
                else:
                    sp.wait_ge(yr_hi, KB)
                src = band_s.rearrange("(u n) -> u n", u=UNITS)[:, TAPS - 1:TAPS - 1 + P * P]
                dst = band0 if n == 0 else band
                sp.dma_start(dst[:, :, :], src.rearrange("u (t n) -> t u n", t=P)).then_inc(band_ld, 16)

            for c in range(CH):
                if c + 1 < CH:
                    a_load(c + 1)
                if c > 0:
                    stat_store(c - 1, 0)
                    stat_store(c - 1, 1)
                if c == CH - 2:
                    b_load(0)
                a_store(c, 0)
                if c == CH - 1:
                    band_skew(0)
                    band_load(0)
                a_store(c, 1)
            b_load(1)
            stat_store(CH - 1, 0)
            for u in range(U_FF + 4, U_V):
                unit_load(sp, u)
            stat_store(CH - 1, 1)

            def res_load(c, m):
                if 8 * c + m >= 2:
                    sp.wait_ge(ff_add, 8 * c + m - 1)
                sp.dma_start(res[:, m % 2, :], h0_s[c, :, m * N:(m + 1) * N]).then_inc(res_ld[m % 2], 16)

            def ff_store(c, m):
                sp.wait_ge(ff_add, 8 * c + m + 1)
                sp.dma_start(h1_s[c, :, m * N:(m + 1) * N], fo[:, m % 2, :]).then_inc(fo_st[m % 2], 16)

            def c_load(n):
                if n == 0:
                    sp.wait_ge(yr_hi, KB * CH)
                else:
                    sp.wait_ge(xc_lo, n * KB)
                for i in range(2):
                    sp.wait_ge(fo_st[i], 16 * 4 * (n + 1))
                sp.dma_start(dc[:, :, :], h1_s[n]).then_inc(c_ld, 16)

            for c in range(CH):
                res_load(c, 0)
                res_load(c, 1)
                if c + 2 < CH:
                    b_load(c + 2)
                if c == CH - 1:
                    for u in range(U_V, U_V + 4):
                        unit_load(sp, u)
                for m in range(KB):
                    if m == 2 and c + 1 < CH:
                        band_skew(c + 1)
                        band_load(c + 1)
                    ff_store(c, m)
                    if m == 5 and c == CH - 2:
                        sp.wait_ge(band_ld, 16 * CH)
                        c_load(0)
                    if m + 2 < KB:
                        res_load(c, m + 2)
            for u in range(U_V + 4, U_O):
                unit_load(sp, u)

            def vs_load(c):
                if c == 0:
                    sp.wait_ge(qk_mm, 8 * CH)
                else:
                    sp.wait_ge(vs_lo, 4 * c)
                sp.wait_ge(vo_st, 16 * 4 * (c + 1))
                sp.dma_start(vs[:, :, :], vals_s[c]).then_inc(vs_ld, 16)

            def h2_load(c):
                if c == 0:
                    sp.wait_ge(qk_mm, 8 * CH)
                elif c == 1:
                    sp.wait_ge(pv_mm, 8 * CH)
                else:
                    sp.wait_ge(ln_d, 8 * (2 * CH + c - 1))
                for g in range(2):
                    if c >= 2:
                        sp.wait_ge(o_st[c % 2][g], 16 * (c // 2))
                    sp.dma_start(h2[c % 2][:, 4 * g:4 * g + 4, :], h1_s[c, :, g * 4 * N:(g + 1) * 4 * N])\
                      .then_inc(o_ld[c % 2][g], 16)

            def vo_store(c, m):
                sp.wait_ge(vo_ev, 8 * c + 2 * m + 2)
                sp.dma_start(vals_s[c, :, m * N:(m + 1) * N], vo[:, :]).then_inc(vo_st, 16)

            c_load(1)
            for c in range(CH):
                if c + 1 == CH:
                    for u in range(U_O, U_O + 4):
                        unit_load(sp, u)
                for m in range(PAIRS):
                    if m == PAIRS - 1 and c + 2 < CH:
                        c_load(c + 2)
                    vo_store(c, m)
                    if c + 1 == CH:
                        unit_load(sp, U_O + 4 + m)
                        if m == 1:
                            vs_load(0)
                            h2_load(0)
            for u in range(U_UP, U_END):
                unit_load(sp, u)
            h2_load(1)

            def d_stat_load(n):
                sp.wait_ge(st_st, 32 * (CH + n + 1))
                if n > 0:
                    sp.wait_ge(xd_sc, 8 * n)
                sp.dma_start(mtd[:, :], stat_s[CH + n, 0].partition_broadcast(P)).then_inc(d_ld, 16)
                sp.dma_start(rtd[:, :], stat_s[CH + n, 1].partition_broadcast(P)).then_inc(d_ld, 16)

            for c in range(CH):
                if c + 1 < CH:
                    vs_load(c + 1)
                if c > 0:
                    stat_store(CH + c - 1, 0)
                for g in range(2):
                    sp.wait_ge(o_ev, 8 * c + 4 * g + 4)
                    sp.dma_start(h2_s[c][g * 4 * P:(g + 1) * 4 * P, :].rearrange("(k p) n -> p k n", p=P),
                                 h2[c % 2][:, 4 * g:4 * g + 4, :]).then_inc(o_st[c % 2][g], 16)
                if c > 0 and c + 1 < CH:
                    h2_load(c + 1)
                if c > 0:
                    stat_store(CH + c - 1, 1)
                if c == 1:
                    d_stat_load(0)
            d_stat_load(1)
            stat_store(2 * CH - 1, 0)
            stat_store(2 * CH - 1, 1)
            for n in range(2, CH):
                d_stat_load(n)
            sp.wait_ge(d_st, 16 * KB * CH)

        @block.gpsimd
        def _(g):
            for t, value in ((ident, 0.0), (mean_w, 1.0 / D), (eps, EPS), (valid, 1.0), (maskf, 1.0), (negs, OTHER)):
                g.memset(t[:, :], value).then_inc(masks_ok, 1)
            g.wait_ge(masks_ok, 6)
            g.affine_select(out=ident[:, :], in_=ident[:, :], compare_op=ALU.not_equal, fill=1.0, base=0,
                            pattern=[[-1, P]], channel_multiplier=1).then_inc(masks_ok, 1)
            for s in range(P // SEQ):
                part = slice(s * SEQ, (s + 1) * SEQ)
                g.wait_ge(masks_ok, 7 + 3 * s)
                g.affine_select(out=valid[part, :], in_=valid[part, :], compare_op=ALU.is_ge, fill=0.0,
                                base=1 - TAPS, pattern=[[1, TAPS]], channel_multiplier=1).then_inc(masks_ok, 1)
                g.wait_ge(masks_ok, 8 + 3 * s)
                g.affine_select(out=maskf[part, part], in_=maskf[part, part], compare_op=ALU.is_gt, fill=0.0,
                                base=0, pattern=[[1, SEQ]], channel_multiplier=-1).then_inc(masks_ok, 1)
                g.wait_ge(masks_ok, 9 + 3 * s)
                g.memset(negs[part, part], MASKED).then_inc(masks_ok, 1)
            g.wait_ge(masks_ok, 13)
            g.tensor_copy(masked[:, :], maskf[:, :]).then_inc(masks_ok, 1)
            g.memset(zero[:, :], 0.0).then_inc(zero_ok, 1)

            def a_sum(c, ks):
                for k in ks:
                    since(g, a_ev, c, 8, k + 1)
                    stat_sum_pool(g, c, k, lambda i: ho[:, i, :])

            g.wait_ge(masks_ok, 14)
            a_sum(0, range(1, KB))
            with g.Fori(0, CH - 2) as c:
                ln_var_pool(g, c)
                a_sum(c + 1, range(1, KB))
            ln_var_pool(g, CH - 2)
            a_sum(CH - 1, range(1, KB))
            ln_var_pool(g, CH - 1)
            g.wait_ge(at_mm, 8)
            for u in range(U_FF, U_V):
                unit_lo(g, u)

            def b_add(c, m):
                since(g, ff_ev, c, 8, m + 1)
                since(g, res_ld[m % 2], c, 64, 16 * (m // 2 + 1))
                g.tensor_tensor(fo[:, m % 2, :], fo[:, m % 2, :], res[:, m % 2, :], ALU.add).then_inc(ff_add, 1)

            def c_sum(n):
                since(g, c_ld, n, 16, 16)
                ln_sum_pool(g, n + CH, lambda k: dc[:, k, :])

            with g.Fori(0, CH - 2) as c:
                for m in range(KB):
                    b_add(c, m)
            for m in range(6):
                b_add(CH - 2, m)
            c_sum(0)
            for m in range(6, KB):
                b_add(CH - 2, m)
            ln_var_pool(g, CH)
            for m in range(KB):
                b_add(CH - 1, m)

            for u in range(U_V, U_O):
                if units[u][3] == "g":
                    unit_lo(g, u)
            with g.Fori(1, CH) as n:
                c_sum(n)
                ln_var_pool(g, n + CH)
                since(g, ln_rstd, n + CH, 1, 1)
                for k in range(KB):
                    g.tensor_tensor(dc[:, k, :], dc[:, k, :], rstd[:, :], ALU.mult).then_inc(xc_sc, 1)
            g.wait_ge(v_mm, 4 * CH)
            for u in range(U_O, U_UP):
                unit_lo(g, u)
            g.wait_ge(pv_mm, 8 * CH)
            g.memset(dn_h[:, :, :].bitcast(F32), 0.0).then_inc(dn_zero, 1)
            g.memset(dn_l[:, :, :].bitcast(F32), 0.0).then_inc(dn_zero, 1)
            g.wait_ge(dn_zero, 2)
            for u in range(U_UP, U_END):
                unit_lo(g, u)

            def o_sum(c):
                for k in range(1, KB):
                    g.wait_ge(o_ev, 8 * c + k + 1)
                    stat_sum_pool(g, 2 * CH + c, k, lambda i: h2[c % 2][:, i, :])

            def gather(n):
                for half in range(2):
                    g.wait_ge(o_st[n % 2][half], 16 * (n // 2 + 1))
                if n == 1:
                    g.wait_ge(o_mm, 8 * CH)
                if n >= 2:
                    g.wait_ge(d_st, 16 * KB * (n - 1))
                for k in range(KB):
                    g.indirect_dma_start(out=hg[:, hg_block(n) + k, :], out_offset=None, in_=h2_s[n],
                                         in_offset=bass.IndirectOffsetOnAxis(ap=rows[:, k:k + 1], axis=0))\
                     .then_inc(g_ld, 16)

            def scatter(c, k):
                g.wait_ge(d_ev, 8 * c + k + 1)
                g.indirect_dma_start(out=outs[c],
                                     out_offset=bass.IndirectOffsetOnAxis(ap=rows[:, k:k + 1], axis=0),
                                     in_=hg[:, hg_block(c) + k, :], in_offset=None).then_inc(d_st, 16)

            g.wait_ge(const_ld, 48)
            o_sum(0)
            for c in range(1, CH):
                ln_var_pool(g, 2 * CH + c - 1)
                if c == 1:
                    gather(0)
                o_sum(c)
            gather(1)
            ln_var_pool(g, 3 * CH - 1)
            for c in range(CH):
                if c > 0 and c + 1 < CH:
                    gather(c + 1)
                for k in range(KB):
                    scatter(c, k)
            g.wait_ge(d_st, 16 * KB * CH)

        @block.scalar
        def _(act):
            act.dma_start(wg_raw[:, :, :], w_gen.rearrange("(k p) n -> p k n", p=P)).then_inc(wg_ok, 16)

            def a_high(c, k):
                since(act, a_ld[k], c, 16, 16)
                released(act, c - 1, k, KB, a_used, a_mm)
                act.activation(xa_h[:, k, :], xs[:, k, :], ACT.Copy).then_inc(a_hi, 1)

            for k in range(KB):
                unit_hi(act, U_PROJ + k)
                a_high(0, k)
            for k in range(KB):
                unit_hi(act, U_PROJ + KB + k)
            act.wait_ge(wg_ok, 16)
            act.activation(wg_h[:, :, :], wg_raw[:, :, :], ACT.Copy).then_inc(wg_ok, 1)

            def a_evac(c, ms):
                for m in ms:
                    since(act, a_st[m // 4], c, 16, 0)
                    since(act, ln_d, c - 1, 8, m + 1)
                    since(act, a_mm, c, 8, m + 1)
                    act.activation(ho[:, m, :], bank[m][:, :], ACT.Identity,
                                   bias=vec[:, B_PROJ + m:B_PROJ + m + 1]).then_inc(a_ev, 1)

            def a_step(c):
                if not (isinstance(c, int) and c == 0):
                    stat_copy_act(act, c - 1, c - 1)
                    for k in range(KB):
                        stat_square_act(act, c - 1, k)
                a_evac(c, A_GROUPS[0])
                if not (isinstance(c, int) and c == 0):
                    stat_std_act(act, c - 1)
                a_evac(c, A_GROUPS[1])
                for k in range(KB - 1):
                    a_high(c + 1, k)
                a_evac(c, A_GROUPS[2])
                a_high(c + 1, KB - 1)

            act.wait_ge(const_ld, 48)
            a_step(0)
            a_step(1)
            with act.Fori(2, CH - 1) as c:
                a_step(c)

            def y_base(n, k):
                since(act, y_scaled, n, 8, k + 1)
                if k == 0:
                    since(act, yt_mm, n - 1, 8, 8)
                src, dst = (db0, yb0) if isinstance(n, int) and n == 0 else (db, yb)
                act.activation(dst[:, k, :], src[:, k, :], ACT.Identity,
                               bias=vec[:, LN_B + k:LN_B + k + 1]).then_inc(y_b, 1)

            def y_high(n, k):
                since(act, yr_used, n, 8, k - 1)
                src = db0 if isinstance(n, int) and n == 0 else db
                act.activation(yr_h[:, k % 2, :], src[:, k, :], ACT.Identity,
                               bias=vec[:, LN_B + k:LN_B + k + 1]).then_inc(yr_hi, 1)

            def gate_logits(n):
                since(act, yr_used, n, 8, 8)
                since(act, lgt_mm, n - 1, 1, 1)
                act.activation(lg[:, :], bank[7][0:LOGITS, :], ACT.Copy).then_inc(lg_ev, 1)

            def gate_exp(n):
                since(act, sm5, n, 7, 3)
                act.activation(lg5[:, :, :], lg5[:, :, :], ACT.Exp).then_inc(exp5, 1)

            def turn_evac(n, h):
                since(act, yt_mm, n, 8, h + 1)
                since(act, cv_mm, n, 8, h - 1)
                act.activation(yt_h[:, h % 2, :], bank[YT_BANK + h % 2][:, :], ACT.Copy).then_inc(yt_hi, 1)
                since(act, at_mm, n, 8, h + 1)
                act.activation(ar_h[:, h % 2, :], bank[AT_BANK + h % 2][:, :], ACT.Copy).then_inc(ar_hi, 1)

            def conv_high(n, h):
                since(act, cv_mm, n, 8, h + 1)
                act.activation(cv_h[:, h, :], bank[CV_BANK + h % 2][:, :], ACT.Copy).then_inc(cv_hi, 1)

            def ff_relu(c, m):
                since(act, ff_mm, c, 8, m + 1)
                since(act, fo_st[m % 2], c, 64, 16 * (m // 2))
                act.activation(fo[:, m % 2, :], bank[m][:, :], ACT.Relu,
                               bias=vec[:, B_FF + m:B_FF + m + 1]).then_inc(ff_ev, 1)

            LAST = CH - 1
            act.wait_ge(band_zeroed, 16)
            for k in range(4):
                y_base(0, k)
            y_high(0, 0)
            y_high(0, 1)
            stat_copy_act(act, LAST - 1, LAST - 1)
            for k in range(KB):
                stat_square_act(act, LAST - 1, k)
                if k + 4 < KB:
                    y_base(0, k + 4)
            a_evac(LAST, A_GROUPS[0])
            stat_std_act(act, LAST - 1)
            for k in range(2, KB):
                y_high(0, k)
            gate_logits(0)
            a_evac(LAST, A_GROUPS[1])
            gate_exp(0)
            for u in range(U_FF, U_FF + 4):
                unit_hi(act, u)
            a_evac(LAST, A_GROUPS[2])
            for h in range(CONV_HEADS + 1):
                if h < CONV_HEADS:
                    turn_evac(0, h)
                    if h == 0:
                        stat_copy_act(act, LAST, LAST)
                if h > 0:
                    conv_high(0, h - 1)
                    stat_square_act(act, LAST, h - 1)
            act.wait_ge(a_st[1], 16 * CH)
            for u in range(U_FF + 4, U_FF + 8):
                unit_hi(act, u)
            stat_std_act(act, LAST)

            def c_squares(n):
                for k in range(KB):
                    ln_square_act(act, n + CH, k, dc[:, k, :])

            def c_std(n):
                if isinstance(n, int) and n == 0:
                    last = lambda e: e.wait_ge(st_st, 32 * CH)
                else:
                    last = lambda e: since(e, xc_sc, n - 1, 8, 8)
                ln_std_act(act, n + CH, last)

            def xc_high(n, k):
                since(act, xc_sc, n, 8, k + 1)
                released(act, n - 1, k, KB, xc_used, qk_mm)
                act.activation(xc_h[:, k, :], dc[:, k, :], ACT.Copy).then_inc(xc_hi, 1)

            def b_step(c, ahead):
                first = isinstance(c, int) and c == 0
                for k in range(KB if ahead else 0):
                    y_base(c + 1, k)
                    y_high(c + 1, k)
                    if first:
                        unit_hi(act, U_FF + 8 + k)
                if ahead:
                    gate_logits(c + 1)
                else:
                    c_squares(0)
                ff_relu(c, 0)
                if first:
                    act.wait_ge(st_st, 32 * CH)
                ff_relu(c, 1)
                if ahead:
                    gate_exp(c + 1)
                ff_relu(c, 2)
                if not ahead:
                    c_std(0)
                    for k in range(KB):
                        xc_high(0, k)
                for m in range(3, 6):
                    ff_relu(c, m)
                for h in range(CONV_HEADS + 1):
                    if ahead and h < CONV_HEADS:
                        turn_evac(c + 1, h)
                    if h == CONV_HEADS:
                        ff_relu(c, 6)
                    if ahead and h > 0:
                        conv_high(c + 1, h - 1)
                ff_relu(c, 7)

            chunks(act, 0, CH - 1, lambda c: b_step(c, True))
            b_step(CH - 1, False)

            def c_softmax_exp(c, m):
                for j in range(2):
                    since(act, s_sub, c, 8, 2 * m + j + 1)
                    act.activation(pr[:, j, :], pr[:, j, :], ACT.Exp).then_inc(s_exp, 1)

            def c_qk(c, m):
                for i, b0 in ((0, B_Q), (1, B_K)):
                    since(act, qk_mm, c, 8, 2 * m + i + 1)
                    if i == 0:
                        since(act, s_mm, c, 8, 2 * m)
                    act.activation(qk_h[:, i, :], bank[i][:, :], ACT.Identity,
                                   bias=vec[:, b0 + m:b0 + m + 1]).then_inc(qk_hi, 1)

            def c_pt(c, m):
                for j in range(2):
                    since(act, pt_mm, c, 8, 2 * m + j + 1)
                    since(act, pv_mm, c, 8, 2 * m + j - 1)
                    act.activation(pt_h[:, j, :], bank[PT_BANK[j]][:, :], ACT.Copy).then_inc(pt_hi, 1)

            def c_vals(c, m):
                for j in range(2):
                    rowsj = slice(HEAD * j, HEAD * j + HEAD)
                    since(act, pv_mm, c, 8, 2 * m + j + 1)
                    if j == 0:
                        since(act, vo_st, c, 64, 16 * m)
                    act.activation(vo[rowsj, :], bank[7][rowsj, :], ACT.Identity,
                                   bias=vec[rowsj, B_V + m:B_V + m + 1]).then_inc(vo_ev, 1)

            for u in range(U_V, U_V + 16):
                unit_hi(act, u)

            def c_values(c, ts):
                for t in ts:
                    since(act, v_mm, c, 4, t + 1)
                    since(act, pv_mm, c - 1, 8, 8)
                    act.activation(v_h[:, t, :], bank[t][:, :], ACT.Copy).then_inc(v_hi, 1)

            c_values(0, range(TILES))
            for u in range(U_V + 16, U_O):
                unit_hi(act, u)
            c_qk(0, 0)

            def c_step(c, ahead):
                later = not (isinstance(c, int) and c == 0)
                c_softmax_exp(c, 0)
                if later:
                    c_vals(c - 1, PAIRS - 1)
                    c_values(c, range(TILES))
                if ahead:
                    c_squares(c + 1)
                c_qk(c, 1)
                c_pt(c, 0)
                c_softmax_exp(c, 1)
                if not ahead:
                    for u in range(U_O, U_O + 4):
                        unit_hi(act, u)
                if ahead:
                    c_std(c + 1)
                c_qk(c, 2)
                c_vals(c, 0)
                if not ahead:
                    unit_hi(act, U_O + 4)
                c_pt(c, 1)
                c_softmax_exp(c, 2)
                if ahead:
                    for k in range(KB):
                        xc_high(c + 1, k)
                c_qk(c, 3)
                c_vals(c, 1)
                if not ahead:
                    unit_hi(act, U_O + 5)
                c_pt(c, 2)
                c_softmax_exp(c, 3)
                if ahead:
                    c_qk(c + 1, 0)
                c_vals(c, 2)
                if not ahead:
                    unit_hi(act, U_O + 6)
                c_pt(c, 3)
                if not ahead:
                    c_vals(c, 3)
                    unit_hi(act, U_O + 7)

            def vs_high(c, ks):
                for k in ks:
                    since(act, vs_ld, c, 16, 16)
                    released(act, c - 1, k, PAIRS, vs_used, o_mm)
                    act.activation(vs_h[:, k, :], vs[:, k, :], ACT.Copy).then_inc(vs_hi, 1)

            chunks(act, 0, CH - 1, lambda c: c_step(c, True))
            c_step(CH - 1, False)

            vs_high(0, range(PAIRS))
            act.wait_ge(dn_zero, 2)
            for u in range(U_UP, U_END):
                unit_hi(act, u)

            def xd_high(n, k):
                since(act, xd_sc, n, 8, k + 1)
                since(act, up_mm, n - 1, 32, 4 * k + 4)
                act.activation(xd_h[:, k, :], dd[:, k, :], ACT.Copy).then_inc(xd_hi, 1)

            for c in range(CH):
                if c > 0:
                    L = 2 * CH + c - 1
                    if c == 1:
                        act.wait_ge(vo_st, 64 * CH)
                    stat_copy_act(act, L, CH + c - 1)
                    for k in range(KB):
                        stat_square_act(act, L, k)
                if c + 1 < CH:
                    vs_high(c + 1, range(PAIRS - 1))
                if c > 0:
                    stat_std_act(act, L, VAR_BANK)
                if c + 1 < CH:
                    vs_high(c + 1, [PAIRS - 1])
            for half in range(2):
                act.wait_ge(o_st[0][half], 16 * (CH // 2))
            xd_high(0, 0)
            xd_high(0, 1)

            def gelus(c, a):
                for i in range(FFB):
                    since(act, up_mm, c, 32, 4 * a + i + 1)
                    since(act, g_lo, c, 32, 4 * a + i - 3)
                    act.activation(gt[:, i, :], bank[i][:, :], ACT.Gelu).then_inc(gelu_ok, 1)
                    since(act, gelu_ok, c, 32, 4 * a + i + 1)
                    since(act, g_used, c, 32, 4 * a + i - 3)
                    act.activation(g_h[:, i, :], gt[:, i, :], ACT.Copy).then_inc(g_hi, 1)

            def d_step(c, ahead):
                first = isinstance(c, int) and c == 0
                for a in range(KB):
                    gelus(c, a)
                    if first:
                        if a == 0:
                            stat_copy_act(act, 3 * CH - 1, 2 * CH - 1)
                        stat_square_act(act, 3 * CH - 1, a)
                        for k in XD_FIRST.get(a, ()):
                            xd_high(0, k)
                    if ahead:
                        for k in XD_SPLIT.get(a, ()):
                            xd_high(c + 1, k)
                if first:
                    stat_std_act(act, 3 * CH - 1)

            chunks(act, 0, CH - 1, lambda c: d_step(c, True))
            d_step(CH - 1, False)

        @block.vector
        def _(v):
            def a_low(c, k):
                since(v, a_hi, c, 8, k + 1)
                v.tensor_tensor(xa_l[:, k, :], xs[:, k, :], xa_h[:, k, :].bitcast(F32),
                                ALU.subtract).then_inc(a_lo, 1)

            for k in range(KB):
                unit_lo(v, U_PROJ + k)
                a_low(0, k)
            for k in range(KB):
                unit_lo(v, U_PROJ + KB + k)
            v.wait_ge(wg_ok, 17)
            v.tensor_tensor(wg_l[:, :, :], wg_raw[:, :, :], wg_h[:, :, :].bitcast(F32), ALU.subtract).then_inc(wg_ok, 1)
            def a_stats(c):
                for k in range(KB):
                    stat_center_dve(v, c, c, k, ho[:, k, :])
                stat_recip_dve(v, c)

            for k in range(KB):
                a_low(1, k)
            with v.Fori(0, CH - 2) as c:
                a_stats(c)
                for k in range(KB):
                    a_low(c + 2, k)

            def y_center(n, k):
                if k == 0:
                    since(v, b_ld, n, 48, 48)
                t = db0 if isinstance(n, int) and n == 0 else db
                v.tensor_tensor(t[:, k, :], t[:, k, :], mt[:, :], ALU.subtract).then_inc(y_cent, 1)

            def y_scale(n, k):
                since(v, y_cent, n, 8, k + 1)
                t = db0 if isinstance(n, int) and n == 0 else db
                v.scalar_tensor_tensor(out=t[:, k, :], in0=t[:, k, :], scalar=vec[:, LN_G + k:LN_G + k + 1],
                                       in1=rt[:, :], op0=ALU.mult, op1=ALU.mult).then_inc(y_scaled, 1)

            def y_prep(n, ks=range(KB)):
                for k in ks:
                    y_center(n, k)
                for k in ks:
                    y_scale(n, k)

            def y_low(n, k):
                since(v, y_b, n, 8, k + 1)
                since(v, yr_hi, n, 8, k + 1)
                src = yb0 if isinstance(n, int) and n == 0 else yb
                v.tensor_tensor(yr_l[:, k % 2, :], src[:, k, :], yr_h[:, k % 2, :].bitcast(F32),
                                ALU.subtract).then_inc(yr_lo, 1)

            def gates(n):
                since(v, lgt_mm, n, 1, 1)
                since(v, skewed, n - 1, 16, 16)
                per = [P, UNITS, TAPS]
                v.tensor_tensor(lg5[:, :, :].rearrange("p (t h) k -> p t (h k)", t=TILES),
                                bank[gate_turn_bank(n)][:, 0:TILES * LOGITS].rearrange("p (t n) -> p t n", t=TILES),
                                bgen[:, :].unsqueeze(1).to_broadcast([P, TILES, LOGITS]),
                                ALU.add).then_inc(sm5, 1)
                since(v, sm5, n, 7, 1)
                v.tensor_reduce(mx5[:, :], lg5[:, :, :], AX.X, ALU.max).then_inc(sm5, 1)
                since(v, sm5, n, 7, 2)
                v.tensor_tensor(lg5[:, :, :], lg5[:, :, :], mx5[:, :].unsqueeze(2).to_broadcast(per),
                                ALU.subtract).then_inc(sm5, 1)
                since(v, exp5, n, 1, 1)
                v.tensor_reduce(su5[:, :], lg5[:, :, :], AX.X, ALU.add).then_inc(sm5, 1)
                since(v, sm5, n, 7, 4)
                v.reciprocal(su5[:, :], su5[:, :]).then_inc(sm5, 1)
                v.tensor_tensor(wk5[:, :, :], lg5[:, :, :], valid[:, :].unsqueeze(1).to_broadcast(per),
                                ALU.mult).then_inc(sm5, 1)
                since(v, sm5, n, 7, 6)
                v.tensor_tensor(wk5[:, :, :], wk5[:, :, :], su5[:, :].unsqueeze(2).to_broadcast(per),
                                ALU.mult).then_inc(sm5, 1)

            def turn_low(n, h):
                since(v, yt_hi, n, 8, h + 1)
                v.tensor_tensor(yt_l[:, h % 2, :], bank[YT_BANK + h % 2][:, :],
                                yt_h[:, h % 2, :].bitcast(F32), ALU.subtract).then_inc(yt_lo, 1)
                since(v, ar_hi, n, 8, h + 1)
                v.tensor_tensor(ar_l[:, h % 2, :], bank[AT_BANK + h % 2][:, :],
                                ar_h[:, h % 2, :].bitcast(F32), ALU.subtract).then_inc(ar_lo, 1)

            def conv_low(n, h):
                since(v, cv_hi, n, 8, h + 1)
                v.tensor_tensor(cv_l[:, h, :], bank[CV_BANK + h % 2][:, :],
                                cv_h[:, h, :].bitcast(F32), ALU.subtract).then_inc(cv_lo, 1)

            v.wait_ge(masks_ok, 14)
            LAST = CH - 1
            y_prep(0, range(4))
            y_low(0, 0)
            y_low(0, 1)
            for k in range(KB):
                stat_center_dve(v, LAST - 1, LAST - 1, k, ho[:, k, :])
                if k + 4 < KB:
                    y_prep(0, [k + 4])
            stat_recip_dve(v, LAST - 1)
            for k in range(2, KB):
                y_low(0, k)
            gates(0)
            for h in range(CONV_HEADS + 1):
                if h < CONV_HEADS:
                    turn_low(0, h)
                if h > 0:
                    stat_center_dve(v, LAST, LAST, h - 1, ho[:, h - 1, :])
                    conv_low(0, h - 1)
            y_prep(1)
            stat_recip_dve(v, LAST)

            def b_step(c, ahead):
                for k in range(KB):
                    y_low(c + 1, k)
                gates(c + 1)
                if ahead:
                    y_prep(c + 2)
                for h in range(CONV_HEADS + 1):
                    if h < CONV_HEADS:
                        turn_low(c + 1, h)
                    if h > 0:
                        conv_low(c + 1, h - 1)

            chunks(v, 0, CH - 2, lambda c: b_step(c, True))
            b_step(CH - 2, False)

            def c_center(n):
                for k in range(KB):
                    ln_center_dve(v, n + CH, k, dc[:, k, :], dc[:, k, :])

            def c_scale_first():
                ln_rstd_dve(v, CH)
                v.wait_ge(ln_sq, 8 * CH + 8)
                for k in range(KB):
                    v.tensor_tensor(dc[:, k, :], dc[:, k, :], rstd[:, :], ALU.mult).then_inc(xc_sc, 1)

            def xc_low(n, k):
                since(v, xc_hi, n, 8, k + 1)
                since(v, xc_sc, n, 8, k + 1)
                v.tensor_tensor(xc_l[:, k, :], dc[:, k, :], xc_h[:, k, :].bitcast(F32),
                                ALU.subtract).then_inc(xc_lo, 1)

            def c_qk(c, m):
                for i, b0 in ((0, B_Q), (1, B_K)):
                    since(v, qk_hi, c, 8, 2 * m + i + 1)
                    v.scalar_tensor_tensor(out=qk_l[:, i, :], in0=bank[i][:, :],
                                           scalar=vec[:, b0 + m:b0 + m + 1], in1=qk_h[:, i, :].bitcast(F32),
                                           op0=ALU.add, op1=ALU.subtract).then_inc(qk_lo, 1)

            def c_softmax_in(c, m):
                for j in range(2):
                    i = 2 * m + j + 1
                    S = bank[4 + j]
                    view = S[:, :].rearrange("p (t n) -> p t n", t=TILES)
                    since(v, s_mm, c, 8, i)
                    v.memset(smax[:, j, :], 0.0)
                    v.copy_predicated(view, masked[:, :].unsqueeze(1).to_broadcast([P, TILES, P]),
                                      negs[:, :].unsqueeze(1).to_broadcast([P, TILES, P])).then_inc(s_masked, 1)
                    since(v, s_masked, c, 8, i)
                    v.tensor_reduce(smax[:, j, :], view, AX.X, ALU.max).then_inc(s_max, 1)
                    since(v, s_max, c, 8, i)
                    since(v, pt_mm, c, 8, i - 2)
                    v.tensor_tensor(pr[:, j, :].rearrange("p (t n) -> p t n", t=TILES), view,
                                    smax[:, j, :].unsqueeze(2).to_broadcast([P, TILES, P]),
                                    ALU.subtract).then_inc(s_sub, 1)

            def c_softmax_out(c, m):
                for j in range(2):
                    i = 2 * m + j + 1
                    view = pr[:, j, :].rearrange("p (t n) -> p t n", t=TILES)
                    since(v, s_exp, c, 8, i)
                    v.tensor_reduce(ssum[:, j, :], view, AX.X, ALU.add).then_inc(s_sum, 1)
                    since(v, s_sum, c, 8, i)
                    v.reciprocal(ssum[:, j, :], ssum[:, j, :]).then_inc(s_rec, 1)
                    since(v, s_rec, c, 8, i)
                    v.tensor_tensor(view, view, ssum[:, j, :].unsqueeze(2).to_broadcast([P, TILES, P]),
                                    ALU.mult).then_inc(s_norm, 1)

            def c_pt(c, m):
                for j in range(2):
                    since(v, pt_hi, c, 8, 2 * m + j + 1)
                    v.tensor_tensor(pt_l[:, j, :], bank[PT_BANK[j]][:, :], pt_h[:, j, :].bitcast(F32),
                                    ALU.subtract).then_inc(pt_lo, 1)

            c_center(0)
            c_scale_first()
            for k in range(KB):
                xc_low(0, k)
            for u in range(U_V, U_V + 16):
                if units[u][3] == "v":
                    unit_lo(v, u)

            def c_values(c, ts):
                for t in ts:
                    since(v, v_hi, c, 4, t + 1)
                    v.tensor_tensor(v_l[:, t, :], bank[t][:, :], v_h[:, t, :].bitcast(F32),
                                    ALU.subtract).then_inc(v_lo, 1)

            c_values(0, range(TILES))
            for u in range(U_V + 16, U_O):
                if units[u][3] == "v":
                    unit_lo(v, u)
            c_qk(0, 0)

            def c_step(c, ahead):
                later = not (isinstance(c, int) and c == 0)
                c_softmax_in(c, 0)
                c_softmax_out(c, 0)
                if later:
                    c_values(c, range(TILES))
                if ahead:
                    c_center(c + 1)
                c_qk(c, 1)
                c_pt(c, 0)
                c_softmax_in(c, 1)
                c_softmax_out(c, 1)
                if ahead:
                    since(v, ln_std, c + 1 + CH, 1, 1)
                    v.reciprocal(rstd[:, :], rstd[:, :]).then_inc(ln_rstd, 1)
                c_qk(c, 2)
                c_pt(c, 1)
                c_softmax_in(c, 2)
                c_softmax_out(c, 2)
                if ahead:
                    for k in range(KB):
                        xc_low(c + 1, k)
                c_qk(c, 3)
                c_pt(c, 2)
                c_softmax_in(c, 3)
                c_softmax_out(c, 3)
                if ahead:
                    c_qk(c + 1, 0)
                c_pt(c, 3)

            chunks(v, 0, CH - 1, lambda c: c_step(c, True))
            c_step(CH - 1, False)

            def o_low(c, ks):
                for k in ks:
                    since(v, vs_hi, c, 4, k + 1)
                    v.tensor_tensor(vs_l[:, k, :], vs[:, k, :], vs_h[:, k, :].bitcast(F32),
                                    ALU.subtract).then_inc(vs_lo, 1)

            def o_evac(c, ms):
                for m in ms:
                    v.wait_ge(o_ld[c % 2][m // 4], 16 * (c // 2 + 1))
                    v.wait_ge(o_mm, 8 * c + m + 1)
                    v.scalar_tensor_tensor(out=h2[c % 2][:, m, :], in0=bank[m][:, :],
                                           scalar=vec[:, B_O + m:B_O + m + 1], in1=h2[c % 2][:, m, :],
                                           op0=ALU.add, op1=ALU.add).then_inc(o_ev, 1)

            def o_center(c, ks):
                for k in ks:
                    stat_center_dve(v, 2 * CH + c, CH + c, k, h2[c % 2][:, k, :])

            def d_prep(n, ks):
                for k in ks:
                    if k == 0:
                        since(v, g_ld, n, 16 * KB, 16 * KB)
                        since(v, d_ld, n, 32, 32)
                    since(v, xd_lo, n - 1, 8, k + 1)
                    since(v, xd_hi, n - 1, 8, k + 1)
                    if isinstance(n, int):
                        dst, src, mean = dd[:, k, :], hg[:, hg_block(n) + k, :], mtd[:, :]
                    else:
                        dst, src, mean = dd[:, k:k + 1, :], hg[:, bass.ds(hg_block(n) + k, 1), :], mtd[:, :].unsqueeze(1)
                    v.tensor_tensor(dst, src, mean, ALU.subtract).then_inc(d_cent, 1)
                for k in ks:
                    since(v, d_cent, n, 8, k + 1)
                    v.tensor_tensor(dd[:, k, :], dd[:, k, :], rtd[:, :], ALU.mult).then_inc(xd_sc, 1)

            def xd_low(n, k):
                since(v, xd_sc, n, 8, k + 1)
                since(v, xd_hi, n, 8, k + 1)
                v.tensor_tensor(xd_l[:, k, :], dd[:, k, :], xd_h[:, k, :].bitcast(F32),
                                ALU.subtract).then_inc(xd_lo, 1)

            o_low(0, range(PAIRS))
            for c in range(CH):
                if c > 0:
                    o_center(c - 1, range(4))
                o_evac(c, A_GROUPS[0])
                if c > 0:
                    o_center(c - 1, range(4, KB))
                o_evac(c, A_GROUPS[1])
                if c + 1 < CH:
                    o_low(c + 1, range(PAIRS - 1))
                else:
                    d_prep(0, range(4, KB))
                o_evac(c, A_GROUPS[2])
                if c + 1 < CH:
                    o_low(c + 1, [PAIRS - 1])
                if c > 0:
                    stat_recip_dve(v, 2 * CH + c - 1)
                if c == CH - 2:
                    d_prep(0, range(4))
            xd_low(0, 0)
            xd_low(0, 1)

            def d_add(c, a):
                since(v, g_used, c, 32, 4 * a + 4)
                if isinstance(c, int):
                    dst, src = hg[:, hg_block(c) + a, :], bank[4 + a % 2][:, :]
                else:
                    dst, src = hg[:, bass.ds(hg_block(c) + a, 1), :], bank[4 + a % 2][:, :].unsqueeze(1)
                v.tensor_tensor(dst, src, dst, ALU.add).then_inc(d_ev, 1)

            def d_step(c, ahead):
                first = isinstance(c, int) and c == 0
                for a in range(KB):
                    for i in range(FFB):
                        since(v, g_hi, c, 32, 4 * a + i + 1)
                        v.tensor_tensor(g_l[:, i, :], gt[:, i, :], g_h[:, i, :].bitcast(F32),
                                        ALU.subtract).then_inc(g_lo, 1)
                    if a >= 1:
                        d_add(c, a - 1)
                    elif not first:
                        d_add(c - 1, KB - 1)
                    if first:
                        o_center(CH - 1, [a])
                        for k in XD_FIRST.get(a, ()):
                            xd_low(0, k)
                    if ahead:
                        d_prep(c + 1, XD_PREP.get(a, ()))
                        for k in XD_SPLIT.get(a, ()):
                            xd_low(c + 1, k)
                if first:
                    stat_recip_dve(v, 3 * CH - 1)

            chunks(v, 0, CH - 1, lambda c: d_step(c, True))
            d_step(CH - 1, False)
            d_add(CH - 1, KB - 1)

        @block.tensor
        def _(pe):
            def a_group(c, g, k):
                ms = A_GROUPS[g]
                if k == 0:
                    since(pe, a_ev, c - 1, 8, ms[-1] + 1)
                    if g == 2:
                        since(pe, ln_std, c - 1, 1, 1)
                if g == 0:
                    since(pe, a_lo, c, 8, k + 1)
                if isinstance(c, int) and c == 0 and g < 2:
                    wait_units(pe, U_PROJ + KB * g + k + 1)
                for m in ms:
                    cols = slice(m * P, (m + 1) * P)
                    mm = split3(pe, bank[m][:, :], (wp_h[:, k, cols], wp_l[:, k, cols]),
                                (xa_h[:, k, :], xa_l[:, k, :]), k == 0, k == KB - 1)
                    if k == KB - 1:
                        mm.then_inc(a_mm, 1)
                if g == 2 and k < KB - 1:
                    mm.then_inc(a_used, 1)

            def a_step(c):
                later = not (isinstance(c, int) and c == 0)
                for g in range(3):
                    for k in range(KB):
                        a_group(c, g, k)
                        if later and (g, k) == (0, 2):
                            if isinstance(c, int):
                                pe.wait_ge(masks_ok, 14)
                            since(pe, a_ev, c - 1, 8, 8)
                            stat_mean_pe(pe, c - 1)
                        if later and (g, k) == (1, 1):
                            stat_var_pe(pe, c - 1, c - 1)

            a_step(0)
            a_step(1)
            with pe.Fori(2, CH - 1) as c:
                a_step(c)

            def gate_block(n, k):
                since(pe, yr_lo, n, 8, k + 1)
                if k == 0:
                    if isinstance(n, int) and n < 2:
                        pe.wait_ge(a_ev, 8 * (CH - 1 + n))
                    else:
                        since(pe, ff_ev, n - 2, 8, 8)
                mm = split3(pe, bank[7][0:LOGITS, :], (wg_h[:, k, :], wg_l[:, k, :]),
                            (yr_h[:, k % 2, :], yr_l[:, k % 2, :]), k == 0, k == KB - 1)
                mm.then_inc(yr_used, 1)

            def gate_turn(n):
                for t in range(TILES):
                    mm = pe.transpose(bank[gate_turn_bank(n)][:, t * LOGITS:(t + 1) * LOGITS],
                                      lg[:, t * P:(t + 1) * P], ident[0:LOGITS, 0:LOGITS])
                mm.then_inc(lgt_mm, 1)

            def turn(n, h):
                first = isinstance(n, int) and n == 0
                if h == 0:
                    since(pe, y_b, n, 8, 8)
                    if first:
                        pe.wait_ge(sm5, 1)
                if h < 2 and not first:
                    since(pe, ff_ev, n - 1, 8, 3 + h)
                if h >= 2:
                    since(pe, yt_lo, n, 8, h - 1)
                y, b = (yb0, band0) if first else (yb, band)
                for t in range(TILES):
                    mm = pe.transpose(bank[YT_BANK + h % 2][:, t * P:(t + 1) * P], y[:, h, t * P:(t + 1) * P],
                                      ident[:, :])
                mm.then_inc(yt_mm, 1)
                if h == 0:
                    since(pe, band_ld, n, 16, 16)
                if h >= 2:
                    since(pe, ar_lo, n, 8, h - 1)
                for t in range(TILES):
                    mm = pe.transpose(bank[AT_BANK + h % 2][:, t * P:(t + 1) * P], b[:, t * CONV_HEADS + h, :],
                                      ident[:, :])
                mm.then_inc(at_mm, 1)

            def conv(n, h):
                if h == 0:
                    since(pe, ff_ev, n - 1, 8, 6)
                if h >= 2:
                    since(pe, cv_lo, n, 8, h - 1)
                since(pe, yt_lo, n, 8, h + 1)
                since(pe, ar_lo, n, 8, h + 1)
                for t in range(TILES):
                    cols = slice(t * P, (t + 1) * P)
                    mm = split3(pe, bank[CV_BANK + h % 2][:, cols], (yt_h[:, h % 2, cols], yt_l[:, h % 2, cols]),
                                (ar_h[:, h % 2, cols], ar_l[:, h % 2, cols]), True, True)
                mm.then_inc(cv_mm, 1)

            def ff_group(c, g, k):
                ms = A_GROUPS[g]
                if g == 0:
                    since(pe, cv_lo, c, 8, k + 1)
                if isinstance(c, int) and c == 0 and g < 2:
                    wait_units(pe, U_FF + KB * g + k + 1)
                for m in ms:
                    cols = slice(m * P, (m + 1) * P)
                    mm = split3(pe, bank[m][:, :], (wf_h[:, k, cols], wf_l[:, k, cols]),
                                (cv_h[:, k, :], cv_l[:, k, :]), k == 0, k == KB - 1)
                    if k == KB - 1:
                        mm.then_inc(ff_mm, 1)

            def b_step(c, ahead):
                first = isinstance(c, int) and c == 0
                gates = GATES_AT[first]
                for i in range(2 * KB):
                    if not ahead and i == 1:
                        pe.wait_ge(ff_ev, 8 * (CH - 1))
                        ln_mean_pe(pe, CH)
                    if not ahead and i == 9:
                        ln_var_pe(pe, CH)
                    if ahead and i == TURN_AFTER[first]:
                        since(pe, lg_ev, c + 1, 1, 1)
                    ff_group(c, i // KB, i % KB)
                    if ahead:
                        for j in gates.get(i, ()):
                            gate_block(c + 1, j)
                    if ahead and i == TURN_AFTER[first]:
                        gate_turn(c + 1)
                if ahead:
                    turn(c + 1, 0)
                    since(pe, sm5, c + 1, 7, 1)
                if isinstance(c, int) and c == 0:
                    pe.wait_ge(ln_std, CH)
                elif ahead:
                    since(pe, ff_ev, c - 1, 8, 8)
                else:
                    pe.wait_ge(ln_std, CH + 1)
                for k in range(KB):
                    ff_group(c, 2, k)
                    if ahead:
                        if k + 1 < KB:
                            turn(c + 1, k + 1)
                        conv(c + 1, k)

            pe.wait_ge(wg_ok, 18)
            LAST = CH - 1
            for k in range(KB):
                a_group(LAST, 0, k)
                if k == 2:
                    pe.wait_ge(a_ev, 8 * LAST)
                    stat_mean_pe(pe, LAST - 1)
            for k in range(KB):
                a_group(LAST, 1, k)
                gate_block(0, k)
                if k == 1:
                    stat_var_pe(pe, LAST - 1, LAST - 1)
            pe.wait_ge(lg_ev, 1)
            for k in range(KB):
                a_group(LAST, 2, k)
                if k == 1:
                    pe.wait_ge(a_ev, 8 * LAST + 1)
                    gate_turn(0)
            pe.wait_ge(a_ev, 8 * CH)
            turn(0, 0)
            stat_mean_pe(pe, LAST)
            for h in range(CONV_HEADS):
                if h + 1 < CONV_HEADS:
                    turn(0, h + 1)
                conv(0, h)
            stat_var_pe(pe, LAST, LAST)

            chunks(pe, 0, CH - 1, lambda c: b_step(c, True))
            b_step(CH - 1, False)

            def c_values(c, ts):
                if isinstance(c, int) and c == 0:
                    pe.wait_ge(ff_ev, 8 * CH)
                elif 2 in ts:
                    since(pe, pt_lo, c - 1, 8, 8)
                else:
                    since(pe, qk_lo, c, 8, 2)
                for k in range(KB):
                    since(pe, xc_lo, c, 8, k + 1)
                    if isinstance(c, int) and c == 0:
                        wait_units(pe, U_V + k + 1)
                    for t in ts:
                        cols = slice(t * P, (t + 1) * P)
                        mm = split3(pe, bank[t][:, :], (xc_h[:, k, cols], xc_l[:, k, cols]),
                                    (wv_h[:, k, :], wv_l[:, k, :]), k == 0, k == KB - 1)
                        if k == KB - 1:
                            mm.then_inc(v_mm, 1)

            def c_qk(c, m, beside=None):
                first = isinstance(c, int) and c == 0
                if m == 1 or (m == 0 and first):
                    since(pe, v_lo, c, 4, 2)
                elif m == 0:
                    since(pe, qk_lo, c - 1, 8, 8)
                cols = slice(m * P, (m + 1) * P)
                for k in range(KB):
                    if m == 0:
                        since(pe, xc_lo, c, 8, k + 1)
                        if first:
                            wait_units(pe, U_QK + 2 * k + 2)
                    for i, (wh, wl) in enumerate(((wq_h, wq_l), (wk_h, wk_l))):
                        mm = split3(pe, bank[i][:, :], (wh[:, k, cols], wl[:, k, cols]),
                                    (xc_h[:, k, :], xc_l[:, k, :]), k == 0, k == KB - 1)
                        if k == KB - 1:
                            mm.then_inc(qk_mm, 1)
                    if m == PAIRS - 1 and k < KB - 1:
                        mm.then_inc(xc_used, 1)
                    if beside and k == 3:
                        beside()

            def c_scores(c, m):
                since(pe, qk_lo, c, 8, 2 * m + 2)
                for j in range(2):
                    since(pe, s_sub, c, 8, 2 * m + j - 1)
                    r = slice(HEAD * j, HEAD * j + HEAD)
                    for t in range(TILES):
                        cols = slice(t * P, (t + 1) * P)
                        mm = split3(pe, bank[4 + j][:, cols], (qk_h[r, 0, cols], qk_l[r, 0, cols]),
                                    (qk_h[r, 1, cols], qk_l[r, 1, cols]), True, True)
                    mm.then_inc(s_mm, 1)

            def c_turn(c, m):
                for j in range(2):
                    since(pe, s_norm, c, 8, 2 * m + j + 1)
                    if m == 0 and j == 0:
                        since(pe, v_lo, c, 4, 4)
                    since(pe, pt_lo, c, 8, 2 * m + j - 1)
                    for t in range(TILES):
                        cols = slice(t * P, (t + 1) * P)
                        mm = pe.transpose(bank[PT_BANK[j]][:, cols], pr[:, j, cols], ident[:, :])
                    mm.then_inc(pt_mm, 1)

            def c_mix(c, m):
                for j in range(2):
                    since(pe, pt_lo, c, 8, 2 * m + j + 1)
                    since(pe, vo_ev, c, 8, 2 * m + j)
                    since(pe, v_lo, c, 4, 4)
                    for t in range(TILES):
                        cols = slice(t * P, (t + 1) * P)
                        pair = slice(m * P, (m + 1) * P)
                        mm = split3(pe, bank[7][:, cols], (v_h[:, t, pair], v_l[:, t, pair]),
                                    (pt_h[:, j, cols], pt_l[:, j, cols]), True, True)
                    mm.then_inc(pv_mm, 1)

            def c_step(c, ahead):
                later = not (isinstance(c, int) and c == 0)
                c_scores(c, 0)
                if later:
                    c_values(c, (0, 1))
                    c_mix(c - 1, 3)
                    c_values(c, (2, 3))
                if ahead:
                    ln_mean_pe(pe, c + 1 + CH)
                c_qk(c, 1)
                c_turn(c, 0)
                c_scores(c, 1)
                c_qk(c, 2, (lambda: ln_var_pe(pe, c + 1 + CH)) if ahead else None)
                c_mix(c, 0)
                c_turn(c, 1)
                c_scores(c, 2)
                c_qk(c, 3)
                c_mix(c, 1)
                c_turn(c, 2)
                c_scores(c, 3)
                if ahead:
                    c_qk(c + 1, 0)
                c_mix(c, 2)
                c_turn(c, 3)

            c_values(0, range(TILES))
            c_qk(0, 0)
            chunks(pe, 0, CH - 1, lambda c: c_step(c, True))
            c_step(CH - 1, False)
            c_mix(CH - 1, 3)

            def o_group(c, g, k):
                ms = A_GROUPS[g]
                if c == 0 and g < 2:
                    wait_units(pe, U_O + PAIRS * g + k + 1)
                if k == 0 and c > 0:
                    pe.wait_ge(o_ev, 8 * (c - 1) + ms[-1] + 1)
                if k == 0 and g == 1 and c > 1:
                    pe.wait_ge(ln_std, 2 * CH + c - 1)
                if k == 0 and g == 2 and c > 0:
                    pe.wait_ge(st_copied, CH + c)
                if g == 0:
                    since(pe, vs_lo, c, 4, k + 1)
                for m in ms:
                    cols = slice(m * P, (m + 1) * P)
                    mm = split3(pe, bank[m][:, :], (wo_h[:, k, cols], wo_l[:, k, cols]),
                                (vs_h[:, k, :], vs_l[:, k, :]), k == 0, k == PAIRS - 1)
                    if k == PAIRS - 1:
                        mm.then_inc(o_mm, 1)
                if g == 2 and k < PAIRS - 1:
                    mm.then_inc(vs_used, 1)

            pe.wait_ge(vo_ev, 8 * CH)
            for c in range(CH):
                for g in range(3):
                    for k in range(PAIRS):
                        o_group(c, g, k)
                        if c > 0 and (g, k) == (0, 2):
                            pe.wait_ge(o_ev, 8 * c)
                            stat_mean_pe(pe, 2 * CH + c - 1)
                        if c > 0 and (g, k) == (2, 3):
                            pe.wait_ge(o_ev, 8 * c + VAR_BANK + 1)
                            stat_var_pe(pe, 2 * CH + c - 1, CH + c - 1, VAR_BANK)

            def ff_up(c, a, i):
                j, blk = i // 2, i % 2
                if i == 0:
                    since(pe, xd_lo, c, 8, a + 1)
                since(pe, gelu_ok, c, 32, 4 * a + i - 3)
                r = slice(FF_IN * j, FF_IN * (j + 1))
                cols = slice(blk * P, (blk + 1) * P)
                mm = split3(pe, bank[i][:, :], (up_h[r, a, cols], up_l[r, a, cols]),
                            (xd_h[r, a, :], xd_l[r, a, :]), True, True)
                mm.then_inc(up_mm, 1)

            def ff_down(c, a, i):
                since(pe, g_lo, c, 32, 4 * a + i + 1)
                if i == 0:
                    since(pe, d_ev, c, 8, a - 1)
                mm = split3(pe, bank[4 + a % 2][:, :], (dn_h[:, FFB * a + i, :], dn_l[:, FFB * a + i, :]),
                            (g_h[:, i, :], g_l[:, i, :]), i == 0, i == FFB - 1)
                mm.then_inc(g_used, 1)

            def d_step(c, ahead):
                for a in range(KB):
                    for i in range(FFB):
                        if a + 1 < KB:
                            ff_up(c, a + 1, i)
                        elif ahead:
                            ff_up(c + 1, 0, i)
                        ff_down(c, a, i)
                    if isinstance(c, int) and c == 0 and a == 0:
                        stat_mean_pe(pe, 3 * CH - 1)
                if isinstance(c, int) and c == 0:
                    stat_var_pe(pe, 3 * CH - 1, 2 * CH - 1)

            pe.wait_ge(o_ev, 8 * CH)
            pe.wait_ge(ln_std, 3 * CH - 1)
            wait_units(pe, U_END)
            for i in range(FFB):
                ff_up(0, 0, i)
            chunks(pe, 0, CH - 1, lambda c: d_step(c, True))
            d_step(CH - 1, False)


A_GROUPS = [(0, 1, 2), (3, 4, 5), (6, 7)]
YT_BANK, AT_BANK, CV_BANK = 0, 2, 4
GATES_AT = [{0: (0,), 1: (1, 2), 2: (3, 4), 3: (5, 6), 4: (7,)}, {4: (0, 1), 5: (2, 3), 6: (4, 5), 7: (6, 7)}]
TURN_AFTER = [6, 8]
PT_BANK = [2, 3]
VAR_BANK = 3
XD_PREP = {3: (0, 1), 4: (2, 3), 5: (4, 5), 6: (6, 7)}
XD_FIRST = {0: (2, 3), 1: (4, 5), 2: (6, 7)}
XD_SPLIT = {4: (0, 1), 5: (2, 3), 6: (4, 5), 7: (6, 7)}


def hg_block(n):
    return (n + 1) % 2 * KB


def gate_turn_bank(n):
    return 0 if isinstance(n, int) and n == 0 else 7


def kernel(**inputs):
    import numpy as np
    import concourse.bacc as bacc
    from concourse.bass_utils import run_bass_kernel_spmd

    a = {k: np.asarray(v) for k, v in inputs.items()}

    def cols(v):
        return v.reshape(-1, P).T

    arrays = {
        "x_t": a["x"].reshape(TOKENS, D).T,
        "w_proj": a["L0_tok_W_proj"],
        "w_ff": a["L0_tok_W_ff"],
        "w_gen": a["L0_tok_W_wgen"],
        "w_qkv_t": a["L0_attn_w_qkv"].T,
        "w_o_t": a["L0_attn_w_o"].T,
        "up": a["L0_ffn_up"],
        "down": a["L0_ffn_down"],
        "vecs": np.concatenate([cols(a["L0_tok_b_proj"]), cols(a["L0_tok_ln_g"]), cols(a["L0_tok_ln_b"]),
                                cols(a["L0_tok_b_ff"]), cols(a["L0_attn_b_o"]), cols(a["L0_attn_b_qkv"])], axis=1),
        "b_gen": a["L0_tok_b_wgen"],
        "perm": cols(a["L0_ffn_perm"]),
    }
    nc = bacc.Bacc("TRN2", target_bir_lowering=False, num_devices=1)
    given, args = {}, []
    for name, v in arrays.items():
        v = np.ascontiguousarray(v)
        given[name] = v
        args.append(nc.dram_tensor(name, v.shape, mybir.dt.from_np(v.dtype), kind="ExternalInput").ap())
    for c in range(CH):
        args.append(nc.dram_tensor(f"out_{c}", (D, N), mybir.dt.float32, kind="ExternalOutput").ap())
    audio_tower(nc, *args)
    r = run_bass_kernel_spmd(nc, [given], core_ids=[0])
    got = np.stack([r.results[0][f"out_{c}"].T for c in range(CH)])
    return np.ascontiguousarray(got).reshape(BATCH, SEQ, D)
```

```python
import concourse.bass as bass
from concourse import mybir
from contextlib import ExitStack

BATCH, FRAMES, CHANNELS, STRIDE = 32, 256, 256, 4
SEQ = FRAMES // STRIDE
D = CHANNELS * STRIDE
TOKENS = BATCH * SEQ
P = 128
KB = D // P
N = 512
CH = TOKENS // N
TILES = N // P
TAPS, CONV_HEADS = 5, 8
LOGITS = TAPS * CONV_HEADS
PART = 512
HEAD = 64
PAIRS = PART // P
FF_HEADS, FF_IN, FF_MID = 16, 64, 256
FFB = 2 * FF_MID // P
EPS = 1e-5
MASKED = -10000.0
OTHER = -3.0e38
B_PROJ, LN_G, LN_B, B_FF, B_O, B_Q, B_K, B_V, B_GEN = 0, 8, 16, 24, 32, 40, 44, 48, 52
VECS = 53
BAND = P * (P + 1)
UNITS = TILES * CONV_HEADS


def audio_tower(nc, x_t, w_proj, w_ff, w_gen, w_qkv_t, w_o_t, up, down, vecs, perm, *outs):
    F32, F32R, I32, U8 = mybir.dt.float32, mybir.dt.float32r, mybir.dt.int32, mybir.dt.uint8
    ALU, ACT, AX = mybir.AluOpType, mybir.ActivationFunctionType, mybir.AxisListType

    h0_s = nc.dram_tensor("h0_s", [CH, P, KB * N], F32, kind="Internal").ap()
    h1_s = nc.dram_tensor("h1_s", [CH, P, KB * N], F32, kind="Internal").ap()
    vals_s = nc.dram_tensor("vals_s", [CH, P, PAIRS * N], F32, kind="Internal").ap()
    h2_s = [nc.dram_tensor(f"h2_s{c}", [D, N], F32, kind="Internal").ap() for c in range(CH)]
    stat_s = nc.dram_tensor("stat_s", [2 * CH, 2, N], F32, kind="Internal").ap()
    band_s = nc.dram_tensor("band_s", [UNITS * BAND], F32, kind="Internal").ap()

    ctx = ExitStack()
    with ctx:
        base = (nc.sbuf_base + 63) // 64 * 64
        def place(name, shape, dt, at):
            return nc.alloc_sbuf_tensor_at(name, shape, dt, offset=base + at)

        def sem(name):
            return ctx.enter_context(nc.semaphore(name))

        KIB = 1024
        R1, R2, CONST = 0, 64 * KIB, 128 * KIB
        STAGE = CONST + 7 * KIB
        LNT = STAGE + 8 * KIB
        E = LNT + 10 * KIB
        ident = place("ident", [P, P], F32, CONST)
        fold = place("fold", [P, LOGITS], F32, CONST + 1792)
        mean_w = place("mean_w", [P, P], F32, CONST + 512)
        negs = place("negs", [P, P], F32, CONST + 1024)
        vec = place("vec", [P, VECS], F32, CONST + 1536)
        valid = place("valid", [P, TAPS], F32, CONST + 1984)
        eps = place("eps", [P, 1], F32, CONST + 2016)
        rows = place("rows", [P, KB], I32, CONST + 2048)
        masked = place("masked", [P, P], U8, CONST + 2176)
        maskf = place("maskf", [P, P], F32, LNT)
        wg = place("wg", [P, KB, 2, LOGITS], F32R, CONST + 2304)
        smax = place("smax", [P, 2, TILES], F32, CONST + 4992)
        ssum = place("ssum", [P, 2, TILES], F32, CONST + 5056)
        mx5 = place("mx5", [P, UNITS], F32, CONST + 5120)
        su5 = place("su5", [P, UNITS], F32, CONST + 5248)
        lg5 = place("lg5", [P, UNITS, TAPS], F32, CONST + 5376)
        wk5 = place("wk5", [P, UNITS, TAPS], F32, CONST + 6016)
        rstd4 = place("rstd4", [P, TILES], F32, CONST + 6656)
        stage = place("stage", [P, 4, N], F32, STAGE)
        wg_raw = place("wg_raw", [P, KB, LOGITS], F32, LNT + 6 * KIB)
        acc = place("acc", [P, N], F32, LNT)
        sq = place("sq", [P, 2, N], F32, LNT + 2 * KIB)
        vacc = place("vacc", [P, N], F32, LNT + 6 * KIB)
        rstd = place("rstd", [P, N], F32, LNT + 8 * KIB)
        wp_h = place("wp_h", [P, KB, D], F32R, R1)
        wp_l = place("wp_l", [P, KB, D], F32R, R1 + 32 * KIB)
        xa_h = place("xa_h", [P, KB, N], F32R, E)
        xa_l = place("xa_l", [P, KB, N], F32R, E + 16 * KIB)
        xs = place("xs", [P, KB, N], F32, R2)
        ho = place("ho", [P, KB, N], F32, R2 + 16 * KIB)
        zero = place("zero", [P, UNITS * BAND // P], F32, E + 32 * KIB)
        mean_t = place("mean_t", [P, N], F32, E + 52 * KIB)
        db0 = place("db0", [P, KB, N], F32, R2 + 32 * KIB)
        band0 = place("band0", [P, UNITS, P], F32, R2 + 32 * KIB)
        yb0 = place("yb0", [P, KB, N], F32, R2 + 48 * KIB)
        wf_h = place("wf_h", [P, KB, D], F32R, R2)
        wf_l = place("wf_l", [P, KB, D], F32R, R2 + 32 * KIB)
        db = place("db", [P, KB, N], F32, R1)
        yb = place("yb", [P, KB, N], F32, R1 + 16 * KIB)
        cv_h = place("cv_h", [P, KB, N], F32R, R1 + 32 * KIB)
        cv_l = place("cv_l", [P, KB, N], F32R, R1 + 48 * KIB)
        yt_h = place("yt_h", [P, 2, N], F32R, E)
        yt_l = place("yt_l", [P, 2, N], F32R, E + 4 * KIB)
        ar_h = place("ar_h", [P, 2, N], F32R, E + 8 * KIB)
        ar_l = place("ar_l", [P, 2, N], F32R, E + 12 * KIB)
        band = place("band", [P, UNITS, P], F32, E + 16 * KIB)
        yr_h = place("yr_h", [P, 2, N], F32R, E + 32 * KIB)
        yr_l = place("yr_l", [P, 2, N], F32R, E + 36 * KIB)
        lg = place("lg", [2 * LOGITS, N], F32, E + 40 * KIB)
        mt = place("mt", [P, N], F32, E + 42 * KIB)
        rt = place("rt", [P, N], F32, E + 44 * KIB)
        res = place("res", [P, 2, N], F32, E + 46 * KIB)
        fo = [place(f"fo{i}", [P, N], F32, at)
              for i, at in enumerate((E + 50 * KIB, E + 52 * KIB, LNT + 2 * KIB, LNT + 4 * KIB))]
        sq0 = place("sq0", [P, 2, N], F32, E + 32 * KIB)
        d3 = place("d3", [P, KB, N], F32, R1 + 16 * KIB)
        dc = place("dc", [P, KB, N], F32, R1)
        v_h = place("v_h", [P, TILES, PART], F32R, R1 + 16 * KIB)
        v_l = place("v_l", [P, TILES, PART], F32R, R1 + 24 * KIB)
        wk_h = place("wk_h", [P, KB, PART], F32R, R1 + 32 * KIB)
        wk_l = place("wk_l", [P, KB, PART], F32R, R1 + 48 * KIB)
        wv_h = place("wv_h", [P, KB, PART], F32R, R2)
        wv_l = place("wv_l", [P, KB, PART], F32R, R2 + 16 * KIB)
        wq_h = place("wq_h", [P, KB, PART], F32R, R2 + 32 * KIB)
        wq_l = place("wq_l", [P, KB, PART], F32R, R2 + 48 * KIB)
        xc_h = place("xc_h", [P, KB, N], F32R, E)
        xc_l = place("xc_l", [P, KB, N], F32R, E + 16 * KIB)
        qk_h = place("qk_h", [P, 2, N], F32R, E + 32 * KIB)
        qk_l = place("qk_l", [P, 2, N], F32R, E + 36 * KIB)
        pr = place("pr", [P, 2, N], F32, E + 40 * KIB)
        pt_h = place("pt_h", [P, 2, N], F32R, E + 44 * KIB)
        pt_l = place("pt_l", [P, 2, N], F32R, E + 48 * KIB)
        vo = place("vo", [P, N], F32, E + 52 * KIB)
        wo_h = place("wo_h", [P, PAIRS, D], F32R, R2)
        wo_l = place("wo_l", [P, PAIRS, D], F32R, R2 + 16 * KIB)
        vs_h = place("vs_h", [P, PAIRS, N], F32R, R1)
        vs_l = place("vs_l", [P, PAIRS, N], F32R, R1 + 8 * KIB)
        vs = place("vs", [P, PAIRS, N], F32, E + 16 * KIB)
        vs0 = place("vs0", [P, PAIRS, N], F32, LNT)
        h2 = [place(f"h2_{i}", [P, KB, N], F32, E + 32 * i * KIB) for i in range(2)]
        up_h = place("up_h", [P, KB, FF_MID], F32R, R1 + 16 * KIB)
        up_l = place("up_l", [P, KB, FF_MID], F32R, R1 + 24 * KIB)
        dn_h = place("dn_h", [P, KB * FFB, P], F32R, R1 + 32 * KIB)
        dn_l = place("dn_l", [P, KB * FFB, P], F32R, R1 + 48 * KIB)
        gt = place("gt", [P, FFB, N], F32, R2)
        g_h = place("g_h", [P, FFB, N], F32R, R2 + 8 * KIB)
        g_l = place("g_l", [P, FFB, N], F32R, R1)
        hg = place("hg", [P, 2 * KB, N], F32, R2 + 16 * KIB)
        dd = place("dd", [P, KB, N], F32, R2 + 48 * KIB)
        xd_h = place("xd_h", [P, KB, N], F32R, E)
        xd_l = place("xd_l", [P, KB, N], F32R, E + 16 * KIB)
        mtd = place("mtd", [P, N], F32, E + 48 * KIB)
        rtd = place("rtd", [P, N], F32, E + 50 * KIB)

        bank = [ctx.enter_context(nc.psum_tensor(f"bank{i}", [P, N], F32)) for i in range(8)]
        LN_BANK = 6

        const_ld = sem("const_ld")
        masks_ok = sem("masks_ok")
        stage_ld = [sem(f"stage_ld{i}") for i in range(4)]
        w_hi = sem("w_hi")
        w_lo_v = sem("w_lo_v")
        w_lo_g = sem("w_lo_g")
        wg_ok = sem("wg_ok")
        zero_ok, band_zeroed = sem("zero_ok"), sem("band_zeroed")
        a_ld = [sem(f"a_ld{k}") for k in range(KB)]
        a_hi, a_lo, a_used, a_mm, a_ev = (sem(s) for s in ("a_hi", "a_lo", "a_used", "a_mm", "a_ev"))
        a_st = [sem(f"a_st{g}") for g in range(2)]
        ln_pool, ln_mean, ln_d, ln_sq, ln_var, ln_std, ln_rstd = (
            sem(s) for s in ("ln_pool", "ln_mean", "ln_d", "ln_sq", "ln_var", "ln_std", "ln_rstd"))
        st_copied, mean_st, rstd_st = sem("st_copied"), sem("mean_st"), sem("rstd_st")
        b_ld, y_cent = sem("b_ld"), sem("y_cent")
        y_scaled, y_b, yr_hi, yr_lo, yr_used, lg_ev, lgt_mm = (
            sem(s) for s in ("y_scaled", "y_b", "yr_hi", "yr_lo", "yr_used", "lg_ev", "lgt_mm"))
        sm5, exp5, skewed = (sem(s) for s in ("sm5", "exp5", "skewed"))
        band_ld = [sem(f"band_ld{i}") for i in range(2)]
        yt_mm, at_mm, yt_hi, ar_hi, yt_lo, ar_lo = (
            sem(s) for s in ("yt_mm", "at_mm", "yt_hi", "ar_hi", "yt_lo", "ar_lo"))
        cv_mm, cv_hi, cv_lo, ff_mm, ff_ev, ff_add = (
            sem(s) for s in ("cv_mm", "cv_hi", "cv_lo", "ff_mm", "ff_ev", "ff_add"))
        res_ld = [sem(f"res_ld{i}") for i in range(2)]
        fo_st = [sem(f"fo_st{i}") for i in range(4)]
        c_ld, xc_sc, xc_hi, xc_lo, xc_used = (sem(s) for s in ("c_ld", "xc_sc", "xc_hi", "xc_lo", "xc_used"))
        v_mm, v_hi, v_lo, qk_mm, qk_hi, qk_lo = (
            sem(s) for s in ("v_mm", "v_hi", "v_lo", "qk_mm", "qk_hi", "qk_lo"))
        s_mm, s_masked, s_max, s_sub, s_exp, s_sum, s_rec, s_norm = (
            sem(s) for s in ("s_mm", "s_masked", "s_max", "s_sub", "s_exp", "s_sum", "s_rec", "s_norm"))
        pt_mm, pt_hi, pt_lo, pv_mm, vo_ev, vo_st = (
            sem(s) for s in ("pt_mm", "pt_hi", "pt_lo", "pv_mm", "vo_ev", "vo_st"))
        vs_ld, vs_hi, vs_lo, vs_used, o_mm, o_ev = (
            sem(s) for s in ("vs_ld", "vs_hi", "vs_lo", "vs_used", "o_mm", "o_ev"))
        o_ld = [[sem(f"o_ld{i}{g}") for g in range(2)] for i in range(2)]
        o_st = [[sem(f"o_st{i}{g}") for g in range(2)] for i in range(2)]
        d_ld, d_cent = sem("d_ld"), sem("d_cent")
        g_ld, xd_sc, xd_hi, xd_lo = (sem(s) for s in ("g_ld", "xd_sc", "xd_hi", "xd_lo"))
        up_mm, gelu_ok, g_hi, g_lo, g_used, d_ev, d_st, dn_zero = (
            sem(s) for s in ("up_mm", "gelu_ok", "g_hi", "g_lo", "g_used", "d_ev", "d_st", "dn_zero"))

        def since(e, s, c, per, k):
            if isinstance(c, int):
                if c * per + k > 0:
                    e.wait_ge(s, c * per + k)
            else:
                e.wait_ge(s, c * per + k)

        def chunks(e, first, last, body):
            body(first)
            if last - first > 1:
                with e.Fori(first + 1, last) as c:
                    body(c)

        def released(e, c, k, blocks, used, done):
            if k < blocks - 1:
                since(e, used, c, blocks - 1, k + 1)
            else:
                since(e, done, c, 8, 8)

        def weight_units():
            units = []
            for half in range(2):
                for k in range(KB):
                    cols = slice(half * N, half * N + N)
                    units.append((w_proj[k * P:(k + 1) * P, cols], wp_h[:, k, cols], wp_l[:, k, cols], "v"))
            for half in range(2):
                for k in range(KB):
                    cols = slice(half * N, half * N + N)
                    units.append((w_ff[k * P:(k + 1) * P, cols], wf_h[:, k, cols], wf_l[:, k, cols], "g"))
            for k in range(KB):
                units.append((w_qkv_t[k * P:(k + 1) * P, 2 * PART:3 * PART], wv_h[:, k, :], wv_l[:, k, :], "v"))
            for k in range(KB):
                for col, h, l, who in ((0, wq_h, wq_l, "g" if k < 4 else "v"), (1, wk_h, wk_l, "v")):
                    units.append((w_qkv_t[k * P:(k + 1) * P, col * PART:(col + 1) * PART],
                                  h[:, k, :], l[:, k, :], who))
            for half in range(2):
                for k in range(PAIRS):
                    cols = slice(half * N, half * N + N)
                    units.append((w_o_t[k * P:(k + 1) * P, cols], wo_h[:, k, cols], wo_l[:, k, cols], "g"))
            for head in range(0, FF_HEADS, 4):
                src = down[head:head + 4].rearrange("h (b p) d -> p h b d", p=P)
                sl = slice(2 * head, 2 * head + 8)
                units.append((src, dn_h[:, sl, :], dn_l[:, sl, :], "g"))
            for k in range(0, KB, 2):
                src = up[2 * k:2 * k + 4].rearrange("(a s) d m -> (s d) a m", s=2)
                units.append((src, up_h[:, k:k + 2, :], up_l[:, k:k + 2, :], "g"))
            return units

        units = weight_units()
        U_PROJ, U_FF, U_V, U_QK, U_O, U_DN, U_UP, U_END = 0, 16, 32, 40, 56, 64, 68, 72
        lo_before = [[sum(1 for u in units[:n] if u[3] == who) for n in range(len(units) + 1)] for who in "vg"]

        def wait_units(e, upto):
            if lo_before[0][upto]:
                e.wait_ge(w_lo_v, lo_before[0][upto])
            if lo_before[1][upto]:
                e.wait_ge(w_lo_g, lo_before[1][upto])

        def unit_load(e, u):
            if u >= 4:
                who = 0 if units[u - 4][3] == "v" else 1
                e.wait_ge((w_lo_v, w_lo_g)[who], lo_before[who][u - 3])
            src = units[u][0]
            if U_DN <= u < U_UP:
                for i in range(4):
                    e.dma_start(stage[:, u % 4, i * P:(i + 1) * P].rearrange("p (b d) -> p b d", b=2),
                                src[:, i]).then_inc(stage_ld[u % 4], 16)
            else:
                dst = stage[:, u % 4, :]
                if u >= U_UP:
                    for i in range(2):
                        for s in range(2):
                            e.dma_start(stage[64 * s:64 * s + 64, u % 4, i * FF_MID:(i + 1) * FF_MID],
                                        up[4 * (u - U_UP) + 2 * i + s]).then_inc(stage_ld[u % 4], 16)
                else:
                    e.dma_start(dst, src).then_inc(stage_ld[u % 4], 16)

        def slot_count(u):
            return sum(16 * (4 if v >= U_DN else 1) for v in range(u % 4, u + 1, 4))

        def unit_views(u):
            st = stage[:, u % 4, :]
            if u < U_DN:
                return [(st, units[u][1], units[u][2])]
            if u >= U_UP:
                return [(st.rearrange("p (a m) -> p a m", a=2), units[u][1], units[u][2])]
            v4 = st.rearrange("p (a s b d) -> p a s b d", a=2, s=2, b=2)
            out_views = []
            for s in range(2):
                h, l = (t.rearrange("p (a s b) (c d) -> p a s b c d", a=2, s=2, c=2)[:, :, s, :, s, :]
                        for t in (units[u][1], units[u][2]))
                out_views.append((v4[:, :, s], h, l))
            return out_views

        def unit_hi(act, u):
            act.wait_ge(stage_ld[u % 4], slot_count(u))
            for i, (st, h, _) in enumerate(unit_views(u)):
                ins = act.activation(h, st, ACT.Copy)
            ins.then_inc(w_hi, 1)

        def unit_lo(e, u):
            e.wait_ge(w_hi, u + 1)
            e.wait_ge(stage_ld[u % 4], slot_count(u))
            s = w_lo_v if units[u][3] == "v" else w_lo_g
            for i, (st, h, l) in enumerate(unit_views(u)):
                ins = e.tensor_tensor(l, st, h.bitcast(F32), ALU.subtract)
            ins.then_inc(s, 1)

        def split3(pe, o, w_hl, x_hl, start, stop):
            (wh, wl), (xh, xl) = w_hl, x_hl
            pe.matmul(o, wh, xh, start=start, stop=False)
            pe.matmul(o, wh, xl, start=False, stop=False)
            return pe.matmul(o, wl, xh, start=False, stop=stop)

        def ln_sum_pool(g, L, blk):
            g.tensor_tensor(acc[:, :], blk(0), blk(1), ALU.add).then_inc(ln_pool, 1)
            for k in range(2, KB):
                since(g, ln_pool, L, 14, k - 1)
                g.tensor_tensor(acc[:, :], acc[:, :], blk(k), ALU.add).then_inc(ln_pool, 1)

        def ln_mean_pe(pe, L):
            since(pe, ln_pool, L, 14, 7)
            since(pe, ln_std, L - 1, 1, 1)
            pe.matmul(bank[LN_BANK][:, :], mean_w[:, :], acc[:, :], start=True, stop=True).then_inc(ln_mean, 1)

        def ln_center_dve(v, L, k, src, dst):
            if k == 0:
                since(v, ln_mean, L, 1, 1)
            v.tensor_tensor(dst, src, bank[LN_BANK][:, :], ALU.subtract).then_inc(ln_d, 1)

        def ln_square_act(act, L, k, d):
            since(act, ln_d, L, 8, k + 1)
            if k >= 2:
                since(act, ln_pool, L, 14, 7 + max(1, k - 2))
            act.activation(squares(L)[:, k % 2, :], d, ACT.Square).then_inc(ln_sq, 1)

        def squares(L):
            return sq0 if isinstance(L, int) and L == CH else sq

        def ln_var_add(g, L, k):
            since(g, ln_sq, L, 8, k + 1)
            if k > 1:
                since(g, ln_pool, L, 14, 7 + k - 1)
            t = squares(L)
            g.tensor_tensor(vacc[:, :], t[:, 0, :] if k == 1 else vacc[:, :], t[:, k % 2, :],
                            ALU.add).then_inc(ln_pool, 1)

        def ln_var_pool(g, L):
            for k in range(1, KB):
                ln_var_add(g, L, k)

        def ln_var_pe(pe, L):
            since(pe, ln_pool, L, 14, 14)
            since(pe, ln_d, L, 8, 8)
            pe.matmul(bank[LN_BANK][:, :], mean_w[:, :], vacc[:, :], start=True, stop=True).then_inc(ln_var, 1)

        def ln_std_act(act, L, last_scale):
            since(act, ln_var, L, 1, 1)
            last_scale(act)
            act.activation(rstd[:, :], bank[LN_BANK][:, :], ACT.Sqrt, bias=eps[:, 0:1]).then_inc(ln_std, 1)

        def ln_rstd_dve(v, L):
            since(v, ln_std, L, 1, 1)
            v.reciprocal(rstd[:, :], rstd[:, :]).then_inc(ln_rstd, 1)
            since(v, ln_rstd, L, 1, 1)

        def stat_sum_pool(g, L, k, blk):
            if k > 1:
                since(g, ln_pool, L, 14, k - 1)
            g.tensor_tensor(acc[:, :], blk(0) if k == 1 else acc[:, :], blk(k), ALU.add).then_inc(ln_pool, 1)

        def stat_copy_act(act, L, S):
            since(act, mean_st, S - 1, 16, 16)
            since(act, ln_d, L - 1, 8, 8)
            since(act, ln_mean, L, 1, 1)
            act.activation(mean_t[:, :], bank[LN_BANK][:, :], ACT.Copy).then_inc(st_copied, 1)

        def stat_center(e, L, S, k, src):
            if k == 0:
                since(e, st_copied, S, 1, 1)
            if k >= 2:
                since(e, ln_pool, L, 14, 7 + max(1, k - 2))
            e.tensor_tensor(sq[:, k % 2, :], src, mean_t[:, :], ALU.subtract).then_inc(ln_d, 1)

        def stat_square_act(act, L, k):
            since(act, ln_d, L, 8, k + 1)
            act.activation(sq[:, k % 2, :], sq[:, k % 2, :], ACT.Square).then_inc(ln_sq, 1)

        def stat_mean_pe(pe, L):
            since(pe, ln_pool, L, 14, 7)
            pe.matmul(bank[LN_BANK][:, :], mean_w[:, :], acc[:, :], start=True, stop=True).then_inc(ln_mean, 1)

        def stat_var_pe(pe, L, S, b=LN_BANK):
            since(pe, ln_pool, L, 14, 14)
            since(pe, st_copied, S, 1, 1)
            for t in range(TILES):
                tokens = vacc[:, :].rearrange("q (p t) -> q t p", t=TILES)[:, t, :]
                mm = pe.matmul(bank[b][:, t:t + 1], tokens, mean_w[:, 0:1],
                               start=True, stop=True)
            mm.then_inc(ln_var, 1)

        def stat_std_act(act, L, b=LN_BANK):
            since(act, ln_var, L, 1, 1)
            S = L - CH if isinstance(L, int) and L >= 2 * CH else L
            since(act, rstd_st, S - 1, 16, 16)
            act.activation(rstd4[:, :], bank[b][:, 0:TILES], ACT.Sqrt, bias=eps[:, 0:1]).then_inc(ln_std, 1)

        def stat_recip_dve(v, L):
            since(v, ln_std, L, 1, 1)
            v.reciprocal(rstd4[:, :], rstd4[:, :]).then_inc(ln_rstd, 1)

        block = ctx.enter_context(nc.Block())

        @block.sync
        def _(sp):
            for k in range(KB):
                unit_load(sp, U_PROJ + k)
                sp.dma_start(xs[:, k, :], x_t[k * P:(k + 1) * P, 0:N]).then_inc(a_ld[k], 16)
                if k == 3:
                    sp.dma_start(vec[:, :], vecs).then_inc(const_ld, 16)
                    sp.dma_start(rows[:, :], perm).then_inc(const_ld, 16)
            for k in range(KB):
                unit_load(sp, U_PROJ + KB + k)
            sp.wait_ge(zero_ok, 1)
            sp.dma_start(band_s.rearrange("(p n) -> p n", p=P), zero[:, :]).then_inc(band_zeroed, 16)

            for u in range(U_FF, U_FF + 4):
                unit_load(sp, u)

            def a_load(c):
                for k in range(KB):
                    sp.wait_ge(a_lo, (c - 1) * KB + k + 1)
                    sp.dma_start(xs[:, k, :], x_t[k * P:(k + 1) * P, c * N:(c + 1) * N]).then_inc(a_ld[k], 16)

            def stat_store(S, i):
                if i == 0:
                    sp.wait_ge(st_copied, S + 1)
                    sp.dma_start(stat_s[S, 0:1, :], mean_t[0:1, :]).then_inc(mean_st, 16)
                else:
                    sp.wait_ge(ln_rstd, S + 1 if S < CH else S + CH + 1)
                    sp.dma_start(stat_s[S, 1].rearrange("(p t) -> p t", t=TILES), rstd4[:, :]).then_inc(rstd_st, 16)

            def a_store(c, g):
                sp.wait_ge(a_ev, c * KB + 4 * g + 4)
                sp.dma_start(h0_s[c, :, g * 4 * N:(g + 1) * 4 * N],
                             ho[:, 4 * g:4 * g + 4, :]).then_inc(a_st[g], 16)

            def b_load(n):
                if n == 0:
                    sp.wait_ge(band_zeroed, 16)
                elif n == 1:
                    sp.wait_ge(a_mm, CH * KB)
                if n > 0:
                    sp.wait_ge(yr_hi, n * KB)
                for g in range(2):
                    sp.wait_ge(a_st[g], 16 * (n + 1))
                sp.wait_ge(mean_st, 16 * (n + 1))
                sp.wait_ge(rstd_st, 16 * (n + 1))
                dst = db0 if n == 0 else db
                sp.dma_start(dst[:, :, :], h0_s[n]).then_inc(b_ld, 16)
                sp.dma_start(mt[:, :], stat_s[n, 0].partition_broadcast(P)).then_inc(b_ld, 16)
                sp.dma_start(rt[:, :], stat_s[n, 1].partition_broadcast(P)).then_inc(b_ld, 16)

            def band_skew(n):
                sp.wait_ge(sm5, n * 7 + 7)
                sp.wait_ge(band_zeroed, 16)
                if n > 0:
                    sp.wait_ge(band_ld[0], 16 * n)
                    sp.wait_ge(band_ld[1], 16 * n)
                dst = band_s.rearrange("(u n) -> u n", u=UNITS)[:, 0:P * (P + 1)]
                dst = dst.rearrange("u (t n) -> t u n", t=P)[:, :, 0:TAPS]
                sp.dma_start(dst, wk5[:, :, :]).then_inc(skewed, 16)

            def band_load(n):
                sp.wait_ge(skewed, 16 * (n + 1))
                if n > 0:
                    sp.wait_ge(at_mm, n * KB)
                else:
                    sp.wait_ge(yr_hi, KB)
                src = band_s.rearrange("(u n) -> u n", u=UNITS)[:, TAPS - 1:TAPS - 1 + P * P]
                src = src.rearrange("u (p n) -> p u n", p=P)
                dst = band0 if n == 0 else band
                for i in range(2):
                    part = slice(i * UNITS // 2, (i + 1) * UNITS // 2)
                    sp.dma_start(dst[:, part, :], src[:, part, :]).then_inc(band_ld[i], 16)

            for c in range(CH):
                if c + 1 < CH:
                    a_load(c + 1)
                if c > 0:
                    stat_store(c - 1, 0)
                    if c < CH - 1:
                        stat_store(c - 1, 1)
                if c == CH - 2:
                    b_load(0)
                a_store(c, 0)
                if c == CH - 1:
                    band_skew(0)
                    band_load(0)
                    stat_store(c - 1, 1)
                a_store(c, 1)
            b_load(1)
            stat_store(CH - 1, 0)
            for u in range(U_FF + 4, U_V):
                unit_load(sp, u)
            stat_store(CH - 1, 1)

            def res_load(c, m):
                if 8 * c + m >= 2:
                    sp.wait_ge(ff_add, 8 * c + m - 1)
                sp.dma_start(res[:, m % 2, :], h0_s[c, :, m * N:(m + 1) * N]).then_inc(res_ld[m % 2], 16)

            def ff_store(c, m):
                sp.wait_ge(ff_add, 8 * c + m + 1)
                sp.dma_start(h1_s[c, :, m * N:(m + 1) * N], fo[m % 4][:, :]).then_inc(fo_st[m % 4], 16)

            def c_load(n):
                if n == 0:
                    sp.wait_ge(yr_hi, KB * CH)
                else:
                    sp.wait_ge(xc_lo, n * KB)
                for i in range(4):
                    sp.wait_ge(fo_st[i], 16 * 2 * (n + 1))
                sp.dma_start(dc[:, :, :], h1_s[n]).then_inc(c_ld, 16)

            for c in range(CH):
                res_load(c, 0)
                res_load(c, 1)
                if c + 2 < CH:
                    b_load(c + 2)
                if c == CH - 1:
                    for u in range(U_V, U_V + 4):
                        unit_load(sp, u)
                for m in range(KB):
                    if m == 2 and c + 1 < CH:
                        band_skew(c + 1)
                        band_load(c + 1)
                    ff_store(c, m)
                    if m == 5 and c == CH - 2:
                        sp.wait_ge(band_ld[1], 16 * CH)
                        c_load(0)
                    if m + 2 < KB:
                        res_load(c, m + 2)
            for u in range(U_V + 4, U_QK + 8):
                unit_load(sp, u)
            c_load(1)
            for u in range(U_QK + 8, U_O):
                unit_load(sp, u)

            def vs_load(c):
                if c == 0:
                    sp.wait_ge(xc_sc, 8 * CH)
                elif c == 1:
                    sp.wait_ge(qk_mm, 8 * CH)
                else:
                    sp.wait_ge(vs_lo, 4 * c)
                sp.wait_ge(vo_st, 16 * 4 * (c + 1))
                sp.dma_start((vs0 if c == 0 else vs)[:, :, :], vals_s[c]).then_inc(vs_ld, 16)

            def h2_load(c):
                if c == 0:
                    sp.wait_ge(qk_mm, 8 * CH)
                elif c == 1:
                    sp.wait_ge(pv_mm, 8 * CH)
                else:
                    sp.wait_ge(ln_d, 8 * (2 * CH + c - 1))
                for g in range(2):
                    if c >= 2:
                        sp.wait_ge(o_st[c % 2][g], 16 * (c // 2))
                    sp.dma_start(h2[c % 2][:, 4 * g:4 * g + 4, :], h1_s[c, :, g * 4 * N:(g + 1) * 4 * N])\
                      .then_inc(o_ld[c % 2][g], 16)

            def vo_store(c, m):
                sp.wait_ge(vo_ev, 8 * c + 2 * m + 2)
                sp.dma_start(vals_s[c, :, m * N:(m + 1) * N], vo[:, :]).then_inc(vo_st, 16)

            for c in range(CH):
                if c + 1 == CH:
                    for u in range(U_O, U_O + 4):
                        unit_load(sp, u)
                    vs_load(0)
                for m in range(PAIRS):
                    if m == PAIRS - 1 and c + 2 < CH:
                        c_load(c + 2)
                    vo_store(c, m)
                    if c + 1 == CH and m == 0:
                        for u in range(U_O + 4, U_DN):
                            unit_load(sp, u)
                    if c + 1 == CH and m == 1:
                            h2_load(0)
                            for u in range(U_DN, U_UP):
                                unit_load(sp, u)
            vs_load(1)
            h2_load(1)
            for u in range(U_UP, U_END):
                unit_load(sp, u)

            def d_stat_load(n):
                sp.wait_ge(mean_st, 16 * (CH + n + 1))
                sp.wait_ge(rstd_st, 16 * (CH + n + 1))
                if n > 0:
                    sp.wait_ge(xd_sc, 8 * n)
                sp.dma_start(mtd[:, :], stat_s[CH + n, 0].partition_broadcast(P)).then_inc(d_ld, 16)
                sp.dma_start(rtd[:, :], stat_s[CH + n, 1].partition_broadcast(P)).then_inc(d_ld, 16)

            for c in range(CH):
                if 1 <= c < CH - 1:
                    vs_load(c + 1)
                if c > 0:
                    stat_store(CH + c - 1, 0)
                for g in range(2):
                    sp.wait_ge(o_ev, 8 * c + 4 * g + 4)
                    sp.dma_start(h2_s[c][g * 4 * P:(g + 1) * 4 * P, :].rearrange("(k p) n -> p k n", p=P),
                                 h2[c % 2][:, 4 * g:4 * g + 4, :]).then_inc(o_st[c % 2][g], 16)
                if c > 0 and c + 1 < CH:
                    h2_load(c + 1)
                if c > 0:
                    stat_store(CH + c - 1, 1)
                if c == 1:
                    d_stat_load(0)
            d_stat_load(1)
            stat_store(2 * CH - 1, 0)
            stat_store(2 * CH - 1, 1)
            for n in range(2, CH):
                d_stat_load(n)
            sp.wait_ge(d_st, 16 * KB * CH)

        @block.gpsimd
        def _(g):
            for t, value in ((ident, 0.0), (mean_w, 1.0 / D), (eps, EPS), (valid, 1.0), (maskf, 1.0), (negs, OTHER), (fold, 0.0)):
                g.memset(t[:, :], value).then_inc(masks_ok, 1)
            g.wait_ge(masks_ok, 7)
            g.affine_select(out=ident[:, :], in_=ident[:, :], compare_op=ALU.not_equal, fill=1.0, base=0,
                            pattern=[[-1, P]], channel_multiplier=1).then_inc(masks_ok, 1)
            for s in range(P // SEQ):
                part = slice(s * SEQ, (s + 1) * SEQ)
                g.wait_ge(masks_ok, 8 + 3 * s)
                g.affine_select(out=valid[part, :], in_=valid[part, :], compare_op=ALU.is_ge, fill=0.0,
                                base=1 - TAPS, pattern=[[1, TAPS]], channel_multiplier=1).then_inc(masks_ok, 1)
                g.wait_ge(masks_ok, 9 + 3 * s)
                g.affine_select(out=maskf[part, part], in_=maskf[part, part], compare_op=ALU.is_gt, fill=0.0,
                                base=0, pattern=[[1, SEQ]], channel_multiplier=-1).then_inc(masks_ok, 1)
                g.wait_ge(masks_ok, 10 + 3 * s)
                g.memset(negs[part, part], MASKED).then_inc(masks_ok, 1)
            g.wait_ge(masks_ok, 14)
            g.tensor_copy(masked[:, :], maskf[:, :]).then_inc(masks_ok, 1)
            for part in range(2):
                g.wait_ge(masks_ok, 15 + part)
                g.affine_select(out=fold[:, :], in_=fold[:, :], compare_op=ALU.not_equal, fill=1.0,
                                base=-part * LOGITS, pattern=[[-1, LOGITS]], channel_multiplier=1).then_inc(masks_ok, 1)
            g.memset(zero[:, :], 0.0).then_inc(zero_ok, 1)

            def a_sum(c, ks):
                for k in ks:
                    since(g, a_ev, c, 8, k + 1)
                    stat_sum_pool(g, c, k, lambda i: ho[:, i, :])

            g.wait_ge(masks_ok, 17)
            a_sum(0, range(1, KB))
            with g.Fori(0, CH - 2) as c:
                ln_var_pool(g, c)
                a_sum(c + 1, range(1, KB))
            ln_var_pool(g, CH - 2)
            a_sum(CH - 1, range(1, KB))
            for k in range(1, KB):
                g.wait_ge(ln_sq, 8 * (CH - 1) + k + 1)
                g.wait_ge(ln_pool, 14 * (CH - 1) + 7 + k - 1)
                g.tensor_tensor(vacc[:, :], d3[:, 0, :] if k == 1 else vacc[:, :], d3[:, k, :],
                                ALU.add).then_inc(ln_pool, 1)
            g.wait_ge(at_mm, 8)
            for u in range(U_FF, U_V):
                unit_lo(g, u)

            def b_add(c, m):
                since(g, ff_ev, c, 8, m + 1)
                since(g, res_ld[m % 2], c, 64, 16 * (m // 2 + 1))
                g.tensor_tensor(fo[m % 4][:, :], fo[m % 4][:, :], res[:, m % 2, :], ALU.add).then_inc(ff_add, 1)

            def c_sum(n):
                since(g, c_ld, n, 16, 16)
                ln_sum_pool(g, n + CH, lambda k: dc[:, k, :])

            with g.Fori(0, CH - 2) as c:
                for m in range(KB):
                    b_add(c, m)
            for m in range(6):
                b_add(CH - 2, m)
            c_sum(0)
            for m in range(6, KB):
                b_add(CH - 2, m)
            ln_var_pool(g, CH)
            for m in range(KB):
                b_add(CH - 1, m)

            for u in range(U_V, U_O):
                if units[u][3] == "g":
                    unit_lo(g, u)
            with g.Fori(1, CH) as n:
                c_sum(n)
                ln_var_pool(g, n + CH)
                since(g, ln_rstd, n + CH, 1, 1)
                for k in range(KB):
                    g.tensor_tensor(dc[:, k, :], dc[:, k, :], rstd[:, :], ALU.mult).then_inc(xc_sc, 1)
            g.wait_ge(v_mm, 4 * CH)
            for u in range(U_O, U_DN):
                unit_lo(g, u)
            g.wait_ge(qk_mm, 8 * CH)
            g.memset(dn_h[:, :, :].bitcast(F32), 0.0).then_inc(dn_zero, 1)
            g.memset(dn_l[:, :, :].bitcast(F32), 0.0).then_inc(dn_zero, 1)
            g.wait_ge(dn_zero, 2)
            for u in range(U_DN, U_UP):
                unit_lo(g, u)

            def o_sum(c):
                for k in range(1, SUM_SPLIT):
                    g.wait_ge(o_ev, 8 * c + k + 1)
                    stat_sum_pool(g, 2 * CH + c, k, lambda i: h2[c % 2][:, i, :])

            def gather(n, ks=range(KB)):
                for half in range(2):
                    g.wait_ge(o_st[n % 2][half], 16 * (n // 2 + 1))
                if n == 1:
                    g.wait_ge(o_mm, 8 * CH)
                    g.wait_ge(g_ld, 16 * KB)
                if n >= 2:
                    g.wait_ge(d_st, 16 * KB * (n - 1))
                for k in ks:
                    g.indirect_dma_start(out=hg[:, hg_block(n) + k, :], out_offset=None, in_=h2_s[n],
                                         in_offset=bass.IndirectOffsetOnAxis(ap=rows[:, k:k + 1], axis=0))\
                     .then_inc(g_ld, 16)

            def scatter(c, k):
                g.wait_ge(d_ev, 8 * c + k + 1)
                g.indirect_dma_start(out=outs[c],
                                     out_offset=bass.IndirectOffsetOnAxis(ap=rows[:, k:k + 1], axis=0),
                                     in_=hg[:, hg_block(c) + k, :], in_offset=None).then_inc(d_st, 16)

            g.wait_ge(const_ld, 32)
            o_sum(0)
            for c in range(1, CH):
                if c == 2:
                    gather(0, range(4))
                if c == 3:
                    g.wait_ge(g_ld, 64)
                    gather(0, range(4, KB))
                ln_var_pool(g, 2 * CH + c - 1)
                o_sum(c)
                if c == 1:
                    for u in range(U_UP, U_END):
                        unit_lo(g, u)
            def d_scale(n, k):
                g.wait_ge(d_cent, 8 * n + k + 1)
                g.tensor_tensor(dd[:, k, :], dd[:, k, :], rtd[:, :], ALU.mult).then_inc(xd_sc, 1)

            gather(1)
            for c in range(CH):
                if c > 0 and c + 1 < CH:
                    gather(c + 1)
                for a in range(KB + 1):
                    if c == 0:
                        for k in STAT_AT.get(a, ()):
                            if k > 0:
                                ln_var_add(g, 3 * CH - 1, k)
                    if c + 1 < CH:
                        for k in XD_PREP.get(a, ()):
                            d_scale(c + 1, k)
                    if a > 0:
                        scatter(c, a - 1)
            g.wait_ge(d_st, 16 * KB * CH)

        @block.scalar
        def _(act):
            act.dma_start(wg_raw[:, :, :], w_gen.rearrange("(k p) n -> p k n", p=P)).then_inc(wg_ok, 16)

            def a_high(c, k):
                since(act, a_ld[k], c, 16, 16)
                released(act, c - 1, k, KB, a_used, a_mm)
                act.activation(xa_h[:, k, :], xs[:, k, :], ACT.Copy).then_inc(a_hi, 1)

            for k in range(KB):
                unit_hi(act, U_PROJ + k)
                a_high(0, k)
            for k in range(KB):
                unit_hi(act, U_PROJ + KB + k)
            act.wait_ge(wg_ok, 16)
            act.activation(wg[:, :, 0, :], wg_raw[:, :, :], ACT.Copy).then_inc(wg_ok, 1)

            def a_evac(c, ms):
                for m in ms:
                    since(act, a_st[m // 4], c, 16, 0)
                    since(act, ln_d, c - 1, 8, m + 1)
                    since(act, a_mm, c, 8, m + 1)
                    act.activation(ho[:, m, :], bank[m][:, :], ACT.Identity,
                                   bias=vec[:, B_PROJ + m:B_PROJ + m + 1]).then_inc(a_ev, 1)

            def a_step(c):
                if not (isinstance(c, int) and c == 0):
                    stat_copy_act(act, c - 1, c - 1)
                    for k in range(KB):
                        stat_square_act(act, c - 1, k)
                a_evac(c, A_GROUPS[0])
                if not (isinstance(c, int) and c == 0):
                    stat_std_act(act, c - 1)
                a_evac(c, A_GROUPS[1])
                for k in range(KB - 1):
                    a_high(c + 1, k)
                a_evac(c, A_GROUPS[2])
                a_high(c + 1, KB - 1)

            act.wait_ge(const_ld, 32)
            a_step(0)
            a_step(1)
            with act.Fori(2, CH - 1) as c:
                a_step(c)

            def y_base(n, k):
                since(act, y_scaled, n, 8, k + 1)
                if k == 0:
                    since(act, yt_mm, n - 1, 8, 8)
                src, dst = (db0, yb0) if isinstance(n, int) and n == 0 else (db, yb)
                act.activation(dst[:, k, :], src[:, k, :], ACT.Identity,
                               bias=vec[:, LN_B + k:LN_B + k + 1]).then_inc(y_b, 1)

            def y_high(n, k):
                since(act, yr_used, n, 8, k - 1)
                src = db0 if isinstance(n, int) and n == 0 else db
                act.activation(yr_h[:, k % 2, :], src[:, k, :], ACT.Identity,
                               bias=vec[:, LN_B + k:LN_B + k + 1]).then_inc(yr_hi, 1)

            def gate_logits(n):
                since(act, yr_used, n, 8, 8)
                since(act, lgt_mm, n - 1, 1, 1)
                act.activation(lg[:, :], bank[7][0:2 * LOGITS, :], ACT.Identity,
                               bias=vec[0:2 * LOGITS, B_GEN:B_GEN + 1]).then_inc(lg_ev, 1)

            def gate_exp(n):
                since(act, sm5, n, 7, 3)
                act.activation(lg5[:, :, :], lg5[:, :, :], ACT.Exp).then_inc(exp5, 1)

            def turn_evac(n, h):
                since(act, yt_mm, n, 8, h + 1)
                since(act, cv_mm, n, 8, h - 1)
                act.activation(yt_h[:, h % 2, :], bank[YT_BANK + h % 2][:, :], ACT.Copy).then_inc(yt_hi, 1)
                since(act, at_mm, n, 8, h + 1)
                act.activation(ar_h[:, h % 2, :], bank[AT_BANK + h % 2][:, :], ACT.Copy).then_inc(ar_hi, 1)

            def conv_high(n, h):
                since(act, cv_mm, n, 8, h + 1)
                act.activation(cv_h[:, h, :], bank[CV_BANK + h % 2][:, :], ACT.Copy).then_inc(cv_hi, 1)

            def ff_relu(c, m):
                since(act, ff_mm, c, 8, m + 1)
                since(act, fo_st[m % 4], c, 32, 16 * (m // 4))
                act.activation(fo[m % 4][:, :], bank[m][:, :], ACT.Relu,
                               bias=vec[:, B_FF + m:B_FF + m + 1]).then_inc(ff_ev, 1)

            LAST = CH - 1
            act.wait_ge(band_zeroed, 16)
            for k in range(4):
                y_base(0, k)
            y_high(0, 0)
            y_high(0, 1)
            stat_copy_act(act, LAST - 1, LAST - 1)
            for k in range(KB):
                stat_square_act(act, LAST - 1, k)
                if k + 4 < KB:
                    y_base(0, k + 4)
                if k >= 5:
                    y_high(0, k - 3)
            a_evac(LAST, A_GROUPS[0])
            for k in range(5, KB):
                y_high(0, k)
            gate_logits(0)
            a_evac(LAST, A_GROUPS[1])
            gate_exp(0)
            for u in range(U_FF, U_FF + 4):
                unit_hi(act, u)
            stat_std_act(act, LAST - 1, VAR_BANK)
            a_evac(LAST, A_GROUPS[2])
            stat_copy_act(act, LAST, LAST)
            for h in range(CONV_HEADS + 1):
                if h < CONV_HEADS:
                    turn_evac(0, h)
                if h > 0:
                    conv_high(0, h - 1)
                    act.wait_ge(ln_d, 8 * LAST + h)
                    act.activation(d3[:, h - 1, :], d3[:, h - 1, :], ACT.Square).then_inc(ln_sq, 1)
            act.wait_ge(a_st[1], 16 * CH)
            for u in range(U_FF + 4, U_FF + 8):
                unit_hi(act, u)
            stat_std_act(act, LAST)

            def c_squares(n):
                for k in range(KB):
                    ln_square_act(act, n + CH, k, dc[:, k, :])

            def c_std(n):
                if isinstance(n, int) and n == 0:
                    last = lambda e: None
                else:
                    last = lambda e: since(e, xc_sc, n - 1, 8, 8)
                ln_std_act(act, n + CH, last)

            def xc_high(n, k):
                since(act, xc_sc, n, 8, k + 1)
                released(act, n - 1, k, KB, xc_used, qk_mm)
                act.activation(xc_h[:, k, :], dc[:, k, :], ACT.Copy).then_inc(xc_hi, 1)

            def b_step(c, ahead):
                first = isinstance(c, int) and c == 0
                if first:
                    act.wait_ge(ln_pool, 14 * CH)
                for k in range(KB if ahead else 0):
                    y_base(c + 1, k)
                    y_high(c + 1, k)
                    if first:
                        unit_hi(act, U_FF + 8 + k)
                if ahead:
                    gate_logits(c + 1)
                else:
                    c_squares(0)
                ff_relu(c, 0)
                if first:
                    act.wait_ge(mean_st, 16 * CH)
                ff_relu(c, 1)
                if ahead:
                    gate_exp(c + 1)
                ff_relu(c, 2)
                if not ahead:
                    c_std(0)
                    for k in range(KB):
                        xc_high(0, k)
                for m in range(3, 6):
                    ff_relu(c, m)
                for h in range(CONV_HEADS + 1):
                    if ahead and h < CONV_HEADS:
                        turn_evac(c + 1, h)
                    if h == CONV_HEADS:
                        ff_relu(c, 6)
                    if ahead and h > 0:
                        conv_high(c + 1, h - 1)
                ff_relu(c, 7)

            chunks(act, 0, CH - 1, lambda c: b_step(c, True))
            b_step(CH - 1, False)

            def c_softmax_exp(c, m):
                for j in range(2):
                    since(act, s_sub, c, 8, 2 * m + j + 1)
                    act.activation(pr[:, j, :], pr[:, j, :], ACT.Exp).then_inc(s_exp, 1)

            def c_qk(c, m):
                for i, b0 in ((0, B_Q), (1, B_K)):
                    since(act, qk_mm, c, 8, 2 * m + i + 1)
                    if i == 0:
                        since(act, s_mm, c, 8, 2 * m)
                    act.activation(qk_h[:, i, :], bank[i][:, :], ACT.Identity,
                                   bias=vec[:, b0 + m:b0 + m + 1]).then_inc(qk_hi, 1)

            def c_pt(c, m, banks=PT_BANK):
                for j in range(2):
                    since(act, pt_mm, c, 8, 2 * m + j + 1)
                    since(act, pv_mm, c, 8, 2 * m + j - 1)
                    act.activation(pt_h[:, j, :], bank[banks[j]][:, :], ACT.Copy).then_inc(pt_hi, 1)

            def c_vals(c, m):
                for j in range(2):
                    rowsj = slice(HEAD * j, HEAD * j + HEAD)
                    since(act, pv_mm, c, 8, 2 * m + j + 1)
                    if j == 0:
                        since(act, vo_st, c, 64, 16 * m)
                    act.activation(vo[rowsj, :], bank[7][rowsj, :], ACT.Identity,
                                   bias=vec[rowsj, B_V + m:B_V + m + 1]).then_inc(vo_ev, 1)

            for u in range(U_V, U_V + 16):
                unit_hi(act, u)

            def c_values(c, ts):
                for t in ts:
                    since(act, v_mm, c, 4, t + 1)
                    since(act, pv_mm, c - 1, 8, 8)
                    act.activation(v_h[:, t, :], bank[t][:, :], ACT.Copy).then_inc(v_hi, 1)

            def vs_high(c, ks):
                for k in ks:
                    since(act, vs_ld, c, 16, 16)
                    released(act, c - 1, k, PAIRS, vs_used, o_mm)
                    src = vs0 if c == 0 else vs
                    act.activation(vs_h[:, k, :], src[:, k, :], ACT.Copy).then_inc(vs_hi, 1)

            c_values(0, range(TILES))
            for u in range(U_V + 16, U_O):
                unit_hi(act, u)
            c_qk(0, 0)

            def c_step(c, ahead):
                later = not (isinstance(c, int) and c == 0)
                c_softmax_exp(c, 0)
                if later:
                    c_vals(c - 1, PAIRS - 1)
                    c_values(c, range(TILES))
                if ahead and later:
                    c_squares(c + 1)
                c_qk(c, 1)
                c_pt(c, 0)
                if ahead and not later:
                    c_squares(c + 1)
                c_softmax_exp(c, 1)
                if not ahead:
                    for u in range(U_O, U_O + 4):
                        unit_hi(act, u)
                    vs_high(0, range(PAIRS))
                if ahead:
                    c_std(c + 1)
                c_qk(c, 2)
                c_vals(c, 0)
                c_pt(c, 1)
                c_softmax_exp(c, 2)
                if ahead:
                    for k in range(KB):
                        xc_high(c + 1, k)
                c_qk(c, 3)
                c_vals(c, 1)
                if not ahead:
                    for u in range(U_O + 4, U_DN):
                        unit_hi(act, u)
                c_pt(c, 2, PT_BANK if ahead else PT_LAST[0])
                c_softmax_exp(c, 3)
                if ahead:
                    c_qk(c + 1, 0)
                c_vals(c, 2)
                if not ahead:
                    act.wait_ge(dn_zero, 2)
                    for u in range(U_DN, U_UP):
                        unit_hi(act, u)
                c_pt(c, 3, PT_BANK if ahead else PT_LAST[1])
                if not ahead:
                    c_vals(c, 3)

            chunks(act, 0, CH - 1, lambda c: c_step(c, True))
            c_step(CH - 1, False)

            def xd_high(n, k):
                since(act, xd_sc, n, 8, k + 1)
                since(act, up_mm, n - 1, 32, 4 * k + 4)
                act.activation(xd_h[:, k, :], dd[:, k, :], ACT.Copy).then_inc(xd_hi, 1)

            for c in range(CH):
                if c > 0:
                    L = 2 * CH + c - 1
                    if c == 1:
                        act.wait_ge(vo_st, 64 * CH)
                    stat_copy_act(act, L, CH + c - 1)
                    for k in range(KB):
                        stat_square_act(act, L, k)
                if c + 1 < CH:
                    vs_high(c + 1, range(PAIRS - 1))
                else:
                    for half in range(2):
                        act.wait_ge(o_st[0][half], 16 * (CH // 2))
                    xd_high(0, 0)
                    xd_high(0, 1)
                if c > 0:
                    stat_std_act(act, L, VAR_BANK)
                if c + 1 < CH:
                    vs_high(c + 1, [PAIRS - 1])
                if c == 1:
                    for u in range(U_UP, U_END):
                        unit_hi(act, u)

            def gelus(c, a):
                for i in range(FFB):
                    since(act, up_mm, c, 32, 4 * a + i + 1)
                    since(act, g_lo, c, 32, 4 * a + i - 3)
                    act.activation(gt[:, i, :], bank[i][:, :], ACT.Gelu).then_inc(gelu_ok, 1)
                    since(act, gelu_ok, c, 32, 4 * a + i + 1)
                    since(act, g_used, c, 32, 4 * a + i - 3)
                    act.activation(g_h[:, i, :], gt[:, i, :], ACT.Copy).then_inc(g_hi, 1)

            def d_step(c, ahead):
                first = isinstance(c, int) and c == 0
                for a in range(KB):
                    gelus(c, a)
                    if first:
                        if a == 2:
                            stat_copy_act(act, 3 * CH - 1, 2 * CH - 1)
                        for k in STAT_AT.get(a - 1, ()):
                            stat_square_act(act, 3 * CH - 1, k)
                        for k in XD_FIRST.get(a, ()):
                            xd_high(0, k)
                if first:
                    for k in STAT_AT[KB - 1]:
                        stat_square_act(act, 3 * CH - 1, k)
                    stat_std_act(act, 3 * CH - 1)

            chunks(act, 0, CH - 1, lambda c: d_step(c, True))
            d_step(CH - 1, False)

        @block.vector
        def _(v):
            def a_low(c, k):
                since(v, a_hi, c, 8, k + 1)
                v.tensor_tensor(xa_l[:, k, :], xs[:, k, :], xa_h[:, k, :].bitcast(F32),
                                ALU.subtract).then_inc(a_lo, 1)

            for k in range(KB):
                unit_lo(v, U_PROJ + k)
                a_low(0, k)
            for k in range(KB):
                unit_lo(v, U_PROJ + KB + k)
            v.wait_ge(wg_ok, 17)
            v.tensor_tensor(wg[:, :, 1, :], wg_raw[:, :, :], wg[:, :, 0, :].bitcast(F32), ALU.subtract).then_inc(wg_ok, 1)
            def a_stats(c):
                for k in range(KB):
                    stat_center(v, c, c, k, ho[:, k, :])
                stat_recip_dve(v, c)

            for k in range(KB):
                a_low(1, k)
            with v.Fori(0, CH - 2) as c:
                a_stats(c)
                for k in range(KB):
                    a_low(c + 2, k)

            def y_center(n, k):
                if k == 0:
                    since(v, b_ld, n, 48, 48)
                t = db0 if isinstance(n, int) and n == 0 else db
                v.tensor_tensor(t[:, k, :], t[:, k, :], mt[:, :], ALU.subtract).then_inc(y_cent, 1)

            def y_scale(n, k):
                since(v, y_cent, n, 8, k + 1)
                t = db0 if isinstance(n, int) and n == 0 else db
                v.scalar_tensor_tensor(out=t[:, k, :], in0=t[:, k, :], scalar=vec[:, LN_G + k:LN_G + k + 1],
                                       in1=rt[:, :], op0=ALU.mult, op1=ALU.mult).then_inc(y_scaled, 1)

            def y_prep(n, ks=range(KB)):
                for k in ks:
                    y_center(n, k)
                for k in ks:
                    y_scale(n, k)

            def y_low(n, k):
                since(v, y_b, n, 8, k + 1)
                since(v, yr_hi, n, 8, k + 1)
                src = yb0 if isinstance(n, int) and n == 0 else yb
                v.tensor_tensor(yr_l[:, k % 2, :], src[:, k, :], yr_h[:, k % 2, :].bitcast(F32),
                                ALU.subtract).then_inc(yr_lo, 1)

            def gates(n):
                since(v, lgt_mm, n, 1, 1)
                since(v, skewed, n - 1, 16, 16)
                per = [P, UNITS, TAPS]
                v.tensor_copy(lg5[:, :, :].rearrange("p (h t) k -> p t h k", t=TILES),
                              bank[gate_turn_bank(n)][:, 0:TILES * LOGITS]
                              .rearrange("p (t h k) -> p t h k", t=TILES, h=CONV_HEADS)).then_inc(sm5, 1)
                since(v, sm5, n, 7, 1)
                v.tensor_reduce(mx5[:, :], lg5[:, :, :], AX.X, ALU.max).then_inc(sm5, 1)
                since(v, sm5, n, 7, 2)
                v.tensor_tensor(lg5[:, :, :], lg5[:, :, :], mx5[:, :].unsqueeze(2).to_broadcast(per),
                                ALU.subtract).then_inc(sm5, 1)
                since(v, exp5, n, 1, 1)
                v.tensor_reduce(su5[:, :], lg5[:, :, :], AX.X, ALU.add).then_inc(sm5, 1)
                since(v, sm5, n, 7, 4)
                v.reciprocal(su5[:, :], su5[:, :]).then_inc(sm5, 1)
                v.tensor_tensor(wk5[:, :, :], lg5[:, :, :], valid[:, :].unsqueeze(1).to_broadcast(per),
                                ALU.mult).then_inc(sm5, 1)
                since(v, sm5, n, 7, 6)
                v.tensor_tensor(wk5[:, :, :], wk5[:, :, :], su5[:, :].unsqueeze(2).to_broadcast(per),
                                ALU.mult).then_inc(sm5, 1)

            def turn_low(n, h):
                since(v, yt_hi, n, 8, h + 1)
                v.tensor_tensor(yt_l[:, h % 2, :], bank[YT_BANK + h % 2][:, :],
                                yt_h[:, h % 2, :].bitcast(F32), ALU.subtract).then_inc(yt_lo, 1)
                since(v, ar_hi, n, 8, h + 1)
                v.tensor_tensor(ar_l[:, h % 2, :], bank[AT_BANK + h % 2][:, :],
                                ar_h[:, h % 2, :].bitcast(F32), ALU.subtract).then_inc(ar_lo, 1)

            def conv_low(n, h):
                since(v, cv_hi, n, 8, h + 1)
                v.tensor_tensor(cv_l[:, h, :], bank[CV_BANK + h % 2][:, :],
                                cv_h[:, h, :].bitcast(F32), ALU.subtract).then_inc(cv_lo, 1)

            v.wait_ge(masks_ok, 17)
            LAST = CH - 1
            y_prep(0, range(4))
            y_low(0, 0)
            y_low(0, 1)
            for k in range(KB):
                stat_center(v, LAST - 1, LAST - 1, k, ho[:, k, :])
                if k + 4 < KB:
                    y_prep(0, [k + 4])
            for k in range(2, KB):
                y_low(0, k)
            gates(0)
            stat_recip_dve(v, LAST - 1)
            v.wait_ge(st_copied, CH)
            v.wait_ge(a_mm, 8 * CH)

            def center_last(k):
                v.tensor_tensor(d3[:, k, :], ho[:, k, :], mean_t[:, :], ALU.subtract).then_inc(ln_d, 1)

            center_last(0)
            center_last(1)
            for h in range(CONV_HEADS + 1):
                if h < CONV_HEADS:
                    turn_low(0, h)
                if h + 2 < KB:
                    center_last(h + 2)
                if h > 0:
                    conv_low(0, h - 1)
            y_prep(1)
            stat_recip_dve(v, LAST)

            def b_step(c, ahead):
                for k in range(KB):
                    y_low(c + 1, k)
                gates(c + 1)
                if ahead:
                    y_prep(c + 2)
                for h in range(CONV_HEADS + 1):
                    if h < CONV_HEADS:
                        turn_low(c + 1, h)
                    if h > 0:
                        conv_low(c + 1, h - 1)

            chunks(v, 0, CH - 2, lambda c: b_step(c, True))
            b_step(CH - 2, False)

            def c_center(n):
                for k in range(KB):
                    ln_center_dve(v, n + CH, k, dc[:, k, :], dc[:, k, :])

            def c_scale_first():
                ln_rstd_dve(v, CH)
                v.wait_ge(ln_sq, 8 * CH + 8)
                for k in range(KB):
                    v.tensor_tensor(dc[:, k, :], dc[:, k, :], rstd[:, :], ALU.mult).then_inc(xc_sc, 1)

            def xc_low(n, k):
                since(v, xc_hi, n, 8, k + 1)
                since(v, xc_sc, n, 8, k + 1)
                v.tensor_tensor(xc_l[:, k, :], dc[:, k, :], xc_h[:, k, :].bitcast(F32),
                                ALU.subtract).then_inc(xc_lo, 1)

            def c_qk(c, m):
                for i, b0 in ((0, B_Q), (1, B_K)):
                    since(v, qk_hi, c, 8, 2 * m + i + 1)
                    v.scalar_tensor_tensor(out=qk_l[:, i, :], in0=bank[i][:, :],
                                           scalar=vec[:, b0 + m:b0 + m + 1], in1=qk_h[:, i, :].bitcast(F32),
                                           op0=ALU.add, op1=ALU.subtract).then_inc(qk_lo, 1)

            def c_softmax_in(c, m):
                for j in range(2):
                    i = 2 * m + j + 1
                    S = bank[4 + j]
                    view = S[:, :].rearrange("p (t n) -> p t n", t=TILES)
                    since(v, s_mm, c, 8, i)
                    v.memset(smax[:, j, :], 0.0)
                    v.copy_predicated(view, masked[:, :].unsqueeze(1).to_broadcast([P, TILES, P]),
                                      negs[:, :].unsqueeze(1).to_broadcast([P, TILES, P])).then_inc(s_masked, 1)
                    since(v, s_masked, c, 8, i)
                    v.tensor_reduce(smax[:, j, :], view, AX.X, ALU.max).then_inc(s_max, 1)
                    since(v, s_max, c, 8, i)
                    since(v, pt_mm, c, 8, i - 2)
                    v.tensor_tensor(pr[:, j, :].rearrange("p (t n) -> p t n", t=TILES), view,
                                    smax[:, j, :].unsqueeze(2).to_broadcast([P, TILES, P]),
                                    ALU.subtract).then_inc(s_sub, 1)

            def c_softmax_out(c, m):
                for j in range(2):
                    i = 2 * m + j + 1
                    view = pr[:, j, :].rearrange("p (t n) -> p t n", t=TILES)
                    since(v, s_exp, c, 8, i)
                    v.tensor_reduce(ssum[:, j, :], view, AX.X, ALU.add).then_inc(s_sum, 1)
                    since(v, s_sum, c, 8, i)
                    v.reciprocal(ssum[:, j, :], ssum[:, j, :]).then_inc(s_rec, 1)
                    since(v, s_rec, c, 8, i)
                    v.tensor_tensor(view, view, ssum[:, j, :].unsqueeze(2).to_broadcast([P, TILES, P]),
                                    ALU.mult).then_inc(s_norm, 1)

            def c_pt(c, m, banks=PT_BANK):
                for j in range(2):
                    since(v, pt_hi, c, 8, 2 * m + j + 1)
                    v.tensor_tensor(pt_l[:, j, :], bank[banks[j]][:, :], pt_h[:, j, :].bitcast(F32),
                                    ALU.subtract).then_inc(pt_lo, 1)

            c_center(0)
            c_scale_first()
            for k in range(KB):
                xc_low(0, k)
            for u in range(U_V, U_V + 16):
                if units[u][3] == "v":
                    unit_lo(v, u)

            def c_values(c, ts):
                for t in ts:
                    since(v, v_hi, c, 4, t + 1)
                    v.tensor_tensor(v_l[:, t, :], bank[t][:, :], v_h[:, t, :].bitcast(F32),
                                    ALU.subtract).then_inc(v_lo, 1)

            c_values(0, range(TILES))
            for u in range(U_V + 16, U_O):
                if units[u][3] == "v":
                    unit_lo(v, u)
            c_qk(0, 0)

            def o_low(c, ks):
                for k in ks:
                    since(v, vs_hi, c, 4, k + 1)
                    src = vs0 if c == 0 else vs
                    v.tensor_tensor(vs_l[:, k, :], src[:, k, :], vs_h[:, k, :].bitcast(F32),
                                    ALU.subtract).then_inc(vs_lo, 1)

            def c_step(c, ahead):
                later = not (isinstance(c, int) and c == 0)
                c_softmax_in(c, 0)
                c_softmax_out(c, 0)
                if later:
                    c_values(c, range(TILES))
                if ahead:
                    c_center(c + 1)
                c_qk(c, 1)
                c_pt(c, 0)
                c_softmax_in(c, 1)
                c_softmax_out(c, 1)
                if ahead:
                    since(v, ln_std, c + 1 + CH, 1, 1)
                    v.reciprocal(rstd[:, :], rstd[:, :]).then_inc(ln_rstd, 1)
                else:
                    o_low(0, range(PAIRS))
                c_qk(c, 2)
                c_pt(c, 1)
                c_softmax_in(c, 2)
                c_softmax_out(c, 2)
                if ahead:
                    for k in range(KB):
                        xc_low(c + 1, k)
                c_qk(c, 3)
                c_pt(c, 2, PT_BANK if ahead else PT_LAST[0])
                c_softmax_in(c, 3)
                c_softmax_out(c, 3)
                if ahead:
                    c_qk(c + 1, 0)
                c_pt(c, 3, PT_BANK if ahead else PT_LAST[1])

            chunks(v, 0, CH - 1, lambda c: c_step(c, True))
            c_step(CH - 1, False)

            def o_evac(c, ms):
                for m in ms:
                    v.wait_ge(o_ld[c % 2][m // 4], 16 * (c // 2 + 1))
                    v.wait_ge(o_mm, 8 * c + m + 1)
                    v.scalar_tensor_tensor(out=h2[c % 2][:, m, :], in0=bank[m][:, :],
                                           scalar=vec[:, B_O + m:B_O + m + 1], in1=h2[c % 2][:, m, :],
                                           op0=ALU.add, op1=ALU.add).then_inc(o_ev, 1)

            def o_sum(c):
                for m in range(SUM_SPLIT, KB):
                    v.wait_ge(o_ev, 8 * c + m + 1)
                    v.wait_ge(ln_pool, 14 * (2 * CH + c) + m - 1)
                    v.tensor_tensor(acc[:, :], acc[:, :], h2[c % 2][:, m, :], ALU.add).then_inc(ln_pool, 1)

            def o_center(c, ks):
                for k in ks:
                    stat_center(v, 2 * CH + c, CH + c, k, h2[c % 2][:, k, :])

            def d_prep(n, ks):
                for k in ks:
                    if k == 0 and isinstance(n, int) and n == 0:
                        v.wait_ge(g_ld, 64)
                        v.wait_ge(d_ld, 32)
                    elif k == 0:
                        since(v, g_ld, n, 16 * KB, 16 * KB)
                        since(v, d_ld, n, 32, 32)
                    elif k == 4 and isinstance(n, int) and n == 0:
                        v.wait_ge(g_ld, 128)
                    since(v, xd_lo, n - 1, 8, k + 1)
                    since(v, xd_hi, n - 1, 8, k + 1)
                    if isinstance(n, int):
                        dst, src, mean = dd[:, k, :], hg[:, hg_block(n) + k, :], mtd[:, :]
                    else:
                        dst, src, mean = dd[:, k:k + 1, :], hg[:, bass.ds(hg_block(n) + k, 1), :], mtd[:, :].unsqueeze(1)
                    v.tensor_tensor(dst, src, mean, ALU.subtract).then_inc(d_cent, 1)
                for k in ks if isinstance(n, int) and n == 0 else ():
                    v.wait_ge(d_cent, k + 1)
                    v.tensor_tensor(dd[:, k, :], dd[:, k, :], rtd[:, :], ALU.mult).then_inc(xd_sc, 1)

            def xd_low(n, k):
                since(v, xd_sc, n, 8, k + 1)
                since(v, xd_hi, n, 8, k + 1)
                v.tensor_tensor(xd_l[:, k, :], dd[:, k, :], xd_h[:, k, :].bitcast(F32),
                                ALU.subtract).then_inc(xd_lo, 1)

            for c in range(CH):
                if c > 0:
                    o_center(c - 1, range(4))
                o_evac(c, A_GROUPS[0])
                for k in range(4, KB) if c > 0 else ():
                    o_center(c - 1, [k])
                    if c == CH - 1:
                        d_prep(0, [k - 4])
                o_evac(c, A_GROUPS[1])
                if c + 1 < CH:
                    o_low(c + 1, range(PAIRS - 1))
                if c == CH - 1:
                    xd_low(0, 0)
                    xd_low(0, 1)
                o_evac(c, A_GROUPS[2])
                if c + 1 < CH:
                    o_low(c + 1, [PAIRS - 1])
                o_sum(c)
                if 0 < c < CH - 1:
                    stat_recip_dve(v, 2 * CH + c - 1)

            def d_add(c, a):
                since(v, g_used, c, 32, 4 * a + 4)
                if isinstance(c, int):
                    dst, src = hg[:, hg_block(c) + a, :], bank[4 + a % 2][:, :]
                else:
                    dst, src = hg[:, bass.ds(hg_block(c) + a, 1), :], bank[4 + a % 2][:, :].unsqueeze(1)
                v.tensor_tensor(dst, src, dst, ALU.add).then_inc(d_ev, 1)

            def d_step(c, ahead):
                first = isinstance(c, int) and c == 0
                for a in range(KB):
                    for i in range(FFB):
                        since(v, g_hi, c, 32, 4 * a + i + 1)
                        v.tensor_tensor(g_l[:, i, :], gt[:, i, :], g_h[:, i, :].bitcast(F32),
                                        ALU.subtract).then_inc(g_lo, 1)
                    if a >= 1:
                        d_add(c, a - 1)
                    elif not first:
                        d_add(c - 1, KB - 1)
                    if first:
                        o_center(CH - 1, STAT_AT.get(a, ()))
                        for k in XD_FIRST.get(a, ()):
                            xd_low(0, k)
                        d_prep(0, [k + 2 for k in XD_FIRST.get(a, ()) if k + 2 < KB])
                        if a == 0:
                            stat_recip_dve(v, 3 * CH - 2)
                    if ahead:
                        d_prep(c + 1, XD_PREP.get(a, ()))
                        for k in XD_SPLIT.get(a, ()):
                            since(v, xd_sc, c + 1, 8, k + 1)
                            since(v, up_mm, c, 32, 4 * k + 4)
                            v.tensor_copy(xd_h[:, k, :], dd[:, k, :]).then_inc(xd_hi, 1)
                            xd_low(c + 1, k)
                if first:
                    stat_recip_dve(v, 3 * CH - 1)

            chunks(v, 0, CH - 1, lambda c: d_step(c, True))
            d_step(CH - 1, False)
            d_add(CH - 1, KB - 1)

        @block.tensor
        def _(pe):
            def a_group(c, g, k):
                ms = A_GROUPS[g]
                if k == 0:
                    since(pe, a_ev, c - 1, 8, ms[-1] + 1)
                    if g == 2 and isinstance(c, int) and c == CH - 1:
                        pe.wait_ge(st_copied, c)
                    elif g == 2:
                        since(pe, ln_std, c - 1, 1, 1)
                if g == 0:
                    since(pe, a_lo, c, 8, k + 1)
                if isinstance(c, int) and c == 0 and g < 2:
                    wait_units(pe, U_PROJ + KB * g + k + 1)
                for m in ms:
                    cols = slice(m * P, (m + 1) * P)
                    mm = split3(pe, bank[m][:, :], (wp_h[:, k, cols], wp_l[:, k, cols]),
                                (xa_h[:, k, :], xa_l[:, k, :]), k == 0, k == KB - 1)
                    if k == KB - 1:
                        mm.then_inc(a_mm, 1)
                if g == 2 and k < KB - 1:
                    mm.then_inc(a_used, 1)

            def a_step(c):
                later = not (isinstance(c, int) and c == 0)
                for g in range(3):
                    for k in range(KB):
                        a_group(c, g, k)
                        if later and (g, k) == (0, 2):
                            if isinstance(c, int):
                                pe.wait_ge(masks_ok, 17)
                            since(pe, a_ev, c - 1, 8, 8)
                            stat_mean_pe(pe, c - 1)
                        if later and (g, k) == (1, 1):
                            stat_var_pe(pe, c - 1, c - 1)

            a_step(0)
            a_step(1)
            with pe.Fori(2, CH - 1) as c:
                a_step(c)

            def gate_block(n, k):
                since(pe, yr_lo, n, 8, k + 1)
                if k == 0:
                    if isinstance(n, int) and n < 2:
                        pe.wait_ge(a_ev, 8 * (CH - 1 + n))
                    else:
                        since(pe, ff_ev, n - 2, 8, 8)
                for whole in (True, False) if k == 0 else (False, True):
                    if whole:
                        mm = pe.matmul(bank[7][0:2 * LOGITS, :], wg[:, k, :, :], yr_h[:, k % 2, :],
                                       start=k == 0, stop=k == KB - 1)
                    else:
                        mm = pe.matmul(bank[7][0:LOGITS, :], wg[:, k, 0, :], yr_l[:, k % 2, :],
                                       start=False, stop=False)
                mm.then_inc(yr_used, 1)

            def gate_turn(n):
                for t in range(TILES):
                    mm = pe.matmul(bank[gate_turn_bank(n)][:, t * LOGITS:(t + 1) * LOGITS],
                                   lg[:, t * P:(t + 1) * P], fold[0:2 * LOGITS, :], start=True, stop=True)
                mm.then_inc(lgt_mm, 1)

            def turn(n, h):
                first = isinstance(n, int) and n == 0
                if h == 0:
                    since(pe, y_b, n, 8, 8)
                    if first:
                        pe.wait_ge(sm5, 1)
                if h == 1 and first:
                    pe.wait_ge(ln_std, CH - 1)
                if h < 2 and not first:
                    since(pe, ff_ev, n - 1, 8, 3 + h)
                if h >= 2:
                    since(pe, yt_lo, n, 8, h - 1)
                y, b = (yb0, band0) if first else (yb, band)
                for t in range(TILES):
                    mm = pe.transpose(bank[YT_BANK + h % 2][:, t * P:(t + 1) * P], y[:, h, t * P:(t + 1) * P],
                                      ident[:, :])
                mm.then_inc(yt_mm, 1)
                if h % 4 == 0:
                    since(pe, band_ld[h // 4], n, 16, 16)
                if h >= 2:
                    since(pe, ar_lo, n, 8, h - 1)
                for t in range(TILES):
                    mm = pe.transpose(bank[AT_BANK + h % 2][:, t * P:(t + 1) * P], b[:, h * TILES + t, :],
                                      ident[:, :])
                mm.then_inc(at_mm, 1)

            def conv(n, h):
                if h < 2:
                    since(pe, ff_ev, n - 1, 8, 5 + h)
                if h >= 2:
                    since(pe, cv_lo, n, 8, h - 1)
                since(pe, yt_lo, n, 8, h + 1)
                since(pe, ar_lo, n, 8, h + 1)
                for t in range(TILES):
                    cols = slice(t * P, (t + 1) * P)
                    mm = split3(pe, bank[CV_BANK + h % 2][:, cols], (yt_h[:, h % 2, cols], yt_l[:, h % 2, cols]),
                                (ar_h[:, h % 2, cols], ar_l[:, h % 2, cols]), True, True)
                mm.then_inc(cv_mm, 1)

            def ff_group(c, g, k):
                ms = A_GROUPS[g]
                if g == 0:
                    since(pe, cv_lo, c, 8, k + 1)
                if isinstance(c, int) and c == 0 and g < 2:
                    wait_units(pe, U_FF + KB * g + k + 1)
                for m in ms:
                    cols = slice(m * P, (m + 1) * P)
                    mm = split3(pe, bank[m][:, :], (wf_h[:, k, cols], wf_l[:, k, cols]),
                                (cv_h[:, k, :], cv_l[:, k, :]), k == 0, k == KB - 1)
                    if k == KB - 1:
                        mm.then_inc(ff_mm, 1)

            def b_step(c, ahead):
                first = isinstance(c, int) and c == 0
                gates = GATES_AT[first]
                for i in range(2 * KB):
                    if not ahead and i == 1:
                        pe.wait_ge(ff_ev, 8 * (CH - 1))
                        ln_mean_pe(pe, CH)
                    if not ahead and i == 9:
                        ln_var_pe(pe, CH)
                    if ahead and i == TURN_AFTER[first]:
                        since(pe, lg_ev, c + 1, 1, 1)
                    ff_group(c, i // KB, i % KB)
                    if ahead:
                        for j in gates.get(i, ()):
                            gate_block(c + 1, j)
                    if ahead and i == TURN_AFTER[first]:
                        gate_turn(c + 1)
                if ahead:
                    turn(c + 1, 0)
                    since(pe, sm5, c + 1, 7, 1)
                if isinstance(c, int) and c == 0:
                    pe.wait_ge(ln_std, CH)
                elif ahead:
                    since(pe, ff_ev, c - 1, 8, 8)
                else:
                    pe.wait_ge(ln_std, CH + 1)
                for k in range(KB):
                    ff_group(c, 2, k)
                    if ahead:
                        if k + 1 < KB:
                            turn(c + 1, k + 1)
                        conv(c + 1, k)

            pe.wait_ge(wg_ok, 18)
            LAST = CH - 1
            for k in range(KB):
                a_group(LAST, 0, k)
                if k == 2:
                    pe.wait_ge(a_ev, 8 * LAST)
                    stat_mean_pe(pe, LAST - 1)
            for k in range(KB):
                a_group(LAST, 1, k)
                gate_block(0, k)
            pe.wait_ge(lg_ev, 1)
            for k in range(KB):
                a_group(LAST, 2, k)
                if k == 0:
                    pe.wait_ge(a_ev, 8 * LAST + 1)
                    gate_turn(0)
                if k == 4:
                    pe.wait_ge(a_ev, 8 * LAST + VAR_BANK + 1)
                    stat_var_pe(pe, LAST - 1, LAST - 1, VAR_BANK)
            pe.wait_ge(a_ev, 8 * CH)
            stat_mean_pe(pe, LAST)
            turn(0, 0)
            for h in range(CONV_HEADS):
                if h + 1 < CONV_HEADS:
                    turn(0, h + 1)
                conv(0, h)
            stat_var_pe(pe, LAST, LAST)

            chunks(pe, 0, CH - 1, lambda c: b_step(c, True))
            b_step(CH - 1, False)

            def c_values(c, ts, beside=None):
                if isinstance(c, int) and c == 0:
                    pe.wait_ge(ff_ev, 8 * CH)
                elif 2 in ts:
                    since(pe, pt_lo, c - 1, 8, 8)
                else:
                    since(pe, qk_lo, c, 8, 2)
                for k in range(KB):
                    since(pe, xc_lo, c, 8, k + 1)
                    if isinstance(c, int) and c == 0:
                        wait_units(pe, U_V + k + 1)
                    if beside and k == 4:
                        beside()
                    for t in ts:
                        cols = slice(t * P, (t + 1) * P)
                        mm = split3(pe, bank[t][:, :], (xc_h[:, k, cols], xc_l[:, k, cols]),
                                    (wv_h[:, k, :], wv_l[:, k, :]), k == 0, k == KB - 1)
                        if k == KB - 1:
                            mm.then_inc(v_mm, 1)

            def c_qk(c, m, beside=None):
                first = isinstance(c, int) and c == 0
                if m == 1 or (m == 0 and first):
                    since(pe, v_lo, c, 4, 2)
                elif m == 0:
                    since(pe, qk_lo, c - 1, 8, 8)
                cols = slice(m * P, (m + 1) * P)
                for k in range(KB):
                    if m == 0:
                        since(pe, xc_lo, c, 8, k + 1)
                        if first:
                            wait_units(pe, U_QK + 2 * k + 2)
                    for i, (wh, wl) in enumerate(((wq_h, wq_l), (wk_h, wk_l))):
                        mm = split3(pe, bank[i][:, :], (wh[:, k, cols], wl[:, k, cols]),
                                    (xc_h[:, k, :], xc_l[:, k, :]), k == 0, k == KB - 1)
                        if k == KB - 1:
                            mm.then_inc(qk_mm, 1)
                    if m == PAIRS - 1 and k < KB - 1:
                        mm.then_inc(xc_used, 1)
                    if beside and k == 3:
                        beside()

            def c_scores(c, m):
                since(pe, qk_lo, c, 8, 2 * m + 2)
                for j in range(2):
                    since(pe, s_sub, c, 8, 2 * m + j - 1)
                    r = slice(HEAD * j, HEAD * j + HEAD)
                    for t in range(TILES):
                        cols = slice(t * P, (t + 1) * P)
                        mm = split3(pe, bank[4 + j][:, cols], (qk_h[r, 0, cols], qk_l[r, 0, cols]),
                                    (qk_h[r, 1, cols], qk_l[r, 1, cols]), True, True)
                    mm.then_inc(s_mm, 1)

            def c_turn(c, m, banks=PT_BANK):
                for j in range(2):
                    since(pe, s_norm, c, 8, 2 * m + j + 1)
                    if m == 0 and j == 0:
                        since(pe, v_lo, c, 4, 4)
                    since(pe, pt_lo, c, 8, 2 * m + j - 1)
                    for t in range(TILES):
                        cols = slice(t * P, (t + 1) * P)
                        mm = pe.transpose(bank[banks[j]][:, cols], pr[:, j, cols], ident[:, :])
                    mm.then_inc(pt_mm, 1)

            def c_mix(c, m, js=(0, 1)):
                for j in js:
                    since(pe, pt_lo, c, 8, 2 * m + j + 1)
                    since(pe, vo_ev, c, 8, 2 * m + j)
                    since(pe, v_lo, c, 4, 4)
                    for t in range(TILES):
                        cols = slice(t * P, (t + 1) * P)
                        pair = slice(m * P, (m + 1) * P)
                        mm = split3(pe, bank[7][:, cols], (v_h[:, t, pair], v_l[:, t, pair]),
                                    (pt_h[:, j, cols], pt_l[:, j, cols]), True, True)
                    mm.then_inc(pv_mm, 1)

            def c_step(c, ahead):
                later = not (isinstance(c, int) and c == 0)
                c_scores(c, 0)
                if later:
                    c_values(c, (0, 1), lambda: c_mix(c - 1, 3, [0]))
                    c_mix(c - 1, 3, [1])
                    c_values(c, (2, 3))
                if ahead:
                    ln_mean_pe(pe, c + 1 + CH)
                c_qk(c, 1)
                c_turn(c, 0)
                c_scores(c, 1)
                c_qk(c, 2, (lambda: ln_var_pe(pe, c + 1 + CH)) if ahead else None)
                c_mix(c, 0, [0])
                c_turn(c, 1)
                c_mix(c, 0, [1])
                c_scores(c, 2)
                c_qk(c, 3)
                c_mix(c, 1, [0])
                c_turn(c, 2, PT_BANK if ahead else PT_LAST[0])
                c_mix(c, 1, [1])
                c_scores(c, 3)
                if ahead:
                    c_qk(c + 1, 0)
                    c_mix(c, 2, [0])
                    c_turn(c, 3)
                    c_mix(c, 2, [1])

            c_values(0, range(TILES))
            c_qk(0, 0)
            chunks(pe, 0, CH - 1, lambda c: c_step(c, True))
            c_step(CH - 1, False)

            def o_group(c, g, k):
                ms = A_GROUPS[g]
                if c == 0 and g < 2:
                    wait_units(pe, U_O + PAIRS * g + k + 1)
                if k == 0 and c > 0:
                    pe.wait_ge(o_ev, 8 * (c - 1) + ms[-1] + 1)
                if k == 0 and g == 1 and c > 1:
                    pe.wait_ge(ln_std, 2 * CH + c - 1)
                if k == 0 and g == 2 and c > 0:
                    pe.wait_ge(st_copied, CH + c)
                if g == 0:
                    since(pe, vs_lo, c, 4, k + 1)
                for m in ms:
                    cols = slice(m * P, (m + 1) * P)
                    mm = split3(pe, bank[m][:, :], (wo_h[:, k, cols], wo_l[:, k, cols]),
                                (vs_h[:, k, :], vs_l[:, k, :]), k == 0, k == PAIRS - 1)
                    if k == PAIRS - 1:
                        mm.then_inc(o_mm, 1)
                if g == 2 and k < PAIRS - 1:
                    mm.then_inc(vs_used, 1)

            for k in range(PAIRS):
                o_group(0, 0, k)
            c_mix(CH - 1, 2, [0])
            pe.wait_ge(s_sub, 8 * CH)
            pe.wait_ge(pt_lo, 8 * CH - 2)
            o_group(0, 1, 0)
            c_mix(CH - 1, 2, [1])
            o_group(0, 1, 1)
            pe.wait_ge(vo_ev, 8 * CH - 2)
            c_turn(CH - 1, 3, PT_LAST[1])
            o_group(0, 1, 2)
            o_group(0, 1, 3)
            pe.wait_ge(pt_lo, 8 * CH)
            c_mix(CH - 1, 3)
            pe.wait_ge(vo_ev, 8 * CH)
            for c in range(CH):
                for g in range(2 if c == 0 else 0, 3):
                    for k in range(PAIRS):
                        o_group(c, g, k)
                        if c > 0 and (g, k) == (0, 2):
                            pe.wait_ge(o_ev, 8 * c)
                            stat_mean_pe(pe, 2 * CH + c - 1)
                        if c > 0 and (g, k) == (2, 3):
                            pe.wait_ge(o_ev, 8 * c + VAR_BANK + 1)
                            stat_var_pe(pe, 2 * CH + c - 1, CH + c - 1, VAR_BANK)

            def ff_up(c, a, i):
                j, blk = i // 2, i % 2
                if i == 0:
                    since(pe, xd_lo, c, 8, a + 1)
                since(pe, gelu_ok, c, 32, 4 * a + i - 3)
                r = slice(FF_IN * j, FF_IN * (j + 1))
                cols = slice(blk * P, (blk + 1) * P)
                mm = split3(pe, bank[i][:, :], (up_h[r, a, cols], up_l[r, a, cols]),
                            (xd_h[r, a, :], xd_l[r, a, :]), True, True)
                mm.then_inc(up_mm, 1)

            def ff_down(c, a, i):
                since(pe, g_lo, c, 32, 4 * a + i + 1)
                if i == 0:
                    since(pe, d_ev, c, 8, a - 1)
                mm = split3(pe, bank[4 + a % 2][:, :], (dn_h[:, FFB * a + i, :], dn_l[:, FFB * a + i, :]),
                            (g_h[:, i, :], g_l[:, i, :]), i == 0, i == FFB - 1)
                mm.then_inc(g_used, 1)

            def d_step(c, ahead):
                for a in range(KB):
                    for i in range(FFB):
                        if a + 1 < KB:
                            ff_up(c, a + 1, i)
                        elif ahead:
                            ff_up(c + 1, 0, i)
                        ff_down(c, a, i)
                    if isinstance(c, int) and c == 0 and a == 1:
                        stat_mean_pe(pe, 3 * CH - 1)
                if isinstance(c, int) and c == 0:
                    stat_var_pe(pe, 3 * CH - 1, 2 * CH - 1)

            pe.wait_ge(o_ev, 8 * (CH - 1) + 4)
            wait_units(pe, U_END)
            for i in range(FFB):
                if i == VAR_BANK:
                    pe.wait_ge(ln_std, 3 * CH - 1)
                ff_up(0, 0, i)
            pe.wait_ge(o_ev, 8 * CH)
            chunks(pe, 0, CH - 1, lambda c: d_step(c, True))
            d_step(CH - 1, False)


A_GROUPS = [(0, 1, 2), (3, 4, 5), (6, 7)]
YT_BANK, AT_BANK, CV_BANK = 0, 2, 4
GATES_AT = [{0: (0,), 1: (1, 2), 2: (3, 4), 3: (5, 6), 4: (7,)}, {4: (0, 1), 5: (2, 3), 6: (4, 5), 7: (6, 7)}]
TURN_AFTER = [6, 8]
PT_BANK, PT_LAST = (2, 3), ((6, 3), (6, 7))
SUM_SPLIT = 5
VAR_BANK = 3
XD_PREP = {3: (0, 1), 4: (2, 3), 5: (4, 5), 6: (6, 7)}
XD_FIRST = {0: (2, 3), 1: (4, 5), 2: (6, 7)}
STAT_AT = {2: (0, 1), 4: (2, 3), 5: (4,), 6: (5,), 7: (6, 7)}
XD_SPLIT = {4: (0, 1), 5: (2, 3), 6: (4, 5), 7: (6, 7)}


def hg_block(n):
    return (n + 1) % 2 * KB


def gate_turn_bank(n):
    return 0 if isinstance(n, int) and n == 0 else 7


def kernel(**inputs):
    import numpy as np
    import concourse.bacc as bacc
    from concourse.bass_utils import run_bass_kernel_spmd

    a = {k: np.asarray(v) for k, v in inputs.items()}

    def cols(v):
        return v.reshape(-1, P).T

    arrays = {
        "x_t": a["x"].reshape(TOKENS, D).T,
        "w_proj": a["L0_tok_W_proj"],
        "w_ff": a["L0_tok_W_ff"],
        "w_gen": a["L0_tok_W_wgen"],
        "w_qkv_t": a["L0_attn_w_qkv"].T,
        "w_o_t": a["L0_attn_w_o"].T,
        "up": a["L0_ffn_up"],
        "down": a["L0_ffn_down"],
        "vecs": np.concatenate([cols(a["L0_tok_b_proj"]), cols(a["L0_tok_ln_g"]), cols(a["L0_tok_ln_b"]),
                                cols(a["L0_tok_b_ff"]), cols(a["L0_attn_b_o"]), cols(a["L0_attn_b_qkv"]),
                                cols(np.pad(a["L0_tok_b_wgen"], (0, P - LOGITS)))], axis=1),
        "perm": cols(a["L0_ffn_perm"]),
    }
    nc = bacc.Bacc("TRN2", target_bir_lowering=False, num_devices=1)
    given, args = {}, []
    for name, v in arrays.items():
        v = np.ascontiguousarray(v)
        given[name] = v
        args.append(nc.dram_tensor(name, v.shape, mybir.dt.from_np(v.dtype), kind="ExternalInput").ap())
    for c in range(CH):
        args.append(nc.dram_tensor(f"out_{c}", (D, N), mybir.dt.float32, kind="ExternalOutput").ap())
    audio_tower(nc, *args)
    r = run_bass_kernel_spmd(nc, [given], core_ids=[0])
    got = np.stack([r.results[0][f"out_{c}"].T for c in range(CH)])
    return np.ascontiguousarray(got).reshape(BATCH, SEQ, D)
```
